# Optimizing a Trainium2 kernel written in Bass

```python
import numpy as np
import jax
import jax.numpy as jnp

def _softmax(x, axis=-1):
    return jax.nn.softmax(x, axis=axis)

def _gelu(x):
    return jax.nn.gelu(x, approximate=True)

def _silu(x):
    return jax.nn.silu(x)

def _sigmoid(x):
    return jax.nn.sigmoid(x)

def _layernorm(x, axis=-1, eps=1e-05):
    m = jnp.mean(x, axis=axis, keepdims=True)
    v = jnp.var(x, axis=axis, keepdims=True)
    return (x - m) / jnp.sqrt(v + eps)

def _scatter_add(tgt, idx, src, axis=0):
    return tgt.at[idx].add(src)

def _segment_sum(src, seg, n):
    return jax.ops.segment_sum(src, seg, n)
kernel_name = 'mk_gps_d1_gnn_r32_342e00'

def setup_inputs(seed: int=0):
    np.random.seed(seed)
    _w = jnp.asarray

    def _rec_inputs():
        import jax
        import jax.numpy as jnp
        _gk = jax.random.key(seed)
        x = -0.0003713 + 1 * jax.random.normal(jax.random.fold_in(_gk, 1), (3125, 256), jnp.float32)
        _s = jax.random.randint(jax.random.fold_in(_gk, 2), (25000,), 0, 3125, jnp.int32)
        _d = jax.random.randint(jax.random.fold_in(_gk, 3), (25000,), 0, 3125, jnp.int32)
        _loop = jnp.arange(3125, dtype=jnp.int32)
        src = jnp.concatenate([_s, _d, _loop])
        dst = jnp.concatenate([_d, _s, _loop])
        _o = jnp.argsort(dst, stable=True)
        src = src[_o]
        dst = dst[_o]
        edge_attr_128 = -2.25437e-05 + 0.999858 * jax.random.normal(jax.random.fold_in(_gk, 12), (53125, 128), jnp.float32)
        return (x, src, dst, edge_attr_128)
    x, src, dst, edge_attr_128 = _rec_inputs()

    def _L0_gnn_setup():
        import jax, jax.numpy as jnp
        import numpy as np
        N_NODES, N_EDGES, N_GRAPHS = (50000, 15625, 64)
        NODE_D, EDGE_D, GLOB_D = (256, 128, 64)
        EPS = 1e-05
        key = jax.random.key(seed)
        ks = jax.random.split(key, 12)
        inp = {'x': jax.random.normal(ks[0], (N_NODES, NODE_D), jnp.float32), 'edge_attr': jax.random.normal(ks[1], (N_EDGES, EDGE_D), jnp.float32), 'u': jax.random.normal(ks[2], (N_GRAPHS, GLOB_D), jnp.float32), 'W1': jax.random.normal(ks[3], (NODE_D + EDGE_D, 4 * EDGE_D), jnp.float32) * 0.02, 'b1': jnp.zeros((4 * EDGE_D,), jnp.float32), 'W2': jax.random.normal(ks[4], (4 * EDGE_D, EDGE_D), jnp.float32) * 0.02, 'b2': jnp.zeros((EDGE_D,), jnp.float32), 'W3': jax.random.normal(ks[5], (NODE_D + EDGE_D + GLOB_D, 4 * NODE_D), jnp.float32) * 0.02, 'b3': jnp.zeros((4 * NODE_D,), jnp.float32), 'W4': jax.random.normal(ks[6], (4 * NODE_D, NODE_D), jnp.float32) * 0.02, 'b4': jnp.zeros((NODE_D,), jnp.float32), 'gamma': jnp.ones((NODE_D,), jnp.float32), 'beta': jnp.zeros((NODE_D,), jnp.float32), 'edge_index': jax.random.randint(ks[7], (2, N_EDGES), 0, N_NODES, jnp.int64 if jax.config.jax_enable_x64 else jnp.int32), 'batch': jnp.sort(jax.random.randint(ks[8], (N_NODES,), 0, N_GRAPHS, jnp.int64 if jax.config.jax_enable_x64 else jnp.int32))}
        return inp
    _L0_gnn_all = _L0_gnn_setup()
    _L0_gnn_in = {k: v for k, v in _L0_gnn_all.items() if k in ('u', 'W1', 'b1', 'W2', 'b2', 'W3', 'b3', 'W4', 'b4', 'gamma', 'beta')}
    del _L0_gnn_all

    def _L0_mix_setup():
        import jax, jax.numpy as jnp
        import numpy as np
        A, Bc, Cc = (0.5, 1.0, 1.0)
        H = 8
        EPS = 1e-12

        def _normalize(t):
            n = jnp.linalg.norm(t, axis=-1, keepdims=True)
            return t / jnp.maximum(n, EPS)
        key = jax.random.key(seed)
        ks = jax.random.split(key, 5)
        B, N, C = (8, 64, 256)
        D = C // H
        x = jax.random.normal(ks[0], (B, N, C), dtype=jnp.float32)
        Wqkv = jax.random.normal(ks[1], (3 * H * D, C), dtype=jnp.float32) * 0.02
        bqkv = jnp.zeros((3 * H * D,), dtype=jnp.float32)
        Wproj = jax.random.normal(ks[2], (C, H * D), dtype=jnp.float32) * 0.02
        bproj = jnp.zeros((C,), dtype=jnp.float32)
        temperature = jnp.ones((1, H, 1, 1), dtype=jnp.float32)
        return {'x': x, 'Wqkv': Wqkv, 'bqkv': bqkv, 'Wproj': Wproj, 'bproj': bproj, 'temperature': temperature}
    _L0_mix_all = _L0_mix_setup()
    _L0_mix_in = {k: v for k, v in _L0_mix_all.items() if k in ('Wqkv', 'bqkv', 'Wproj', 'bproj', 'temperature')}
    del _L0_mix_all

    def _L0_ffn_setup():
        import jax, jax.numpy as jnp
        import numpy as np
        B, S, H, F, E, K = (8, 128, 256, 512, 16, 2)
        EPS = 1e-05
        key = jax.random.key(seed)
        ks = jax.random.split(key, 9)
        sc = 0.02
        return {'x': jax.random.normal(ks[0], (B, S, H), dtype=jnp.float32), 'gate_w': jax.random.normal(ks[1], (H, E), dtype=jnp.float32) * sc, 'gate_b': jnp.zeros((E,), dtype=jnp.float32), 'w1': jax.random.normal(ks[2], (E, H, F), dtype=jnp.float32) * sc, 'b1': jnp.zeros((E, F), dtype=jnp.float32), 'w2': jax.random.normal(ks[3], (E, F, H), dtype=jnp.float32) * sc, 'b2': jnp.zeros((E, H), dtype=jnp.float32), 'gamma': jnp.ones((H,), dtype=jnp.float32), 'beta': jnp.zeros((H,), dtype=jnp.float32)}
    _L0_ffn_all = _L0_ffn_setup()
    _L0_ffn_in = {k: v for k, v in _L0_ffn_all.items() if k in ('gate_w', 'gate_b', 'w1', 'b1', 'w2', 'b2', 'gamma', 'beta')}
    del _L0_ffn_all
    return {'x': x, 'src': src, 'dst': dst, 'edge_attr_128': edge_attr_128, 'L0_gnn_u': _L0_gnn_in['u'], 'L0_gnn_W1': _L0_gnn_in['W1'], 'L0_gnn_b1': _L0_gnn_in['b1'], 'L0_gnn_W2': _L0_gnn_in['W2'], 'L0_gnn_b2': _L0_gnn_in['b2'], 'L0_gnn_W3': _L0_gnn_in['W3'], 'L0_gnn_b3': _L0_gnn_in['b3'], 'L0_gnn_W4': _L0_gnn_in['W4'], 'L0_gnn_b4': _L0_gnn_in['b4'], 'L0_gnn_gamma': _L0_gnn_in['gamma'], 'L0_gnn_beta': _L0_gnn_in['beta'], 'L0_mix_Wqkv': _L0_mix_in['Wqkv'], 'L0_mix_bqkv': _L0_mix_in['bqkv'], 'L0_mix_Wproj': _L0_mix_in['Wproj'], 'L0_mix_bproj': _L0_mix_in['bproj'], 'L0_mix_temperature': _L0_mix_in['temperature'], 'L0_ffn_gate_w': _L0_ffn_in['gate_w'], 'L0_ffn_gate_b': _L0_ffn_in['gate_b'], 'L0_ffn_w1': _L0_ffn_in['w1'], 'L0_ffn_b1': _L0_ffn_in['b1'], 'L0_ffn_w2': _L0_ffn_in['w2'], 'L0_ffn_b2': _L0_ffn_in['b2'], 'L0_ffn_gamma': _L0_ffn_in['gamma'], 'L0_ffn_beta': _L0_ffn_in['beta']}

def reference(x, src, dst, edge_attr_128, L0_gnn_u, L0_gnn_W1, L0_gnn_b1, L0_gnn_W2, L0_gnn_b2, L0_gnn_W3, L0_gnn_b3, L0_gnn_W4, L0_gnn_b4, L0_gnn_gamma, L0_gnn_beta, L0_mix_Wqkv, L0_mix_bqkv, L0_mix_Wproj, L0_mix_bproj, L0_mix_temperature, L0_ffn_gate_w, L0_ffn_gate_b, L0_ffn_w1, L0_ffn_b1, L0_ffn_w2, L0_ffn_b2, L0_ffn_gamma, L0_ffn_beta):
    import jax
    import jax.numpy as jnp

    def _L0_gnn_ref(x, edge_attr, u, W1, b1, W2, b2, W3, b3, W4, b4, gamma, beta, edge_index, batch):
        import jax, jax.numpy as jnp
        import numpy as np
        N_NODES, N_EDGES, N_GRAPHS = (50000, 15625, 64)
        NODE_D, EDGE_D, GLOB_D = (256, 128, 64)
        EPS = 1e-05
        row, col = (edge_index[0], edge_index[1])
        n = x.shape[0]
        e = jnp.concatenate([x[row], edge_attr], axis=1)
        e = jnp.maximum(e @ W1 + b1, 0.0) @ W2 + b2
        s = jax.ops.segment_sum(e, col, num_segments=n)
        cnt = jax.ops.segment_sum(jnp.ones((col.shape[0],), x.dtype), col, num_segments=n)
        agg = s / jnp.maximum(cnt, 1.0)[:, None]
        h = jnp.concatenate([x, agg, u[batch]], axis=1)
        h = jnp.maximum(h @ W3 + b3, 0.0) @ W4 + b4
        y = h + x
        mu = jnp.mean(y, axis=-1, keepdims=True)
        var = jnp.mean((y - mu) ** 2, axis=-1, keepdims=True)
        return (y - mu) * jax.lax.rsqrt(var + EPS) * gamma + beta

    def _L0_mix_ref(x, Wqkv, bqkv, Wproj, bproj, temperature):
        import jax, jax.numpy as jnp
        import numpy as np
        A, Bc, Cc = (0.5, 1.0, 1.0)
        H = 8
        EPS = 1e-12

        def _normalize(t):
            n = jnp.linalg.norm(t, axis=-1, keepdims=True)
            return t / jnp.maximum(n, EPS)
        B, N, C = x.shape
        D = C // H
        scale = float(D) ** 0.25
        qkv = (x @ Wqkv.T + bqkv).reshape(B, N, 3, H, D)
        qkv = jnp.transpose(qkv, (2, 0, 3, 1, 4))
        q, k, v = (qkv[0], qkv[1], qkv[2])
        q = q * scale
        v1 = jnp.concatenate([jnp.ones((B, H, N, 1), dtype=v.dtype), v], axis=-1)
        qn = _normalize(q) * (scale * temperature)
        kn = _normalize(k) * scale
        vN = v1 / N
        kv_mod = jnp.einsum('bhni,bhnj,bhne->bhije', kn, kn, vN)
        kv = jnp.einsum('bhnd,bhne->bhde', kn, vN)
        vsum = jnp.sum(vN, axis=-2)[:, :, None, :]
        y = A * jnp.einsum('bhni,bhnj,bhije->bhne', qn, qn, kv_mod) + scale ** 2 * Bc * jnp.einsum('bhnd,bhde->bhne', qn, kv) + scale ** 4 * Cc * vsum
        y_norm, y = (y[..., :1], y[..., 1:])
        y = y / y_norm
        out = jnp.transpose(y, (0, 2, 1, 3)).reshape(B, N, H * D)
        return out @ Wproj.T + bproj

    def _L0_ffn_ref(x, gate_w, gate_b, w1, b1, w2, b2, gamma, beta):
        import jax, jax.numpy as jnp
        import numpy as np
        B, S, H, F, E, K = (8, 128, 256, 512, 16, 2)
        EPS = 1e-05
        gate_logits = x @ gate_w + gate_b
        topk_vals, topk_idx = jax.lax.top_k(gate_logits, K)
        topk_w = jax.nn.softmax(topk_vals, axis=-1)
        h = jax.nn.relu(jnp.einsum('bsh,ehf->bsef', x, w1) + b1)
        expert_out = jnp.einsum('bsef,efh->bseh', h, w2) + b2
        sel = jnp.take_along_axis(expert_out, topk_idx[:, :, :, None], axis=2)
        moe = jnp.sum(topk_w[..., None] * sel, axis=2)
        y = x + moe
        mu = jnp.mean(y, axis=-1, keepdims=True)
        var = jnp.var(y, axis=-1, keepdims=True)
        return (y - mu) / jnp.sqrt(var + EPS) * gamma + beta
    edge_index = jnp.stack([src, dst])
    batch0 = jnp.zeros((3125,), jnp.int32)
    xn = _layernorm(x, axis=-1)
    x = x + _L0_gnn_ref(xn, edge_attr_128, L0_gnn_u, L0_gnn_W1, L0_gnn_b1, L0_gnn_W2, L0_gnn_b2, L0_gnn_W3, L0_gnn_b3, L0_gnn_W4, L0_gnn_b4, L0_gnn_gamma, L0_gnn_beta, edge_index, batch0) + _L0_mix_ref(xn[None], L0_mix_Wqkv, L0_mix_bqkv, L0_mix_Wproj, L0_mix_bproj, L0_mix_temperature)[0]
    x = x + _L0_ffn_ref(_layernorm(x, axis=-1)[None], L0_ffn_gate_w, L0_ffn_gate_b, L0_ffn_w1, L0_ffn_b1, L0_ffn_w2, L0_ffn_b2, L0_ffn_gamma, L0_ffn_beta)[0]
    return x

_drawn_inputs = setup_inputs


def setup_inputs(seed=0):
    import zlib

    import numpy as np

    out = dict(_drawn_inputs(seed))
    spreads = {'L0_gnn_b1': (0.0, 0.8),
     'L0_gnn_b2': (0.0, 2.0),
     'L0_gnn_b3': (0.0, 0.359),
     'L0_gnn_b4': (0.0, 0.1),
     'L0_gnn_gamma': (1.0, 0.2),
     'L0_gnn_beta': (0.0, 0.1),
     'L0_mix_bqkv': (0.0, 0.508),
     'L0_mix_bproj': (0.0, 0.1),
     'L0_mix_temperature': (1.0, 0.6),
     'L0_ffn_gate_b': (0.0, 0.343),
     'L0_ffn_b1': (0.0, 0.8),
     'L0_ffn_b2': (0.0, 0.325),
     'L0_ffn_gamma': (1.0, 0.2),
     'L0_ffn_beta': (0.0, 0.1)}
    factors = {'edge_attr_128': 8.0,
     'L0_gnn_W1': 8.0,
     'L0_gnn_W2': 8.0,
     'L0_mix_Wqkv': 8.0,
     'L0_mix_Wproj': 3.612,
     'L0_ffn_w1': 2.73,
     'L0_gnn_u': 2.796}
    for name, (base, spread) in spreads.items():
        noise = np.random.default_rng([zlib.crc32(name.encode()), seed]).standard_normal(out[name].shape)
        drawn = base * np.exp(spread * noise) if base else spread * noise
        out[name] = jnp.asarray(drawn.astype(out[name].dtype))
    for name, factor in factors.items():
        out[name] = (out[name] * factor).astype(out[name].dtype)
    return out
```

```python
import concourse.bass as bass
from concourse import mybir
from contextlib import ExitStack

F32 = mybir.dt.float32
I32 = mybir.dt.int32
U32 = mybir.dt.uint32
ALU = mybir.AluOpType
ACT = mybir.ActivationFunctionType
X = mybir.AxisListType.X

P = 128
N = 3125
D = 256
ED = 128
HID = 512
E = 53125
NT = (N + P - 1) // P
LAST = N - (NT - 1) * P
ET = E // P
EL = E - ET * P
G = 5
NG = ET // G
assert NG * G == ET and NG % 2 == 1 and NT % 2 == 1
W = 64
LAG = 3
H = 8
HD = D // H
HQ = HD // 2
NF = 16 * HD
FT = HD + HQ + 1
FW = NF + FT
FB = NF // P
VW = HD + 1
FH = 4 * D
NE = 16
FE = 512
MT = (2 * N + NE * (P - 1)) // P
SCALE = float(HD) ** 0.25
LN_EPS = 1e-5
NORM_EPS = 1e-12


def rows(ap, n, width, start=0):
    return bass.AP(tensor=ap.tensor, offset=ap.offset + start, ap=[[0, n], [1, width]])


class Chain:

    def __init__(self, eng, sem, turn, per):
        self.eng, self.sem, self.start, self.per, self.n = eng, sem, turn * per, per, 0

    def __call__(self, ins):
        self.n += 1
        assert self.n <= self.per
        ins.then_inc(self.sem, 1)
        self.eng.wait_ge(self.sem, self.start + self.n)

    def end(self):
        assert self.n == self.per, (self.n, self.per)


def each_tile(eng, body):
    body(0, 0, 0, P, P)
    body(1, 0, 1, P, P)
    half = NT // 2
    with eng.Fori(1, half - 1) as i:
        body(2 * i, i, 0, P, P)
        body(2 * i + 1, i, 1, P, P)
    body(NT - 3, half - 1, 0, P, P)
    body(NT - 2, half - 1, 1, P, LAST)
    body(NT - 1, half, 0, LAST, 0)


def known(t, least):
    return not isinstance(t, int) or t >= least


def carry_wait(eng, carrier):
    eng.sem_inc(carrier, 1)


class Memory:

    def __init__(self, nc, tag):
        self.nc, self.tag, self.ctx = nc, tag, ExitStack()

    def __enter__(self):
        self.ctx.__enter__()
        return self

    def __exit__(self, *a):
        return self.ctx.__exit__(*a)

    def sb(self, name, shape, dt=F32):
        return self.ctx.enter_context(self.nc.sbuf_tensor(self.tag + name, shape, dt))

    def ps(self, name, shape):
        return self.ctx.enter_context(self.nc.psum_tensor(self.tag + name, shape, F32))

    def sem(self, name):
        return self.ctx.enter_context(self.nc.semaphore(self.tag + name))


def setup_phase(nc, m, c, a):
    with Memory(nc, "s_") as l:
        groups_i = l.sb("groups_i", [NG + 1, G * P], I32)
        lohi = l.sb("lohi", [NG + 1, 2])
        lo_rows = l.sb("lo_rows", [NG + 1, P])
        hi_rows = l.sb("hi_rows", [NG + 1, P])
        dst_i = l.sb("dst_i", [P, ET + 1], I32)
        span = l.sb("span", [P, NG + 1])
        widest = l.sb("widest", [1, 1])
        windows_i = l.sb("windows_i", [1, 1], I32)
        ps_lo = l.ps("ps_lo", [P, 512])
        ps_hi = l.ps("ps_hi", [P, 512])
        dst_in = l.sem("dst_in")
        src_in = l.sem("src_in")
        filled = l.sem("filled")
        ident_made = l.sem("ident_made")
        masks_made = l.sem("masks_made")
        step = l.sem("step")
        lohi_made = l.sem("lohi_made")
        spread = l.sem("spread")

        with nc.Block() as block:
            @block.sync
            def _(sp):
                sp.dma_start(groups_i[0:NG, :], a["dst"][0:NG * G * P].rearrange("(g e) -> g e", g=NG)).then_inc(dst_in, 16)
                sp.dma_start(groups_i[NG:NG + 1, :], a["dst"][E - G * P:E].rearrange("(g e) -> g e", g=1)).then_inc(dst_in, 16)
                sp.dma_start(dst_i[:, 0:ET], a["dst_cols"]).then_inc(dst_in, 16)
                sp.dma_start(dst_i[0:EL, ET:ET + 1], a["dst_tail"]).then_inc(dst_in, 16)
                sp.dma_start(c["src"][:, 0:ET], a["src_cols"]).then_inc(src_in, 16)
                sp.dma_start(c["src"][0:EL, ET:ET + 1], a["src_tail"]).then_inc(src_in, 16)
                sp.wait_ge(src_in, 32)

            @block.gpsimd
            def _(pool):
                nc.gpsimd.memset(c["ident"][:, :], 0.0).then_inc(filled, 1)
                nc.gpsimd.memset(c["ones"][:, :], 1.0).then_inc(filled, 1)
                nc.gpsimd.memset(c["before"][:, :], 1.0).then_inc(filled, 1)
                nc.gpsimd.memset(c["zeros"][:, :], 0.0).then_inc(filled, 1)
                pool.wait_ge(filled, 4)
                nc.gpsimd.affine_select(out=c["ident"][:, :], in_=c["ident"][:, :], compare_op=ALU.not_equal,
                                        fill=1.0, base=0, pattern=[[-1, P]], channel_multiplier=1).then_inc(ident_made, 1)
                nc.gpsimd.affine_select(out=c["before"][:, :], in_=c["before"][:, :], compare_op=ALU.is_gt,
                                        fill=0.0, base=0, pattern=[[1, P]], channel_multiplier=-1).then_inc(masks_made, 1)
                nc.gpsimd.iota(c["iota"][:, :], pattern=[[1, W]], base=0, channel_multiplier=0,
                               allow_small_or_imprecise_dtypes=True).then_inc(masks_made, 1)
                pool.wait_ge(masks_made, 2)

            @block.vector
            def _(dve):
                n = [0]

                def link(ins):
                    n[0] += 1
                    ins.then_inc(step, 1)
                    dve.wait_ge(step, n[0])

                link(nc.vector.memset(c["eps"][:, :], LN_EPS))
                link(nc.vector.memset(c["acc"][:, :, :], 0.0))
                link(nc.vector.memset(lo_rows[:, :], 1.0))
                dve.wait_ge(dst_in, 64)
                link(nc.vector.tensor_reduce(lohi[:, 0:1], groups_i[:, :], X, ALU.min))
                link(nc.vector.tensor_reduce(lohi[:, 1:2], groups_i[:, :], X, ALU.max))
                link(nc.vector.tensor_scalar(hi_rows[:, :], lo_rows[:, :], lohi[:, 1:2], None, ALU.mult))
                link(nc.vector.tensor_scalar(lo_rows[:, :], lo_rows[:, :], lohi[:, 0:1], None, ALU.mult))
                nc.vector.tensor_copy(c["dst_rel"][:, 0:ET], dst_i[:, 0:ET]).then_inc(lohi_made, 1)
                dve.wait_ge(lohi_made, 1)
                link(nc.vector.tensor_copy(c["dst_rel"][0:EL, ET:ET + 1], dst_i[0:EL, ET:ET + 1]))
                dve.wait_ge(spread, 2)
                link(nc.vector.tensor_copy(c["base"][:, :], ps_lo[:, 0:NG + 1]))
                link(nc.vector.tensor_tensor(span[:, :], ps_hi[:, 0:NG + 1], c["base"][:, :], ALU.subtract))
                link(nc.vector.tensor_reduce(widest[:, :], span[0:1, :], X, ALU.max))
                link(nc.vector.tensor_copy(windows_i[:, :], widest[:, :]))
                link(nc.vector.tensor_scalar(windows_i[:, :], windows_i[:, :], W.bit_length() - 1, None, ALU.arith_shift_right))
                link(nc.vector.tensor_scalar(c["passes"][:, :], windows_i[:, :], 1, None, ALU.add))
                link(nc.vector.tensor_copy(c["base_i"][:, :], c["base"][0:1, :]))
                view = c["dst_rel"][:, 0:ET].rearrange("p (g u) -> p g u", u=G)
                link(nc.vector.tensor_tensor(view, view, c["base"][:, 0:NG].unsqueeze(2).to_broadcast([P, NG, G]), ALU.subtract))
                link(nc.vector.tensor_tensor(c["dst_rel"][0:EL, ET:ET + 1], c["dst_rel"][0:EL, ET:ET + 1],
                                             c["base"][0:EL, NG:NG + 1], ALU.subtract))

            @block.tensor
            def _(pe):
                pe.wait_ge(ident_made, 1)
                pe.wait_ge(lohi_made, 1)
                nc.tensor.matmul(ps_lo[:, 0:NG + 1], lo_rows[:, :], c["ident"][0:NG + 1, 0:NG + 1], start=True, stop=True).then_inc(spread, 1)
                nc.tensor.matmul(ps_hi[:, 0:NG + 1], hi_rows[:, :], c["ident"][0:NG + 1, 0:NG + 1], start=True, stop=True).then_inc(spread, 1)


def node_phase(nc, m, c, a, d):
    with Memory(nc, "a_") as l:
        w1a = l.sb("w1a", [P, 2, HID])
        wkv = l.sb("wkv", [P, 2, 2 * D])
        b1_all = l.sb("b1_all", [P, HID])
        bkv_all = l.sb("bkv_all", [P, 2 * D])
        x_in = [l.sb(f"x{p}", [P, D]) for p in range(2)]
        xn = [l.sb(f"xn{p}", [P, D]) for p in range(2)]
        xT = [l.sb(f"xT{p}", [P, 2, P]) for p in range(2)]
        proj = [l.sb(f"proj{p}", [P, HID]) for p in range(2)]
        v1 = [l.sb(f"v1{p}", [P, H, VW]) for p in range(2)]
        feat = [l.sb(f"feat{p}", [P, H, FW]) for p in range(2)]
        k_raw = l.sb("k_raw", [P, H, HD])
        k_sq = l.sb("k_sq", [P, H, HD])
        kk = l.sb("kk", [P, H, HD + HQ])
        stats = l.sb("stats", [P, 6])
        mv = l.sb("mv", [P, 2])
        rstd = l.sb("rstd", [P, 1])
        ssq = l.sb("ssq", [P, H])
        norm = l.sb("norm", [P, H])
        ps_kv = [l.ps(f"ps_sum{j}", [P, 512]) for j in range(3)]
        ps_t = l.ps("ps_t", [P, 2, 2, P])
        ps_p = [l.ps(f"ps_p{p}", [P, 512]) for p in range(2)]
        ps_k = [l.ps(f"ps_k{p}", [P, 512]) for p in range(2)]
        weights_in = l.sem("weights_in")
        x_loaded = [l.sem(f"x_loaded{p}") for p in range(2)]
        xn_stored = [l.sem(f"xn_stored{p}") for p in range(2)]
        xT_stored = [l.sem(f"xT_stored{p}") for p in range(2)]
        p_stored = [l.sem(f"p_stored{p}") for p in range(2)]
        const_made = l.sem("const_made")
        var_ready = l.sem("var_ready")
        std_ready = l.sem("std_ready")
        xn_ready = l.sem("xn_ready")
        turned = l.sem("turned")
        xT_ready = l.sem("xT_ready")
        p_done = l.sem("p_done")
        kv_done = l.sem("kv_done")
        p_ready = l.sem("p_ready")
        ssq_ready = l.sem("ssq_ready")
        norm_ready = l.sem("norm_ready")
        feat_ready = l.sem("feat_ready")
        feat_used = l.sem("feat_used")
        sums_read = l.sem("sums_read")
        norm_step = l.sem("norm_step")
        key_step = l.sem("key_step")
        x_d, wkv_d = a["x"], a["wqkvT"]

        with nc.Block() as block:
            @block.sync
            def _(sp):
                for p in range(2):
                    sp.dma_start(x_in[p][:, :], x_d[p * P:(p + 1) * P, :]).then_inc(x_loaded[p], 16)
                sp.dma_start(w1a[:, :, :], a["W1"][0:D, :].rearrange("(c k) f -> k c f", c=2)).then_inc(weights_in, 16)
                sp.dma_start(wkv[:, :, :], wkv_d[:, D:3 * D].rearrange("(c k) f -> k c f", c=2)).then_inc(weights_in, 16)
                sp.dma_start(b1_all[:, :], rows(a["b1"], P, HID)).then_inc(weights_in, 16)
                sp.dma_start(bkv_all[:, :], rows(a["bqkv"], P, 2 * D, D)).then_inc(weights_in, 16)

                def body(t, i, p, r, nr):
                    sp.wait_ge(xn_ready, t + 1)
                    ahead = t + 2 if not isinstance(t, int) or t + 2 < NT else None
                    if ahead is not None:
                        n = LAST if isinstance(t, int) and t == NT - 3 else P
                        sp.dma_start(x_in[p][0:n, :], x_d[bass.ds(ahead * P, n), :]).then_inc(x_loaded[p], 16)
                    sp.dma_start(d["xn"][bass.ds(t * P, r), :], xn[p][0:r, :]).then_inc(xn_stored[p], 16)
                    sp.wait_ge(xT_ready, t + 1)
                    sp.dma_start(d["xT"][bass.ds(t * P, P), :].rearrange("k (c n) -> k c n", c=2)[:, :, 0:r],
                                 xT[p][:, :, 0:r]).then_inc(xT_stored[p], 16)
                    sp.wait_ge(p_ready, t + 1)
                    sp.dma_start(d["proj"][bass.ds(t * P, r), :], proj[p][0:r, :]).then_inc(p_stored[p], 16)

                each_tile(sp, body)
                for p in range(2):
                    for stored in (xn_stored, xT_stored, p_stored):
                        sp.wait_ge(stored[p], 16 * ((NT + 1 - p) // 2))

            @block.vector
            def _(dve):
                for p in range(2):
                    nc.vector.memset(v1[p][:, :, 0:1], 1.0)
                    last = nc.vector.memset(feat[p][:, :, FW - 1:FW], SCALE ** 4)
                last.then_inc(const_made, 1)
                dve.wait_ge(const_made, 1)

                def node_norm(t, i, p, r):
                    link = Chain(dve, norm_step, t, 2)
                    dve.wait_ge(x_loaded[p], 16 * (i + 1))
                    link(nc.vector.bn_stats(stats[0:r, :], x_in[p][0:r, :]))
                    carry_wait(dve, c["carrier_dve"])
                    nc.vector.bn_aggr(mv[0:r, :], stats[0:r, :]).then_inc(var_ready, 1)
                    dve.wait_ge(std_ready, t + 1)
                    link(nc.vector.reciprocal(rstd[0:r, :], rstd[0:r, :]))
                    if known(t, 2):
                        dve.wait_ge(xn_stored[p], 16 * i)
                        dve.wait_ge(turned, t - 1)
                    nc.vector.tensor_scalar(xn[p][0:r, :], x_in[p][0:r, :], mv[0:r, 0:1], rstd[0:r, :],
                                            ALU.subtract, ALU.mult).then_inc(xn_ready, 1)
                    dve.wait_ge(xn_ready, t + 1)
                    link.end()

                def keys(t, i, p, r):
                    link = Chain(dve, key_step, t, 8)
                    dve.wait_ge(p_done, t + 1)
                    if known(t, 2):
                        dve.wait_ge(p_stored[p], 16 * i)
                    nc.vector.tensor_tensor(proj[p][0:r, :], ps_p[p][0:r, :], b1_all[0:r, :], ALU.add).then_inc(p_ready, 1)
                    dve.wait_ge(kv_done, t + 1)
                    link(nc.vector.tensor_tensor(k_raw[0:r, :, :], ps_k[p][0:r, 0:D].rearrange("n (h e) -> n h e", h=H),
                                                 bkv_all[0:r, 0:D].rearrange("n (h e) -> n h e", h=H), ALU.add))
                    link(nc.vector.tensor_tensor(k_sq[0:r, :, :], k_raw[0:r, :, :], k_raw[0:r, :, :], ALU.mult))
                    nc.vector.tensor_reduce(ssq[0:r, :], k_sq[0:r, :, :], X, ALU.add).then_inc(ssq_ready, 1)
                    if known(t, 2):
                        dve.wait_ge(feat_used, t - 1)
                    link(nc.vector.tensor_tensor(v1[p][0:r, :, 1:VW], ps_k[p][0:r, D:2 * D].rearrange("n (h e) -> n h e", h=H),
                                                 bkv_all[0:r, D:2 * D].rearrange("n (h e) -> n h e", h=H), ALU.add))
                    dve.wait_ge(norm_ready, t + 1)
                    link(nc.vector.tensor_scalar(norm[0:r, :], norm[0:r, :], NORM_EPS, None, ALU.max))
                    link(nc.vector.reciprocal(norm[0:r, :], norm[0:r, :]))
                    link(nc.vector.scalar_tensor_tensor(kk[0:r, :, 0:HD], k_raw[0:r, :, :], SCALE * SCALE,
                                                        norm[0:r, :].unsqueeze(2).to_broadcast([r, H, HD]), ALU.mult, ALU.mult))
                    link(nc.vector.tensor_copy(kk[0:r, :, HD:HD + HQ], kk[0:r, :, 0:HQ]))
                    products(nc, kk, feat[p], r)
                    nc.vector.tensor_scalar(feat[p][0:r, :, NF:NF + HD], kk[0:r, :, 0:HD], SCALE ** 2, None, ALU.mult)
                    link(nc.vector.tensor_tensor(feat[p][0:r, :, NF + HD:NF + HD + HQ], kk[0:r, :, 0:HQ], kk[0:r, :, HQ:HD], ALU.mult))
                    nc.vector.tensor_scalar(feat[p][0:r, :, 0:HD], feat[p][0:r, :, 0:HD], 0.5, None, ALU.mult).then_inc(feat_ready, 1)
                    dve.wait_ge(feat_ready, t + 1)
                    link.end()

                node_norm(0, 0, 0, P)

                def body(t, i, p, r, nr):
                    if nr:
                        node_norm(t + 1, i + p, 1 - p, nr)
                    if isinstance(t, int) and t == 0:
                        dve.wait_ge(weights_in, 64)
                    keys(t, i, p, r)

                each_tile(dve, body)

            @block.scalar
            def _(act):
                def root(t, i, p, r):
                    act.wait_ge(var_ready, t + 1)
                    nc.scalar.activation(rstd[0:r, :], mv[0:r, 1:2], ACT.Sqrt, bias=c["eps"][0:r, :]).then_inc(std_ready, 1)

                def copy_xT(t, i, p, r):
                    act.wait_ge(turned, t + 1)
                    if known(t, 2):
                        act.wait_ge(xT_stored[p], 16 * i)
                        act.wait_ge(kv_done, t - 1)
                    nc.scalar.activation(xT[p][:, :, 0:r], ps_t[:, p, :, 0:r], ACT.Copy).then_inc(xT_ready, 1)

                root(0, 0, 0, P)
                copy_xT(0, 0, 0, P)

                def body(t, i, p, r, nr):
                    if nr:
                        root(t + 1, i + p, 1 - p, nr)
                        copy_xT(t + 1, i + p, 1 - p, nr)
                    act.wait_ge(ssq_ready, t + 1)
                    nc.scalar.activation(norm[0:r, :], ssq[0:r, :], ACT.Sqrt, scale=SCALE * SCALE).then_inc(norm_ready, 1)

                each_tile(act, body)
                act.wait_ge(feat_used, NT)
                for j in range(3):
                    n = min(3, H - 3 * j)
                    last = nc.scalar.activation(c["sums"][:, 3 * j:3 * j + n, :, :].rearrange("f h b e -> f (h b e)"),
                                                ps_kv[j][:, 0:n * (FB + 1) * VW], ACT.Copy, scale=1.0 / N)
                last.then_inc(sums_read, 1)
                act.wait_ge(sums_read, 1)

            @block.tensor
            def _(pe):
                for j in range(3):
                    nc.tensor.matmul(ps_kv[j][:, :], c["zeros"][:, 0:P], c["zeros"][:, :], start=True, stop=False, skip_group_check=True)

                def turn(t, i, p, r):
                    pe.wait_ge(xn_ready, t + 1)
                    if known(t, 2):
                        pe.wait_ge(xT_ready, t - 1)
                    for k in range(2):
                        last = nc.tensor.transpose(ps_t[:, p, k, 0:r], xn[p][0:r, k * P:(k + 1) * P], c["ident"][0:r, 0:r])
                    last.then_inc(turned, 1)

                def sums(t, i, p, r):
                    pe.wait_ge(feat_ready, t + 1)
                    for h in range(H):
                        for b in range(FB + 1):
                            w = P if b < FB else FT
                            at = ((h % 3) * (FB + 1) + b) * VW
                            last = nc.tensor.matmul(ps_kv[h // 3][0:w, at:at + VW], feat[p][0:r, h, b * P:b * P + w], v1[p][0:r, h, :],
                                                    start=False, stop=False, skip_group_check=True)
                    last.then_inc(feat_used, 1)

                turn(0, 0, 0, P)

                def body(t, i, p, r, nr):
                    if nr:
                        turn(t + 1, i + p, 1 - p, nr)
                    if isinstance(t, int) and t == 0:
                        pe.wait_ge(weights_in, 64)
                    pe.wait_ge(xT_ready, t + 1)
                    if known(t, 2):
                        pe.wait_ge(p_ready, t - 1)
                        pe.wait_ge(feat_ready, t - 1)
                    for k in range(2):
                        last = nc.tensor.matmul(ps_p[p][0:r, :], xT[p][:, k, 0:r], w1a[:, k, :], start=(k == 0), stop=(k == 1))
                    last.then_inc(p_done, 1)
                    for k in range(2):
                        last = nc.tensor.matmul(ps_k[p][0:r, :], xT[p][:, k, 0:r], wkv[:, k, :], start=(k == 0), stop=(k == 1))
                    last.then_inc(kv_done, 1)
                    if known(t, 1):
                        sums(t - 1, None, 1 - p, P)

                each_tile(pe, body)
                sums(NT - 1, NT // 2, 0, LAST)


def products(nc, kk, feat, r):
    one = kk[0:r, :, :]
    step = [list(x) for x in one.ap]
    shifted = bass.AP(tensor=one.tensor, offset=one.offset, ap=[step[0], step[1], [1, NF // HD], [1, HD]])
    return nc.vector.tensor_tensor(feat[0:r, :, 0:NF].rearrange("n h (d i) -> n h d i", i=HD),
                                   kk[0:r, :, 0:HD].unsqueeze(2).to_broadcast([r, H, NF // HD, HD]), shifted, ALU.mult)


def edge_phase(nc, m, c, a, d):
    with Memory(nc, "e_") as l:
        w1b = l.sb("w1b", [P, HID])
        attr = [l.sb(f"attr{p}", [P, G * P]) for p in range(2)]
        idx = [l.sb(f"idx{p}", [P, G], I32) for p in range(2)]
        hid = [l.sb(f"hid{s}", [P, HID]) for s in range(2 * G)]
        hot = [l.sb(f"hot{p}", [P, G, W]) for p in range(2)]
        hot_sum = [l.sb(f"hot_sum{p}", [P, W]) for p in range(2)]
        ps_h = [l.ps(f"ps_h{b}", [P, 512]) for b in range(5)]
        ps_s = [l.ps(f"ps_s{p}", [P, FB + 1, W]) for p in range(2)]
        w_in = l.sem("w_in")

        with nc.Block() as block:
            @block.sync
            def _(sp):
                sp.dma_start(w1b[:, :], a["W1"][D:D + ED, :]).then_inc(w_in, 16)
                sp.wait_ge(w_in, 16)

        sems = {k: l.sem(k) for k in ("idx_ready", "prod_done", "added", "hid_ready", "seg_done", "hot_ready", "hot_summed",
                                      "sum_done", "acc_done")}
        attr_in = [l.sem(f"attr_in{p}") for p in range(2)]
        rows_in = [l.sem(f"rows_in{s}") for s in range(2 * G)]

        passes = nc.values_load(c["passes"][0:1, 0:1], min_val=1, max_val=(N + W - 1) // W + 1)
        with nc.Fori(0, passes):
            edge_pass(nc, c, a, d, w1b, attr, idx, hid, hot, hot_sum, ps_h, ps_s, sems, attr_in, rows_in)
            with nc.Block() as block:
                @block.sync
                def _(sp):
                    for s in list(sems.values()) + attr_in + rows_in:
                        sp.sem_clear(s)

                @block.vector
                def _(dve):
                    nc.vector.tensor_scalar(c["dst_rel"][:, 0:ET], c["dst_rel"][:, 0:ET], float(W), None, ALU.subtract)
                    nc.vector.tensor_scalar(c["dst_rel"][0:EL, ET:ET + 1], c["dst_rel"][0:EL, ET:ET + 1], float(W), None, ALU.subtract)
                    nc.vector.tensor_scalar(c["base"][0:1, :], c["base"][0:1, :], float(W), float(N), ALU.add, ALU.min).then_inc(c["base_moved"], 1)
                    dve.wait_ge(c["base_moved"], 1)
                    nc.vector.tensor_copy(c["base_i"][:, :], c["base"][0:1, :]).then_inc(c["base_moved"], 1)
                    dve.wait_ge(c["base_moved"], 2)
                    dve.sem_clear(c["base_moved"])


def edge_pass(nc, c, a, d, w1b, attr, idx, hid, hot, hot_sum, ps_h, ps_s, sems, attr_in, rows_in):
    idx_ready, prod_done, added, hid_ready = sems["idx_ready"], sems["prod_done"], sems["added"], sems["hid_ready"]
    seg_done, hot_ready, hot_summed = sems["seg_done"], sems["hot_ready"], sems["hot_summed"]
    sum_done, acc_done = sems["sum_done"], sems["acc_done"]

    def each_group(eng, body):
        body(0, 0, 0, G, P)
        body(1, 0, 1, G, P)
        with eng.Fori(1, NG // 2) as i:
            body(2 * i, i, 0, G, P)
            body(2 * i + 1, i, 1, G, P)
        body(NG - 1, NG // 2, 0, G, P)
        body(NG, NG // 2, 1, 1, EL)

    with nc.Block() as block:
        @block.sync
        def _(sp):
            def body(g, i, p, n, r):
                if known(g, 2):
                    sp.wait_ge(prod_done, G * (g - 1))
                sp.dma_start(attr[p][:, 0:(n - 1) * P + r], a["attrT"][:, bass.ds(g * (G * P), (n - 1) * P + r)]).then_inc(attr_in[p], 16)

            each_group(sp, body)

        @block.gpsimd
        def _(pool):
            def body(g, i, p, n, r):
                if known(g, 2):
                    for u in range(G):
                        pool.wait_ge(rows_in[p * G + u], 16 * i)
                nc.gpsimd.tensor_copy(idx[p][0:r, 0:n], c["src"][0:r, bass.ds(g * G, n)]).then_inc(idx_ready, 1)
                pool.wait_ge(idx_ready, g + 1)
                for u in range(n):
                    if known(g, 2):
                        pool.wait_ge(seg_done, (g - 2) * G + u + 1)
                    carry_wait(pool, c["carrier_pool"])
                    nc.gpsimd.indirect_dma_start(
                        out=hid[p * G + u][0:r, :], out_offset=None, in_=d["proj"][:, :],
                        in_offset=bass.IndirectOffsetOnAxis(ap=idx[p][0:r, u:u + 1].bitcast(U32), axis=0)).then_inc(rows_in[p * G + u], 16)

            each_group(pool, body)

        @block.tensor
        def _(pe):
            def segment(g, p, u, n, r):
                pe.wait_ge(hid_ready, g * G + u + 1)
                if u == 0:
                    pe.wait_ge(hot_ready, g + 1)
                    if known(g, 2):
                        pe.wait_ge(acc_done, g - 1)
                for k in range(FB):
                    last = nc.tensor.matmul(ps_s[p][:, k, :], hid[p * G + u][0:r, k * P:(k + 1) * P], hot[p][0:r, u, :],
                                            start=(u == 0 and k == 0), stop=(u == n - 1 and k == FB - 1), skip_group_check=True)
                last.then_inc(seg_done, 1)
                if u == n - 1:
                    pe.wait_ge(hot_summed, g + 1)
                    nc.tensor.matmul(ps_s[p][:, FB, :], c["ones"][0:r, :], hot_sum[p][0:r, :],
                                     start=False, stop=True, skip_group_check=True).then_inc(sum_done, 1)

            def body(g, i, p, n, r):
                for u in range(n):
                    s = p * G + u
                    if u == 0:
                        pe.wait_ge(attr_in[p], 16 * (i + 1))
                    if known(g, 1):
                        pe.wait_ge(added, (g - 1) * G + u + 1)
                    nc.tensor.matmul(ps_h[s % 5][0:r, :], attr[p][:, u * P:u * P + r], w1b[:, :], start=True, stop=True).then_inc(prod_done, 1)
                    if u >= LAG:
                        segment(g, p, u - LAG, n, r)
                    elif known(g, 1):
                        segment(g - 1, 1 - p, u + G - LAG, G, P)

            each_group(pe, body)
            for u in range(G - LAG + 1, G):
                segment(NG - 1, 0, u, G, P)
            segment(NG, 1, 0, 1, EL)

        @block.vector
        def _(dve):
            def add_window(g, p):
                at = dve.value_load(c["base_i"][0:1, bass.ds(g, 1)], min_val=0, max_val=N)
                dve.wait_ge(sum_done, g + 1)
                if known(g, 1):
                    dve.wait_ge(acc_done, g)
                window = c["acc"][:, :, bass.ds(at, W)]
                nc.vector.tensor_tensor(window, ps_s[p][:, :, :], window, ALU.add).then_inc(acc_done, 1)

            def body(g, i, p, n, r):
                if known(g, 2):
                    dve.wait_ge(sum_done, g - 1)
                nc.vector.tensor_tensor(hot[p][0:r, 0:n, :], c["dst_rel"][0:r, bass.ds(g * G, n)].unsqueeze(2).to_broadcast([r, n, W]),
                                        c["iota"][0:r, :].unsqueeze(1).to_broadcast([r, n, W]), ALU.is_equal).then_inc(hot_ready, 1)
                for u in range(n):
                    s = p * G + u
                    dve.wait_ge(prod_done, g * G + u + 1)
                    dve.wait_ge(rows_in[s], 16 * (i + 1))
                    nc.vector.tensor_tensor(hid[s][0:r, :], ps_h[s % 5][0:r, :], hid[s][0:r, :], ALU.add).then_inc(added, 1)
                    if u == 0:
                        dve.wait_ge(hot_ready, g + 1)
                        nc.vector.tensor_reduce(hot_sum[p][0:r, :], hot[p][0:r, 0:n, :].rearrange("e u w -> e w u"), X, ALU.add).then_inc(hot_summed, 1)
                    if u == min(LAG, n - 1) and known(g, 1):
                        add_window(g - 1, 1 - p)

            each_group(dve, body)
            add_window(NG, 1)
            dve.wait_ge(acc_done, NG + 1)

        @block.scalar
        def _(act):
            def body(g, i, p, n, r):
                for u in range(n):
                    act.wait_ge(added, g * G + u + 1)
                    nc.scalar.activation(hid[p * G + u][0:r, :], hid[p * G + u][0:r, :], ACT.Relu).then_inc(hid_ready, 1)

            each_group(act, body)


def update_phase(nc, m, c, a, d):
    with Memory(nc, "u_") as l:
        w2 = l.sb("w2", [P, FB, ED])
        w3 = l.sb("w3", [P, 3, FH])
        w3u = l.sb("w3u", [64, FH])
        u_col = l.sb("u_col", [64, 1])
        w4 = l.sb("w4", [P, FH // P, D])
        wq = l.sb("wq", [P, 2, D])
        wproj = l.sb("wproj", [P, 2, D])
        gate_w = l.sb("gate_w", [P, 2, NE])
        b2 = l.sb("b2", [ED, 1])
        b3 = l.sb("b3", [P, FH // P])
        bq_all = l.sb("bq_all", [P, D])
        b4_all = l.sb("b4_all", [P, D])
        gamma_all = l.sb("gamma_all", [P, D])
        shift_all = l.sb("shift_all", [P, D])
        bproj_all = l.sb("bproj_all", [P, D])
        gate_b_all = l.sb("gate_b_all", [P, NE])
        temp_all = l.sb("temp_all", [P, H])
        x_in = [l.sb(f"x{p}", [P, D]) for p in range(2)]
        xn = [l.sb(f"xn{p}", [P, D]) for p in range(2)]
        xT = [l.sb(f"xT{p}", [P, 2, P]) for p in range(2)]
        q_raw = l.sb("q_raw", [P, H, HD])
        q_sq = l.sb("q_sq", [P, H, HD])
        qq = l.sb("qq", [P, H, HD + HQ])
        feat = [l.sb(f"feat{p}", [P, H, FW]) for p in range(1)] * 2
        featT = l.sb("featT", [P, H + 2, 4, P])
        ssq = l.sb("ssq", [P, H])
        norm = l.sb("norm", [P, H])
        y_inv = l.sb("y_inv", [P, H])
        o = l.sb("o", [P, D])
        oT = l.sb("oT", [P, 2, P])
        cnt = l.sb("cnt", [P, P])
        aggT = [l.sb(f"aggT{p}", [P, P]) for p in range(2)]
        hT = l.sb("hT", [P, FH // P, P])
        y = l.sb("y", [P, D])
        xr = [l.sb(f"xr{p}", [P, D]) for p in range(2)]
        z = [l.sb(f"z{p}", [P, D]) for p in range(2)]
        zT = l.sb("zT", [P, 2, P])
        stats = l.sb("stats", [P, 6])
        mv = l.sb("mv", [P, 2])
        rstd = l.sb("rstd", [P, 1])
        logits = l.sb("logits", [P, NE])
        top_v = l.sb("top_v", [P, 8])
        top_i = l.sb("top_i", [P, 8], U32)
        top_f = l.sb("top_f", [P, 2])
        ps_q = l.ps("ps_q", [P, 512])
        ps_f = [l.ps(f"ps_f{j}", [P, 4, P]) for j in range(2)]
        ps_y = l.ps("ps_y", [P, 512])
        ps_h = [l.ps(f"ps_h{j}", [P, 4, P]) for j in range(2)]
        ps_o = l.ps("ps_o", [P, 512])
        ps_s = l.ps("ps_s", [P, 512])
        ps_turn = ps_s[:, 0:2 * P].rearrange("f (k n) -> f k n", k=2)
        ps_agg = ps_s[:, 2 * P:3 * P]
        ps_gate = ps_s[:, 3 * P:3 * P + NE]
        s = {k: l.sem(k) for k in (
            "weights_in", "b3_done", "b3_ready", "consts_ready", "setup_step", "agg_done", "agg_ready", "mlp1_done", "hT_ready", "q_done", "ssq_ready",
            "norm_ready", "feat_ready", "batch_turned", "batch_copied", "y_done", "o_ready", "o_turned", "oT_ready",
            "mlp2_done", "proj_done", "var1_ready", "std1_ready", "var2_ready", "std2_ready", "z_ready", "z_turned", "zT_ready",
            "gate_done", "routed", "agg_step", "q_step", "o_step", "final_step", "route_step")}
        loaded = [l.sem(f"loaded{p}") for p in range(2)]
        stored = [l.sem(f"stored{p}") for p in range(2)]
        NB = H + 2

        with nc.Block() as block:
            @block.sync
            def _(sp):
                def load(t, p, r):
                    sp.dma_start(x_in[p][0:r, :], a["x"][bass.ds(t * P, r), :]).then_inc(loaded[p], 16)
                    sp.dma_start(xn[p][0:r, :], d["xn"][bass.ds(t * P, r), :]).then_inc(loaded[p], 16)
                    sp.dma_start(xT[p][:, :, 0:r], d["xT"][bass.ds(t * P, P), :].rearrange("k (c n) -> k c n", c=2)[:, :, 0:r]).then_inc(loaded[p], 16)

                w = [
                    (w2[:, :, :], a["W2"].rearrange("(k f) e -> f k e", f=P)),
                    (w3[:, :, :], a["W3"][0:3 * P, :].rearrange("(k f) e -> f k e", f=P)),
                    (w3u[:, :], a["W3"][3 * P:3 * P + 64, :]),
                    (u_col[:, :], a["u"][0:1, :].rearrange("a k -> k a")),
                    (w4[:, :, :], a["W4"].rearrange("(k f) e -> f k e", f=P)),
                    (wq[:, :, :], a["wqkvT"][:, 0:D].rearrange("(k f) e -> f k e", f=P)),
                    (wproj[:, :, :], a["wprojT"].rearrange("(k f) e -> f k e", f=P)),
                    (gate_w[:, :, :], a["gate_w"].rearrange("(k f) e -> f k e", f=P)),
                    (b2[:, :], a["b2"].rearrange("(f a) -> f a", a=1)),
                    (b3[:, :], a["b3"].rearrange("(k f) -> f k", f=P)),
                    (bq_all[:, :], rows(a["bqkv"], P, D)),
                    (b4_all[:, :], rows(a["b4"], P, D)),
                    (gamma_all[:, :], rows(a["gnn_gamma"], P, D)),
                    (shift_all[:, :], rows(a["gnn_beta"], P, D)),
                    (bproj_all[:, :], rows(a["bproj"], P, D)),
                    (gate_b_all[:, :], rows(a["gate_b"], P, NE)),
                    (temp_all[:, :], rows(a["temperature"], P, H)),
                ]
                with nc.allow_non_contiguous_dma(reason="a few bias columns"):
                    for to, frm in w:
                        sp.dma_start(to, frm).then_inc(s["weights_in"], 16)
                sp.wait_ge(s["weights_in"], 16 * len(w))
                sp.sem_inc(s["b3_done"], 1)
                load(0, 0, P)
                load(1, 1, P)

                def body(t, i, p, r, nr):
                    sp.wait_ge(s["z_ready"], t + 1)
                    sp.dma_start(d["xr"][bass.ds(t * P, r), :], xr[p][0:r, :]).then_inc(stored[p], 16)
                    sp.dma_start(d["z"][bass.ds(t * P, r), :], z[p][0:r, :]).then_inc(stored[p], 16)
                    if not isinstance(t, int) or t + 2 < NT:
                        n = LAST if isinstance(t, int) and t == NT - 3 else P
                        load(t + 2, p, n)

                each_tile(sp, body)
                for p in range(2):
                    sp.wait_ge(stored[p], 32 * ((NT + 1 - p) // 2))

            @block.tensor
            def _(pe):
                pe.wait_ge(s["b3_done"], 1)
                for j in range(FH // P):
                    last = nc.tensor.matmul(ps_s[:, j:j + 1], w3u[:, j * P:(j + 1) * P], u_col[:, :], start=(j == 0), stop=(j == FH // P - 1), skip_group_check=True)
                last.then_inc(s["b3_done"], 1)
                pe.wait_ge(s["consts_ready"], 1)

                def query(t, i, p, r):
                    pe.wait_ge(loaded[p], 48 * (i + 1))
                    if known(t, 1):
                        pe.wait_ge(s["ssq_ready"], t)
                    for k in range(2):
                        last = nc.tensor.matmul(ps_q[0:r, 0:D], xT[p][:, k, 0:r], wq[:, k, :], start=(k == 0), stop=(k == 1))
                    last.then_inc(s["q_done"], 1)

                def gate(t, i, p, r):
                    pe.wait_ge(s["z_ready"], t + 1)
                    for k in range(2):
                        last = nc.tensor.transpose(ps_turn[:, k, 0:r], z[p][0:r, k * P:(k + 1) * P], c["ident"][0:r, 0:r])
                    last.then_inc(s["z_turned"], 1)
                    pe.wait_ge(s["zT_ready"], t + 1)
                    for k in range(2):
                        last = nc.tensor.matmul(ps_gate[0:r, :], zT[:, k, 0:r], gate_w[:, k, :], start=(k == 0), stop=(k == 1))
                    last.then_inc(s["gate_done"], 1)

                def turn_batch(t, p, r, b):
                    g = t * NB + b
                    if known(t, 1) or b >= 2:
                        pe.wait_ge(s["batch_copied"], g - 1)
                    if b < 2:
                        carry_wait(pe, c["carrier_pe"])
                    for j in range(4):
                        if b < 2:
                            last = nc.tensor.transpose(ps_f[b % 2][0:FT, j, 0:r], feat[p][0:r, 4 * b + j, NF:FW], c["ident"][0:r, 0:r])
                        else:
                            last = nc.tensor.transpose(ps_f[b % 2][:, j, 0:r], feat[p][0:r, b - 2, j * P:(j + 1) * P], c["ident"][0:r, 0:r])
                    last.then_inc(s["batch_turned"], 1)

                def attend(t, r, h):
                    pe.wait_ge(s["batch_copied"], t * NB + h + 3)
                    for b in range(FB + 1):
                        if b < FB:
                            lhs, rhs = featT[:, h + 2, b, 0:r], c["sums"][:, h, b, :]
                        else:
                            lhs, rhs = featT[0:FT, h // 4, h % 4, 0:r], c["sums"][0:FT, h, b, :]
                        last = nc.tensor.matmul(ps_y[0:r, h * VW:(h + 1) * VW], lhs, rhs, start=(b == 0), stop=(b == FB))
                    return last

                query(0, 0, 0, P)

                def body(t, i, p, r, nr):
                    if known(t, 1):
                        pe.wait_ge(s["agg_ready"], t)
                    for k in range(FB):
                        last = nc.tensor.matmul(ps_agg[:, 0:r], w2[:, k, :], c["acc"][:, k, bass.ds(t * P, r)], start=(k == 0), stop=(k == FB - 1))
                    last.then_inc(s["agg_done"], 1)
                    pe.wait_ge(s["feat_ready"], t + 1)
                    for b in range(NB):
                        turn_batch(t, p, r, b)
                        if b == 3 and known(t, 1):
                            pe.wait_ge(s["o_ready"], t)
                        if b >= 3:
                            attend(t, r, b - 3)
                    if nr:
                        query(t + 1, i + p, 1 - p, nr)
                    pe.wait_ge(s["agg_ready"], t + 1)
                    attend(t, r, H - 1).then_inc(s["y_done"], 1)
                    if known(t, 1):
                        pe.wait_ge(s["hT_ready"], t)
                    for j in range(FH // P):
                        for k in range(3):
                            last = nc.tensor.matmul(ps_h[j // 4][:, j % 4, 0:r], w3[:, k, j * P:(j + 1) * P],
                                                    xT[p][:, k, 0:r] if k < 2 else aggT[p][:, 0:r], start=(k == 0), stop=(k == 2))
                    last.then_inc(s["mlp1_done"], 1)
                    if known(t, 1):
                        gate(t - 1, None, 1 - p, P)
                    if known(t, 1):
                        pe.wait_ge(s["routed"], t)
                    pe.wait_ge(s["o_ready"], t + 1)
                    for k in range(2):
                        last = nc.tensor.transpose(ps_turn[:, k, 0:r], o[0:r, k * P:(k + 1) * P], c["ident"][0:r, 0:r])
                    last.then_inc(s["o_turned"], 1)
                    pe.wait_ge(s["hT_ready"], t + 1)
                    if known(t, 1):
                        pe.wait_ge(s["z_ready"], t)
                    for j in range(FH // P):
                        last = nc.tensor.matmul(ps_o[0:r, 0:D], hT[:, j, 0:r], w4[:, j, :], start=(j == 0), stop=(j == FH // P - 1))
                    last.then_inc(s["mlp2_done"], 1)
                    pe.wait_ge(s["oT_ready"], t + 1)
                    pe.wait_ge(s["final_step"], 11 * t + 1)
                    for k in range(2):
                        last = nc.tensor.matmul(ps_o[0:r, D:2 * D], oT[:, k, 0:r], wproj[:, k, :], start=(k == 0), stop=(k == 1))
                    last.then_inc(s["proj_done"], 1)

                each_tile(pe, body)
                gate(NT - 1, None, 0, LAST)

            @block.scalar
            def _(act):
                def root(t, i, p, r):
                    act.wait_ge(s["ssq_ready"], t + 1)
                    nc.scalar.activation(norm[0:r, :], ssq[0:r, :], ACT.Sqrt, scale=SCALE * SCALE).then_inc(s["norm_ready"], 1)

                def copy_zT(t, r):
                    act.wait_ge(s["z_turned"], t + 1)
                    if known(t, 1):
                        act.wait_ge(s["gate_done"], t)
                    nc.scalar.activation(zT[:, :, 0:r], ps_turn[:, :, 0:r], ACT.Copy).then_inc(s["zT_ready"], 1)

                root(0, 0, 0, P)

                def body(t, i, p, r, nr):
                    for b in range(NB):
                        act.wait_ge(s["batch_turned"], t * NB + b + 1)
                        if known(t, 1) and b == 0:
                            act.wait_ge(s["y_done"], t)
                        w = FT if b < 2 else P
                        nc.scalar.activation(featT[0:w, b, :, 0:r], ps_f[b % 2][0:w, :, 0:r], ACT.Copy).then_inc(s["batch_copied"], 1)
                    if nr:
                        root(t + 1, i + p, 1 - p, nr)
                    act.wait_ge(s["mlp1_done"], t + 1)
                    if known(t, 1):
                        act.wait_ge(s["mlp2_done"], t)
                    for j in range(FH // P):
                        last = nc.scalar.activation(hT[:, j, 0:r], ps_h[j // 4][:, j % 4, 0:r], ACT.Relu, bias=b3[:, j:j + 1])
                    last.then_inc(s["hT_ready"], 1)
                    if known(t, 1):
                        copy_zT(t - 1, P)
                    act.wait_ge(s["o_turned"], t + 1)
                    if known(t, 1):
                        act.wait_ge(s["proj_done"], t)
                    nc.scalar.activation(oT[:, :, 0:r], ps_turn[:, :, 0:r], ACT.Copy).then_inc(s["oT_ready"], 1)
                    for k in ("1", "2"):
                        act.wait_ge(s[f"var{k}_ready"], t + 1)
                        nc.scalar.activation(rstd[0:r, :], mv[0:r, 1:2], ACT.Sqrt, bias=c["eps"][0:r, :]).then_inc(s[f"std{k}_ready"], 1)

                each_tile(act, body)
                copy_zT(NT - 1, LAST)

            @block.vector
            def _(dve):
                link = Chain(dve, s["setup_step"], 0, 4)
                dve.wait_ge(s["b3_done"], 2)
                link(nc.vector.tensor_tensor(b3[:, :], ps_s[:, 0:FH // P], b3[:, :], ALU.add))
                link(nc.vector.tensor_tensor(shift_all[:, :], shift_all[:, :], bproj_all[:, :], ALU.add))
                link(nc.vector.tensor_scalar(temp_all[:, :], temp_all[:, :], SCALE * SCALE, None, ALU.mult))
                link(nc.vector.memset(c["chosen"][:, :, :, :], 0.0))
                nc.vector.memset(c["gate_v"][:, :, :], 0.0)
                nc.vector.memset(feat[0][:, :, FW - 1:FW], 1.0).then_inc(s["consts_ready"], 1)
                dve.wait_ge(s["consts_ready"], 1)

                def queries(t, i, p, r):
                    link = Chain(dve, s["q_step"], t, 7)
                    dve.wait_ge(s["q_done"], t + 1)
                    link(nc.vector.tensor_tensor(q_raw[0:r, :, :], ps_q[0:r, 0:D].rearrange("n (h e) -> n h e", h=H),
                                                 bq_all[0:r, :].rearrange("n (h e) -> n h e", h=H), ALU.add))
                    link(nc.vector.tensor_tensor(q_sq[0:r, :, :], q_raw[0:r, :, :], q_raw[0:r, :, :], ALU.mult))
                    nc.vector.tensor_reduce(ssq[0:r, :], q_sq[0:r, :, :], X, ALU.add).then_inc(s["ssq_ready"], 1)
                    dve.wait_ge(s["norm_ready"], t + 1)
                    link(nc.vector.tensor_scalar(norm[0:r, :], norm[0:r, :], NORM_EPS, None, ALU.max))
                    link(nc.vector.reciprocal(norm[0:r, :], norm[0:r, :]))
                    link(nc.vector.tensor_tensor(norm[0:r, :], norm[0:r, :], temp_all[0:r, :], ALU.mult))
                    link(nc.vector.tensor_tensor(qq[0:r, :, 0:HD], q_raw[0:r, :, :], norm[0:r, :].unsqueeze(2).to_broadcast([r, H, HD]), ALU.mult))
                    link(nc.vector.tensor_copy(qq[0:r, :, HD:HD + HQ], qq[0:r, :, 0:HQ]))
                    if known(t, 1):
                        dve.wait_ge(s["batch_turned"], t * NB)
                    products(nc, qq, feat[p], r)
                    nc.vector.tensor_copy(feat[p][0:r, :, NF:NF + HD], qq[0:r, :, 0:HD])
                    nc.vector.tensor_tensor(feat[p][0:r, :, NF + HD:NF + HD + HQ], qq[0:r, :, 0:HQ], qq[0:r, :, HQ:HD], ALU.mult).then_inc(s["feat_ready"], 1)
                    dve.wait_ge(s["feat_ready"], t + 1)
                    link.end()

                def route(t, p, r):
                    link = Chain(dve, s["route_step"], t, 4)
                    dve.wait_ge(s["gate_done"], t + 1)
                    link(nc.vector.tensor_tensor(logits[0:r, :], ps_gate[0:r, :], gate_b_all[0:r, :], ALU.add))
                    carry_wait(dve, c["carrier_dve"])
                    link(nc.vector.max(top_v[0:r, :], logits[0:r, :]))
                    carry_wait(dve, c["carrier_dve"])
                    link(nc.vector.max_index(top_i[0:r, :], top_v[0:r, :], logits[0:r, :]))
                    link(nc.vector.tensor_copy(top_f[0:r, :], top_i[0:r, 0:2]))
                    nc.vector.tensor_copy(c["gate_v"][0:r, bass.ds(t, 1), :], top_v[0:r, 0:2].unsqueeze(1))
                    for k in range(2):
                        last = nc.vector.tensor_scalar(c["chosen"][0:r, k, bass.ds(t, 1), :], c["iota"][0:r, 0:NE].unsqueeze(1), top_f[0:r, k:k + 1], None, ALU.is_equal)
                    last.then_inc(s["routed"], 1)
                    dve.wait_ge(s["routed"], t + 1)
                    link.end()

                queries(0, 0, 0, P)

                def body(t, i, p, r, nr):
                    link = Chain(dve, s["agg_step"], t, 3)
                    counts = c["acc"][:, FB, bass.ds(t * P, r)]
                    link(nc.vector.tensor_scalar(cnt[:, 0:r], counts, 1.0, None, ALU.max))
                    link(nc.vector.reciprocal(cnt[:, 0:r], cnt[:, 0:r]))
                    dve.wait_ge(s["agg_done"], t + 1)
                    link(nc.vector.scalar_tensor_tensor(aggT[p][:, 0:r], counts, b2[:, 0:1], ps_agg[:, 0:r], ALU.mult, ALU.add))
                    nc.vector.tensor_tensor(aggT[p][:, 0:r], aggT[p][:, 0:r], cnt[:, 0:r], ALU.mult).then_inc(s["agg_ready"], 1)
                    link.end()
                    if nr:
                        queries(t + 1, i + p, 1 - p, nr)
                    link = Chain(dve, s["o_step"], t, 1)
                    dve.wait_ge(s["y_done"], t + 1)
                    heads = ps_y[0:r, 0:H * VW].rearrange("n (h e) -> n h e", h=H)
                    link(nc.vector.reciprocal(y_inv[0:r, :].unsqueeze(2), heads[:, :, 0:1]))
                    if known(t, 1):
                        dve.wait_ge(s["o_turned"], t)
                    nc.vector.tensor_tensor(o[0:r, :].rearrange("n (h e) -> n h e", h=H), heads[:, :, 1:VW],
                                            y_inv[0:r, :].unsqueeze(2).to_broadcast([r, H, HD]), ALU.mult).then_inc(s["o_ready"], 1)
                    link.end()
                    if known(t, 1):
                        route(t - 1, 1 - p, P)
                    link = Chain(dve, s["final_step"], t, 11)
                    dve.wait_ge(s["mlp2_done"], t + 1)
                    link(nc.vector.tensor_tensor(y[0:r, :], ps_o[0:r, 0:D], xn[p][0:r, :], ALU.add))
                    link(nc.vector.tensor_tensor(y[0:r, :], y[0:r, :], b4_all[0:r, :], ALU.add))
                    link(nc.vector.bn_stats(stats[0:r, :], y[0:r, :]))
                    carry_wait(dve, c["carrier_dve"])
                    nc.vector.bn_aggr(mv[0:r, :], stats[0:r, :]).then_inc(s["var1_ready"], 1)
                    dve.wait_ge(s["std1_ready"], t + 1)
                    link(nc.vector.reciprocal(rstd[0:r, :], rstd[0:r, :]))
                    link(nc.vector.tensor_scalar(y[0:r, :], y[0:r, :], mv[0:r, 0:1], rstd[0:r, :], ALU.subtract, ALU.mult))
                    link(nc.vector.tensor_tensor(y[0:r, :], y[0:r, :], gamma_all[0:r, :], ALU.mult))
                    link(nc.vector.tensor_tensor(y[0:r, :], y[0:r, :], shift_all[0:r, :], ALU.add))
                    link(nc.vector.tensor_tensor(y[0:r, :], y[0:r, :], x_in[p][0:r, :], ALU.add))
                    dve.wait_ge(s["proj_done"], t + 1)
                    if known(t, 2):
                        dve.wait_ge(stored[p], 32 * i)
                    link(nc.vector.tensor_tensor(xr[p][0:r, :], ps_o[0:r, D:2 * D], y[0:r, :], ALU.add))
                    link(nc.vector.bn_stats(stats[0:r, :], xr[p][0:r, :]))
                    carry_wait(dve, c["carrier_dve"])
                    nc.vector.bn_aggr(mv[0:r, :], stats[0:r, :]).then_inc(s["var2_ready"], 1)
                    dve.wait_ge(s["std2_ready"], t + 1)
                    link(nc.vector.reciprocal(rstd[0:r, :], rstd[0:r, :]))
                    nc.vector.tensor_scalar(z[p][0:r, :], xr[p][0:r, :], mv[0:r, 0:1], rstd[0:r, :], ALU.subtract, ALU.mult).then_inc(s["z_ready"], 1)
                    dve.wait_ge(s["z_ready"], t + 1)
                    link.end()

                each_tile(dve, body)
                route(NT - 1, 0, LAST)


def route_phase(nc, m, c, a, d):
    with Memory(nc, "r_") as l:
        both = l.sb("both", [P, NT, NE])
        rank = l.sb("rank", [P, NT, NE])
        total = l.sb("total", [P, NT, NE])
        run = l.sb("run", [P, NE])
        tiles_i = l.sb("tiles_i", [P, NE], I32)
        tiles = l.sb("tiles", [P, NE])
        ends = l.sb("ends", [P, NE])
        begins = l.sb("begins", [P, NE])
        prod = l.sb("prod", [P, NT, NE])
        slot_f = l.sb("slot_f", [P, 2, NT])
        over = l.sb("over", [1, MT, NE])
        tile_no = l.sb("tile_no", [1, MT])
        owner = l.sb("owner", [1, MT])
        gap = l.sb("gap", [P, NT])
        z_all = l.sb("z_all", [P, NT, D])
        ps_rank = l.ps("ps_rank", [P, 512])
        ps_total = l.ps("ps_total", [P, 512])
        step = l.sem("step")
        both_ready = l.sem("both_ready")
        ranked = l.sem("ranked")
        gap_ready = l.sem("gap_ready")
        exp_ready = l.sem("exp_ready")
        slots_ready = l.sem("slots_ready")
        z_in = l.sem("z_in")
        placed = [l.sem(f"placed{j}") for j in range(4)]
        iota_made = l.sem("iota_made")
        assert NT * NE <= 512

        with nc.Block() as block:
            @block.sync
            def _(sp):
                sp.dma_start(z_all[:, 0:NT - 1, :], d["z"][0:(NT - 1) * P, :].rearrange("(t n) e -> n t e", n=P)).then_inc(z_in, 16)
                sp.dma_start(z_all[0:LAST, NT - 1, :], d["z"][(NT - 1) * P:N, :]).then_inc(z_in, 16)
                sp.wait_ge(z_in, 32)

            @block.tensor
            def _(pe):
                pe.wait_ge(both_ready, 1)
                flat = both[:, :, :].rearrange("n t e -> n (t e)")
                nc.tensor.matmul(ps_rank[:, 0:NT * NE], c["before"][:, :], flat, start=True, stop=True).then_inc(ranked, 1)
                nc.tensor.matmul(ps_total[:, 0:NT * NE], c["ones"][:, :], flat, start=True, stop=True).then_inc(ranked, 1)

            @block.scalar
            def _(act):
                act.wait_ge(gap_ready, 1)
                nc.scalar.activation(gap[:, :], gap[:, :], ACT.Exp).then_inc(exp_ready, 1)

            @block.vector
            def _(dve):
                n = [0]

                def link(ins):
                    n[0] += 1
                    ins.then_inc(step, 1)
                    dve.wait_ge(step, n[0])

                nc.vector.tensor_tensor(both[:, :, :], c["chosen"][:, 0, :, :], c["chosen"][:, 1, :, :], ALU.add).then_inc(both_ready, 1)
                nc.vector.tensor_tensor(gap[:, :].unsqueeze(2), c["gate_v"][:, :, 1:2], c["gate_v"][:, :, 0:1], ALU.subtract).then_inc(gap_ready, 1)
                dve.wait_ge(exp_ready, 1)
                link(nc.vector.tensor_scalar(c["mix_w"][:, 0, :], gap[:, :], 1.0, None, ALU.add))
                link(nc.vector.reciprocal(c["mix_w"][:, 0, :], c["mix_w"][:, 0, :]))
                link(nc.vector.tensor_tensor(c["mix_w"][:, 1, :], gap[:, :], c["mix_w"][:, 0, :], ALU.mult))
                dve.wait_ge(ranked, 2)
                link(nc.vector.tensor_copy(rank[:, :, :].rearrange("n t e -> n (t e)"), ps_rank[:, 0:NT * NE]))
                link(nc.vector.tensor_copy(total[:, :, :].rearrange("n t e -> n (t e)"), ps_total[:, 0:NT * NE]))
                link(nc.vector.tensor_copy(run[:, :], total[:, 0, :]))
                for t in range(1, NT):
                    link(nc.vector.tensor_tensor(rank[:, t, :], rank[:, t, :], run[:, :], ALU.add))
                    link(nc.vector.tensor_tensor(run[:, :], run[:, :], total[:, t, :], ALU.add))
                link(nc.vector.tensor_scalar(run[:, :], run[:, :], float(P - 1), None, ALU.add))
                link(nc.vector.tensor_copy(tiles_i[:, :], run[:, :]))
                link(nc.vector.tensor_scalar(tiles_i[:, :], tiles_i[:, :], P.bit_length() - 1, None, ALU.arith_shift_right))
                link(nc.vector.tensor_copy(tiles[:, :], tiles_i[:, :]))
                link(nc.vector.tensor_copy(ends[:, 0:1], tiles[:, 0:1]))
                for e in range(1, NE):
                    link(nc.vector.tensor_tensor(ends[:, e:e + 1], ends[:, e - 1:e], tiles[:, e:e + 1], ALU.add))
                link(nc.vector.tensor_tensor(begins[:, :], ends[:, :], tiles[:, :], ALU.subtract))
                link(nc.vector.tensor_scalar(begins[:, :], begins[:, :], float(P), None, ALU.mult))
                link(nc.vector.tensor_tensor(rank[:, :, :], rank[:, :, :], begins[:, :].unsqueeze(1).to_broadcast([P, NT, NE]), ALU.add))
                for k in range(2):
                    link(nc.vector.tensor_tensor(prod[:, :, :], rank[:, :, :], c["chosen"][:, k, :, :], ALU.mult))
                    link(nc.vector.tensor_reduce(slot_f[:, k, :], prod[:, :, :], X, ALU.add))
                nc.vector.tensor_copy(c["slots"][:, :, :], slot_f[:, :, :]).then_inc(slots_ready, 1)
                dve.wait_ge(iota_made, 1)
                link(nc.vector.tensor_tensor(over[:, :, :], ends[0:1, :].unsqueeze(1).to_broadcast([1, MT, NE]),
                                             tile_no[:, :].unsqueeze(2).to_broadcast([1, MT, NE]), ALU.is_le))
                link(nc.vector.tensor_reduce(owner[:, :], over[:, :, :], X, ALU.add))
                link(nc.vector.tensor_scalar(c["owner"][:, :], owner[:, :], float(NE - 1), None, ALU.min))
                for k in range(2):
                    link(nc.vector.tensor_tensor(prod[:, :, :], c["chosen"][:, k, :, :], c["mix_w"][:, k, :].unsqueeze(2).to_broadcast([P, NT, NE]), ALU.mult))
                    if k == 0:
                        link(nc.vector.tensor_copy(c["share"][:, :, :], prod[:, :, :]))
                    else:
                        link(nc.vector.tensor_tensor(c["share"][:, :, :], c["share"][:, :, :], prod[:, :, :], ALU.add))

            @block.gpsimd
            def _(pool):
                nc.gpsimd.iota(tile_no[:, :], pattern=[[1, MT]], base=0, channel_multiplier=0,
                               allow_small_or_imprecise_dtypes=True).then_inc(iota_made, 1)
                pool.wait_ge(slots_ready, 1)
                pool.wait_ge(z_in, 32)
                for t in range(NT):
                    r = P if t < NT - 1 else LAST
                    for k in range(2):
                        j = (2 * t + k) % 4
                        nc.gpsimd.indirect_dma_start(
                            out=d["rows"][:, :], out_offset=bass.IndirectOffsetOnAxis(ap=c["slots"][0:r, k, t:t + 1].bitcast(U32), axis=0),
                            in_=z_all[0:r, t, :], in_offset=None).then_inc(placed[j], 16)
                for j in range(4):
                    pool.wait_ge(placed[j], 16 * ((2 * NT - j + 3) // 4))


def clear_rows(nc, c, d):
    with Memory(nc, "z_") as l:
        cleared = l.sem("cleared")
        with nc.Block() as block:
            @block.sync
            def _(sp):
                view = d["rows"].rearrange("(j n) e -> n j e", n=P)
                half = MT // 2
                for j in range(2):
                    sp.dma_start(view[:, j * half:(j + 1) * half, :],
                                 c["zeros"][:, 0:D].unsqueeze(1).to_broadcast([P, half, D])).then_inc(cleared, 16)
                sp.wait_ge(cleared, 32)


def expert_phase(nc, m, c, a, d):
    with Memory(nc, "m_") as l:
        w1 = [l.sb(f"w1{p}", [P, 2, FE]) for p in range(2)]
        w2 = [l.sb(f"w2{p}", [P, FE // P, D]) for p in range(2)]
        b1 = [l.sb(f"b1{p}", [P, FE // P]) for p in range(2)]
        z = [l.sb(f"z{p}", [P, D]) for p in range(2)]
        zT = [l.sb(f"zT{p}", [P, 2, P]) for p in range(2)]
        hT = [l.sb(f"hT{p}", [P, FE // P, P]) for p in range(2)]
        y = [l.sb(f"y{p}", [P, D]) for p in range(2)]
        ps_t = [l.ps(f"ps_t{p}", [P, 2, P]) for p in range(2)]
        ps_h = [l.ps(f"ps_h{p}", [P, FE // P, P]) for p in range(2)]
        ps_y = [l.ps(f"ps_y{p}", [P, D]) for p in range(2)]
        w_in = [l.sem(f"w_in{p}") for p in range(2)]
        z_in = [l.sem(f"z_in{p}") for p in range(2)]
        y_out = [l.sem(f"y_out{p}") for p in range(2)]
        turned = l.sem("turned")
        zT_ready = l.sem("zT_ready")
        up_done = l.sem("up_done")
        hT_ready = l.sem("hT_ready")
        down_done = l.sem("down_done")
        y_ready = l.sem("y_ready")

        def each(eng, body):
            body(0, 0, 0)
            body(1, 0, 1)
            with eng.Fori(1, MT // 2) as i:
                body(2 * i, i, 0)
                body(2 * i + 1, i, 1)

        with nc.Block() as block:
            @block.sync
            def _(sp):
                def body(t, i, p):
                    e = sp.value_load(c["owner"][0:1, bass.ds(t, 1)], min_val=0, max_val=NE - 1)
                    if known(t, 2):
                        sp.wait_ge(down_done, t - 1)
                    sp.dma_start(z[p][:, :], d["rows"][bass.ds(t * P, P), :]).then_inc(z_in[p], 16)
                    sp.dma_start(w1[p][:, :, :], a["ew1"][bass.ds(e * D, D), :].rearrange("(k f) n -> f k n", f=P)).then_inc(w_in[p], 16)
                    sp.dma_start(b1[p][:, :], a["eb1"][bass.ds(e * P, P), :]).then_inc(w_in[p], 16)
                    sp.dma_start(w2[p][:, :, :], a["ew2"][bass.ds(e * FE, FE), :].rearrange("(k f) n -> f k n", f=P)).then_inc(w_in[p], 16)

                each(sp, body)

            @block.tensor
            def _(pe):
                def turn(t, i, p):
                    pe.wait_ge(z_in[p], 16 * (i + 1))
                    if known(t, 2):
                        pe.wait_ge(zT_ready, t - 1)
                    for k in range(2):
                        last = nc.tensor.transpose(ps_t[p][:, k, :], z[p][:, k * P:(k + 1) * P], c["ident"][:, :])
                    last.then_inc(turned, 1)

                def up(t, i, p):
                    pe.wait_ge(zT_ready, t + 1)
                    pe.wait_ge(w_in[p], 48 * (i + 1))
                    if known(t, 2):
                        pe.wait_ge(hT_ready, t - 1)
                    for f in range(FE // P):
                        for k in range(2):
                            last = nc.tensor.matmul(ps_h[p][:, f, :], w1[p][:, k, f * P:(f + 1) * P], zT[p][:, k, :], start=(k == 0), stop=(k == 1))
                    last.then_inc(up_done, 1)

                def down(t, p):
                    pe.wait_ge(hT_ready, t + 1)
                    if known(t, 2):
                        pe.wait_ge(y_ready, t - 1)
                    for f in range(FE // P):
                        last = nc.tensor.matmul(ps_y[p][:, :], hT[p][:, f, :], w2[p][:, f, :], start=(f == 0), stop=(f == FE // P - 1))
                    last.then_inc(down_done, 1)

                def body(t, i, p):
                    turn(t, i, p)
                    up(t, i, p)
                    if known(t, 1):
                        down(t - 1, 1 - p)

                each(pe, body)
                down(MT - 1, 1)

            @block.scalar
            def _(act):
                def body(t, i, p):
                    act.wait_ge(up_done, t + 1)
                    if known(t, 2):
                        act.wait_ge(down_done, t - 1)
                    for f in range(FE // P):
                        last = nc.scalar.activation(hT[p][:, f, :], ps_h[p][:, f, :], ACT.Relu, bias=b1[p][:, f:f + 1])
                    last.then_inc(hT_ready, 1)

                each(act, body)

            @block.vector
            def _(dve):
                def take(t, p, i):
                    dve.wait_ge(down_done, t + 1)
                    if known(t, 2):
                        dve.wait_ge(y_out[p], 16 * i)
                    nc.vector.tensor_copy(y[p][:, :], ps_y[p][:, :]).then_inc(y_ready, 1)

                def body(t, i, p):
                    dve.wait_ge(turned, t + 1)
                    if known(t, 2):
                        dve.wait_ge(up_done, t - 1)
                    nc.vector.tensor_copy(zT[p][:, :, :], ps_t[p][:, :, :]).then_inc(zT_ready, 1)
                    if known(t, 1):
                        take(t - 1, 1 - p, i - 1 + p)

                each(dve, body)
                take(MT - 1, 1, MT // 2 - 1)

            @block.gpsimd
            def _(pool):
                def body(t, i, p):
                    pool.wait_ge(y_ready, t + 1)
                    pool.dma_start(d["outs"][bass.ds(t * P, P), :], y[p][:, :]).then_inc(y_out[p], 16)

                each(pool, body)
                for p in range(2):
                    pool.wait_ge(y_out[p], 16 * (MT // 2))


def combine_phase(nc, m, c, a, d, out):
    with Memory(nc, "c_") as l:
        eb2 = l.sb("eb2", [NE, D])
        gamma_all = l.sb("gamma_all", [P, D])
        beta_all = l.sb("beta_all", [P, D])
        xr = [l.sb(f"xr{p}", [P, D]) for p in range(2)]
        z = [l.sb(f"z{p}", [P, D]) for p in range(2)]
        y1 = [l.sb(f"y1{p}", [P, D]) for p in range(2)]
        y2 = [l.sb(f"y2{p}", [P, D]) for p in range(2)]
        idx = [l.sb(f"idx{p}", [P, 2], I32) for p in range(2)]
        mix = [l.sb(f"mix{p}", [P, 2]) for p in range(2)]
        share = [l.sb(f"share{p}", [P, NE]) for p in range(2)]
        shareT = [l.sb(f"shareT{p}", [NE, P]) for p in range(2)]
        y = l.sb("y", [P, D])
        res = [l.sb(f"res{p}", [P, D]) for p in range(2)]
        stats = l.sb("stats", [P, 6])
        mv = l.sb("mv", [P, 2])
        rstd = l.sb("rstd", [P, 1])
        ps_t = [l.ps(f"ps_t{p}", [NE, P]) for p in range(2)]
        ps_b = [l.ps(f"ps_b{p}", [P, D]) for p in range(2)]
        weights_in = l.sem("weights_in")
        loaded = [l.sem(f"loaded{p}") for p in range(2)]
        got1 = [l.sem(f"got1{p}") for p in range(2)]
        got2 = [l.sem(f"got2{p}") for p in range(2)]
        stored = [l.sem(f"stored{p}") for p in range(2)]
        picked = l.sem("picked")
        turned = l.sem("turned")
        shareT_ready = l.sem("shareT_ready")
        bias_done = l.sem("bias_done")
        step = l.sem("step")
        var_ready = l.sem("var_ready")
        std_ready = l.sem("std_ready")
        res_ready = l.sem("res_ready")

        with nc.Block() as block:
            @block.sync
            def _(sp):
                def load(t, p, r):
                    sp.dma_start(xr[p][0:r, :], d["xr"][bass.ds(t * P, r), :]).then_inc(loaded[p], 16)
                    sp.dma_start(z[p][0:r, :], d["z"][bass.ds(t * P, r), :]).then_inc(loaded[p], 16)

                sp.dma_start(eb2[:, :], a["eb2"]).then_inc(weights_in, 16)
                sp.dma_start(gamma_all[:, :], rows(a["ffn_gamma"], P, D)).then_inc(weights_in, 16)
                sp.dma_start(beta_all[:, :], rows(a["ffn_beta"], P, D)).then_inc(weights_in, 16)
                load(0, 0, P)
                load(1, 1, P)

                def body(t, i, p, r, nr):
                    sp.wait_ge(res_ready, t + 1)
                    sp.dma_start(out[bass.ds(t * P, r), :], res[p][0:r, :]).then_inc(stored[p], 16)
                    if not isinstance(t, int) or t + 2 < NT:
                        load(t + 2, p, LAST if isinstance(t, int) and t == NT - 3 else P)

                each_tile(sp, body)
                for p in range(2):
                    sp.wait_ge(stored[p], 16 * ((NT + 1 - p) // 2))

            @block.gpsimd
            def _(pool):
                def body(t, i, p, r, nr):
                    if known(t, 2):
                        pool.wait_ge(res_ready, t - 1)
                        pool.wait_ge(turned, t - 1)
                        pool.wait_ge(got1[p], 16 * i)
                        pool.wait_ge(got2[p], 16 * i)
                    nc.gpsimd.tensor_copy(idx[p][0:r, :].unsqueeze(2), c["slots"][0:r, :, bass.ds(t, 1)])
                    nc.gpsimd.tensor_copy(mix[p][0:r, :].unsqueeze(2), c["mix_w"][0:r, :, bass.ds(t, 1)])
                    nc.gpsimd.tensor_copy(share[p][0:r, :].unsqueeze(1), c["share"][0:r, bass.ds(t, 1), :]).then_inc(picked, 1)
                    pool.wait_ge(picked, t + 1)
                    carry_wait(pool, c["carrier_pool"])
                    for k, (to, got) in enumerate(((y1[p], got1[p]), (y2[p], got2[p]))):
                        nc.gpsimd.indirect_dma_start(
                            out=to[0:r, :], out_offset=None, in_=d["outs"][:, :],
                            in_offset=bass.IndirectOffsetOnAxis(ap=idx[p][0:r, k:k + 1].bitcast(U32), axis=0)).then_inc(got, 16)

                each_tile(pool, body)

            @block.tensor
            def _(pe):
                def body(t, i, p, r, nr):
                    pe.wait_ge(picked, t + 1)
                    if known(t, 2):
                        pe.wait_ge(shareT_ready, t - 1)
                        pe.wait_ge(res_ready, t - 1)
                    nc.tensor.transpose(ps_t[p][:, 0:r], share[p][0:r, :], c["ident"][0:r, 0:r]).then_inc(turned, 1)
                    if isinstance(t, int) and t == 0:
                        pe.wait_ge(weights_in, 48)
                    pe.wait_ge(shareT_ready, t + 1)
                    nc.tensor.matmul(ps_b[p][0:r, :], shareT[p][:, 0:r], eb2[:, :], start=True, stop=True).then_inc(bias_done, 1)

                each_tile(pe, body)

            @block.scalar
            def _(act):
                def copy_share(t, i, p, r):
                    act.wait_ge(turned, t + 1)
                    if known(t, 2):
                        act.wait_ge(bias_done, t - 1)
                    nc.scalar.activation(shareT[p][:, 0:r], ps_t[p][:, 0:r], ACT.Copy).then_inc(shareT_ready, 1)

                def body(t, i, p, r, nr):
                    copy_share(t, i, p, r)
                    act.wait_ge(var_ready, t + 1)
                    nc.scalar.activation(rstd[0:r, :], mv[0:r, 1:2], ACT.Sqrt, bias=c["eps"][0:r, :]).then_inc(std_ready, 1)

                each_tile(act, body)

            @block.vector
            def _(dve):
                def body(t, i, p, r, nr):
                    if isinstance(t, int) and t == 0:
                        dve.wait_ge(weights_in, 48)
                    link = Chain(dve, step, t, 8)
                    dve.wait_ge(loaded[p], 32 * (i + 1))
                    dve.wait_ge(bias_done, t + 1)
                    link(nc.vector.tensor_tensor(y[0:r, :], ps_b[p][0:r, :], z[p][0:r, :], ALU.add))
                    for k, (frm, got) in enumerate(((y1[p], got1[p]), (y2[p], got2[p]))):
                        dve.wait_ge(got, 16 * (i + 1))
                        link(nc.vector.scalar_tensor_tensor(y[0:r, :], frm[0:r, :], mix[p][0:r, k:k + 1], y[0:r, :], ALU.mult, ALU.add))
                    link(nc.vector.bn_stats(stats[0:r, :], y[0:r, :]))
                    carry_wait(dve, c["carrier_dve"])
                    nc.vector.bn_aggr(mv[0:r, :], stats[0:r, :]).then_inc(var_ready, 1)
                    dve.wait_ge(std_ready, t + 1)
                    link(nc.vector.reciprocal(rstd[0:r, :], rstd[0:r, :]))
                    link(nc.vector.tensor_scalar(y[0:r, :], y[0:r, :], mv[0:r, 0:1], rstd[0:r, :], ALU.subtract, ALU.mult))
                    link(nc.vector.tensor_tensor(y[0:r, :], y[0:r, :], gamma_all[0:r, :], ALU.mult))
                    if known(t, 2):
                        dve.wait_ge(stored[p], 16 * i)
                    link(nc.vector.tensor_tensor(y[0:r, :], y[0:r, :], beta_all[0:r, :], ALU.add))
                    nc.vector.tensor_tensor(res[p][0:r, :], y[0:r, :], xr[p][0:r, :], ALU.add).then_inc(res_ready, 1)
                    dve.wait_ge(res_ready, t + 1)
                    link.end()

                each_tile(dve, body)


def gps_layer_kernel(nc, a, out):
    with Memory(nc, "k_") as m:
        c = {
            "ident": m.sb("ident", [P, P]),
            "ones": m.sb("ones", [P, P]),
            "before": m.sb("before", [P, P]),
            "zeros": m.sb("zeros", [P, 512]),
            "iota": m.sb("iota", [P, W]),
            "eps": m.sb("eps", [P, 1]),
            "src": m.sb("src", [P, ET + 1], I32),
            "dst_rel": m.sb("dst_rel", [P, ET + 1]),
            "base": m.sb("base", [P, NG + 1]),
            "base_i": m.sb("base_i", [1, NG + 1], I32),
            "passes": m.sb("passes", [1, 1], I32),
            "acc": m.sb("acc", [P, FB + 1, N + W]),
            "sums": m.sb("sums", [P, H, FB + 1, VW]),
            "chosen": m.sb("chosen", [P, 2, NT, NE]),
            "gate_v": m.sb("gate_v", [P, NT, 2]),
            "mix_w": m.sb("mix_w", [P, 2, NT]),
            "slots": m.sb("slots", [P, 2, NT], I32),
            "share": m.sb("share", [P, NT, NE]),
            "owner": m.sb("owner", [1, MT], I32),
            "base_moved": m.sem("base_moved"),
            "carrier_dve": m.sem("carrier_dve"),
            "carrier_pool": m.sem("carrier_pool"),
            "carrier_pe": m.sem("carrier_pe"),
        }
        d = {
            "xn": nc.dram_tensor("xn_kept", [N, D], F32, kind="Internal").ap(),
            "xT": nc.dram_tensor("xT_kept", [NT * P, 2 * P], F32, kind="Internal").ap(),
            "proj": nc.dram_tensor("proj_kept", [N, HID], F32, kind="Internal").ap(),
            "xr": nc.dram_tensor("xr_kept", [N, D], F32, kind="Internal").ap(),
            "z": nc.dram_tensor("z_kept", [N, D], F32, kind="Internal").ap(),
            "rows": nc.dram_tensor("rows_kept", [MT * P, D], F32, kind="Internal").ap(),
            "outs": nc.dram_tensor("outs_kept", [MT * P, D], F32, kind="Internal").ap(),
        }
        setup_phase(nc, m, c, a)
        clear_rows(nc, c, d)
        node_phase(nc, m, c, a, d)
        edge_phase(nc, m, c, a, d)
        update_phase(nc, m, c, a, d)
        route_phase(nc, m, c, a, d)
        expert_phase(nc, m, c, a, d)
        combine_phase(nc, m, c, a, d, out)


def _layout(inputs):
    import numpy as np

    def arr(k):
        return np.asarray(inputs[k])

    src, dst = arr("src"), arr("dst")
    whole = ET * P
    return {
        "x": arr("x"),
        "dst": dst,
        "dst_cols": dst[:whole].reshape(ET, P).T,
        "dst_tail": dst[whole:].reshape(EL, 1),
        "src_cols": src[:whole].reshape(ET, P).T,
        "src_tail": src[whole:].reshape(EL, 1),
        "attrT": arr("edge_attr_128").T,
        "u": arr("L0_gnn_u"),
        "W1": arr("L0_gnn_W1"), "b1": arr("L0_gnn_b1"), "W2": arr("L0_gnn_W2"), "b2": arr("L0_gnn_b2"),
        "W3": arr("L0_gnn_W3"), "b3": arr("L0_gnn_b3"), "W4": arr("L0_gnn_W4"), "b4": arr("L0_gnn_b4"),
        "gnn_gamma": arr("L0_gnn_gamma"), "gnn_beta": arr("L0_gnn_beta"),
        "wqkvT": arr("L0_mix_Wqkv").T, "bqkv": arr("L0_mix_bqkv"),
        "wprojT": arr("L0_mix_Wproj").T, "bproj": arr("L0_mix_bproj"),
        "temperature": arr("L0_mix_temperature").reshape(H),
        "gate_w": arr("L0_ffn_gate_w"), "gate_b": arr("L0_ffn_gate_b"),
        "ew1": arr("L0_ffn_w1").reshape(NE * D, FE),
        "eb1": arr("L0_ffn_b1").reshape(NE, FE // P, P).transpose(0, 2, 1).reshape(NE * P, FE // P),
        "ew2": arr("L0_ffn_w2").reshape(NE * FE, D),
        "eb2": arr("L0_ffn_b2"),
        "ffn_gamma": arr("L0_ffn_gamma"), "ffn_beta": arr("L0_ffn_beta"),
    }


def kernel(**inputs):
    import numpy as np
    import concourse.bacc as bacc
    from concourse.bass_utils import run_bass_kernel_spmd

    nc = bacc.Bacc("TRN2", target_bir_lowering=False, num_devices=1)
    arrays, aps = {}, {}
    for name, value in _layout(inputs).items():
        value = np.ascontiguousarray(value)
        arrays[f"in_{name}"] = value
        aps[name] = nc.dram_tensor(f"in_{name}", value.shape, mybir.dt.from_np(value.dtype), kind="ExternalInput").ap()
    out = nc.dram_tensor("out_0", (N, D), F32, kind="ExternalOutput").ap()
    gps_layer_kernel(nc, aps, out)
    r = run_bass_kernel_spmd(nc, [arrays], core_ids=[0])
    return r.results[0]["out_0"]
```

```python
import concourse.bass as bass
from concourse import mybir
from contextlib import ExitStack

F32 = mybir.dt.float32
F32R = mybir.dt.float32r
BF16 = mybir.dt.bfloat16
I32 = mybir.dt.int32
U32 = mybir.dt.uint32
ALU = mybir.AluOpType
ACT = mybir.ActivationFunctionType
X = mybir.AxisListType.X

P = 128
N = 3125
D = 256
ED = 128
HID = 512
E = 53125
NT = (N + P - 1) // P
LAST = N - (NT - 1) * P
ET = E // P
EL = E - ET * P
G = 5
NG = ET // G
assert NG * G == ET and NG % 2 == 1 and NT % 2 == 1
W = 64
LAG = 3
H = 8
HD = D // H
HQ = HD // 2
NF = 16 * HD
FT = HD + HQ + 1
FW = NF + FT
FB = NF // P
VW = HD + 1
FH = 4 * D
NE = 16
FE = 512
MT = (2 * N + NE * (P - 1)) // P
DEEP = 4
SET = 4
assert MT % DEEP == 0 and NE % SET == 0
SCALE = float(HD) ** 0.25
VN = 96
ZN = VN - VW
LN_EPS = 1e-5
NORM_EPS = 1e-12


def rows(ap, n, width, start=0):
    return bass.AP(tensor=ap.tensor, offset=ap.offset + start, ap=[[0, n], [1, width]])


class Chain:

    def __init__(self, eng, sem, turn, per):
        self.eng, self.sem, self.start, self.per, self.n = eng, sem, turn * per, per, 0

    def __call__(self, ins):
        self.n += 1
        assert self.n <= self.per
        ins.then_inc(self.sem, 1)
        self.eng.wait_ge(self.sem, self.start + self.n)

    def end(self):
        assert self.n == self.per, (self.n, self.per)


def each_tile(eng, body):
    body(0, 0, 0, P, P)
    body(1, 0, 1, P, P)
    half = NT // 2
    with eng.Fori(1, half - 1) as i:
        body(2 * i, i, 0, P, P)
        body(2 * i + 1, i, 1, P, P)
    body(NT - 3, half - 1, 0, P, P)
    body(NT - 2, half - 1, 1, P, LAST)
    body(NT - 1, half, 0, LAST, 0)


def known(t, least):
    return not isinstance(t, int) or t >= least


def known_before(t, end):
    return not isinstance(t, int) or t < end


def tile_rows(t):
    return LAST if isinstance(t, int) and t == NT - 1 else P


def carry_wait(eng, carrier):
    eng.sem_inc(carrier, 1)


class Memory:

    def __init__(self, nc, tag):
        self.nc, self.tag, self.ctx = nc, tag, ExitStack()

    def __enter__(self):
        self.ctx.__enter__()
        return self

    def __exit__(self, *a):
        return self.ctx.__exit__(*a)

    def sb(self, name, shape, dt=F32):
        return self.ctx.enter_context(self.nc.sbuf_tensor(self.tag + name, shape, dt))

    def ps(self, name, shape):
        return self.ctx.enter_context(self.nc.psum_tensor(self.tag + name, shape, F32))

    def sem(self, name):
        return self.ctx.enter_context(self.nc.semaphore(self.tag + name))


def setup_phase(nc, m, c, a):
    with Memory(nc, "s_") as l:
        groups_i = l.sb("groups_i", [NG + 1, G * P], I32)
        lohi = l.sb("lohi", [NG + 1, 2])
        lo_rows = l.sb("lo_rows", [NG + 1, P])
        hi_rows = l.sb("hi_rows", [NG + 1, P])
        dst_i = l.sb("dst_i", [P, ET + 1], I32)
        span = l.sb("span", [P, NG + 1])
        widest = l.sb("widest", [1, 1])
        windows_i = l.sb("windows_i", [1, 1], I32)
        ps_lo = l.ps("ps_lo", [P, 512])
        ps_hi = l.ps("ps_hi", [P, 512])
        dst_in = l.sem("dst_in")
        src_in = l.sem("src_in")
        filled = l.sem("filled")
        ident_made = l.sem("ident_made")
        masks_made = l.sem("masks_made")
        step = l.sem("step")
        lohi_made = l.sem("lohi_made")
        spread = l.sem("spread")

        with nc.Block() as block:
            @block.sync
            def _(sp):
                sp.dma_start(groups_i[0:NG, :], a["dst"][0:NG * G * P].rearrange("(g e) -> g e", g=NG)).then_inc(dst_in, 16)
                sp.dma_start(groups_i[NG:NG + 1, :], a["dst"][E - G * P:E].rearrange("(g e) -> g e", g=1)).then_inc(dst_in, 16)
                sp.dma_start(dst_i[:, 0:ET], a["dst_cols"]).then_inc(dst_in, 16)
                sp.dma_start(dst_i[0:EL, ET:ET + 1], a["dst_tail"]).then_inc(dst_in, 16)
                sp.dma_start(c["src"][:, 0:ET], a["src_cols"]).then_inc(src_in, 16)
                sp.dma_start(c["src"][0:EL, ET:ET + 1], a["src_tail"]).then_inc(src_in, 16)
                sp.wait_ge(src_in, 32)

            @block.gpsimd
            def _(pool):
                nc.gpsimd.memset(c["ident"][:, :], 0.0).then_inc(filled, 1)
                nc.gpsimd.memset(c["ones"][:, :], 1.0).then_inc(filled, 1)
                nc.gpsimd.memset(c["before"][:, :], 1.0).then_inc(filled, 1)
                nc.gpsimd.memset(c["zeros"][:, :], 0.0).then_inc(filled, 1)
                pool.wait_ge(filled, 4)
                nc.gpsimd.affine_select(out=c["ident"][:, :], in_=c["ident"][:, :], compare_op=ALU.not_equal,
                                        fill=1.0, base=0, pattern=[[-1, P]], channel_multiplier=1).then_inc(ident_made, 1)
                nc.gpsimd.affine_select(out=c["before"][:, :], in_=c["before"][:, :], compare_op=ALU.is_gt,
                                        fill=0.0, base=0, pattern=[[1, P]], channel_multiplier=-1).then_inc(masks_made, 1)
                nc.gpsimd.iota(c["iota"][:, :], pattern=[[1, W]], base=0, channel_multiplier=0,
                               allow_small_or_imprecise_dtypes=True).then_inc(masks_made, 1)
                pool.wait_ge(masks_made, 2)

            @block.vector
            def _(dve):
                n = [0]

                def link(ins):
                    n[0] += 1
                    ins.then_inc(step, 1)
                    dve.wait_ge(step, n[0])

                link(nc.vector.memset(c["eps"][:, :], LN_EPS))
                link(nc.vector.memset(c["sums"][:, :, H:H + 2, :], 0.0))
                link(nc.vector.memset(lo_rows[:, :], 1.0))
                dve.wait_ge(dst_in, 64)
                link(nc.vector.tensor_reduce(lohi[:, 0:1], groups_i[:, :], X, ALU.min))
                link(nc.vector.tensor_reduce(lohi[:, 1:2], groups_i[:, :], X, ALU.max))
                link(nc.vector.tensor_scalar(hi_rows[:, :], lo_rows[:, :], lohi[:, 1:2], None, ALU.mult))
                link(nc.vector.tensor_scalar(lo_rows[:, :], lo_rows[:, :], lohi[:, 0:1], None, ALU.mult))
                nc.vector.tensor_copy(c["dst_rel"][:, 0:ET], dst_i[:, 0:ET]).then_inc(lohi_made, 1)
                dve.wait_ge(lohi_made, 1)
                link(nc.vector.tensor_copy(c["dst_rel"][0:EL, ET:ET + 1], dst_i[0:EL, ET:ET + 1]))
                dve.wait_ge(spread, 2)
                link(nc.vector.tensor_copy(c["base"][:, :], ps_lo[:, 0:NG + 1]))
                link(nc.vector.tensor_tensor(span[:, :], ps_hi[:, 0:NG + 1], c["base"][:, :], ALU.subtract))
                link(nc.vector.tensor_reduce(widest[:, :], span[0:1, :], X, ALU.max))
                link(nc.vector.tensor_copy(windows_i[:, :], widest[:, :]))
                link(nc.vector.tensor_scalar(windows_i[:, :], windows_i[:, :], W.bit_length() - 1, None, ALU.arith_shift_right))
                link(nc.vector.tensor_scalar(c["passes"][:, :], windows_i[:, :], 1, None, ALU.add))
                link(nc.vector.tensor_copy(c["base_i"][:, :], c["base"][0:1, :]))
                view = c["dst_rel"][:, 0:ET].rearrange("p (g u) -> p g u", u=G)
                link(nc.vector.tensor_tensor(view, view, c["base"][:, 0:NG].unsqueeze(2).to_broadcast([P, NG, G]), ALU.subtract))
                link(nc.vector.tensor_tensor(c["dst_rel"][0:EL, ET:ET + 1], c["dst_rel"][0:EL, ET:ET + 1],
                                             c["base"][0:EL, NG:NG + 1], ALU.subtract))

            @block.tensor
            def _(pe):
                pe.wait_ge(ident_made, 1)
                pe.wait_ge(lohi_made, 1)
                nc.tensor.matmul(ps_lo[:, 0:NG + 1], lo_rows[:, :], c["ident"][0:NG + 1, 0:NG + 1], start=True, stop=True).then_inc(spread, 1)
                nc.tensor.matmul(ps_hi[:, 0:NG + 1], hi_rows[:, :], c["ident"][0:NG + 1, 0:NG + 1], start=True, stop=True).then_inc(spread, 1)


def node_phase(nc, m, c, a, d):
    with Memory(nc, "a_") as l:
        w1a = l.sb("w1a", [P, 2, HID])
        wkv = l.sb("wkv", [P, 2, 2 * D])
        b1_all = l.sb("b1_all", [P, HID])
        bkv_all = l.sb("bkv_all", [P, 2 * D])
        x_in = [l.sb(f"x{p}", [P, D]) for p in range(2)]
        xn = [l.sb(f"xn{p}", [P, D]) for p in range(2)]
        xT = [l.sb(f"xT{p}", [P, 2, P]) for p in range(2)]
        proj = [l.sb(f"proj{p}", [P, HID]) for p in range(2)]
        v1 = [l.sb(f"v1{p}", [P, H, VN + ZN]) for p in range(2)]
        feat = [l.sb(f"feat{p}", [P, H, FW]) for p in range(2)]
        k_raw = l.sb("k_raw", [P, H, HD])
        k_sq = l.sb("k_sq", [P, H, HD])
        kk = l.sb("kk", [P, H, HD + HQ])
        stats = l.sb("stats", [P, 6])
        mv = l.sb("mv", [P, 2])
        rstd = l.sb("rstd", [P, 1])
        ssq = l.sb("ssq", [P, H])
        norm = l.sb("norm", [P, H])
        ps_kv = [l.ps(f"ps_sum{j}", [P, 512]) for j in range(3)]
        ps_t = l.ps("ps_t", [P, 2, 2, P])
        ps_p = [l.ps(f"ps_p{p}", [P, 512]) for p in range(2)]
        ps_k = [l.ps(f"ps_k{p}", [P, 512]) for p in range(2)]
        weights_in = l.sem("weights_in")
        x_loaded = [l.sem(f"x_loaded{p}") for p in range(2)]
        xn_stored = [l.sem(f"xn_stored{p}") for p in range(2)]
        xT_stored = [l.sem(f"xT_stored{p}") for p in range(2)]
        p_stored = [l.sem(f"p_stored{p}") for p in range(2)]
        const_made = l.sem("const_made")
        v1_cleared = l.sem("v1_cleared")
        var_ready = l.sem("var_ready")
        std_ready = l.sem("std_ready")
        xn_ready = l.sem("xn_ready")
        turned = l.sem("turned")
        xT_ready = l.sem("xT_ready")
        p_done = l.sem("p_done")
        kv_done = l.sem("kv_done")
        p_ready = l.sem("p_ready")
        ssq_ready = l.sem("ssq_ready")
        norm_ready = l.sem("norm_ready")
        feat_ready = l.sem("feat_ready")
        feat_used = l.sem("feat_used")
        sums_read = l.sem("sums_read")
        norm_step = l.sem("norm_step")
        key_step = l.sem("key_step")
        rows_cleared = l.sem("rows_cleared")
        acc_cleared = l.sem("acc_cleared")
        x_d, wkv_d = a["x"], a["wqkvT"]

        with nc.Block() as block:
            @block.gpsimd
            def _(pool):
                for k in range(FB + 1):
                    nc.gpsimd.memset(c["acc"][:, k, :], 0.0).then_inc(acc_cleared, 1)
                view = d["rows"].rearrange("(j n) e -> n j e", n=P)
                half = MT // 2
                for j in range(2):
                    pool.dma_start(view[:, j * half:(j + 1) * half, :],
                                   c["zeros"][:, 0:D].unsqueeze(1).to_broadcast([P, half, D])).then_inc(rows_cleared, 16)
                pool.wait_ge(rows_cleared, 32)
                pool.wait_ge(acc_cleared, FB + 1)

            @block.sync
            def _(sp):
                for p in range(2):
                    sp.dma_start(x_in[p][:, :], x_d[p * P:(p + 1) * P, :]).then_inc(x_loaded[p], 16)
                sp.dma_start(w1a[:, :, :], a["W1"][0:D, :].rearrange("(c k) f -> k c f", c=2)).then_inc(weights_in, 16)
                sp.dma_start(wkv[:, :, :], wkv_d[:, D:3 * D].rearrange("(c k) f -> k c f", c=2)).then_inc(weights_in, 16)
                sp.dma_start(b1_all[:, :], rows(a["b1"], P, HID)).then_inc(weights_in, 16)
                sp.dma_start(bkv_all[:, :], rows(a["bqkv"], P, 2 * D, D)).then_inc(weights_in, 16)

                def body(t, i, p, r, nr):
                    sp.wait_ge(xn_ready, t + 1)
                    ahead = t + 2 if not isinstance(t, int) or t + 2 < NT else None
                    if ahead is not None:
                        n = LAST if isinstance(t, int) and t == NT - 3 else P
                        sp.dma_start(x_in[p][0:n, :], x_d[bass.ds(ahead * P, n), :]).then_inc(x_loaded[p], 16)
                    sp.dma_start(d["xn"][bass.ds(t * P, r), :], xn[p][0:r, :]).then_inc(xn_stored[p], 16)
                    sp.wait_ge(xT_ready, t + 1)
                    sp.dma_start(d["xT"][bass.ds(t * P, P), :].rearrange("k (c n) -> k c n", c=2)[:, :, 0:r],
                                 xT[p][:, :, 0:r]).then_inc(xT_stored[p], 16)
                    sp.wait_ge(p_ready, t + 1)
                    sp.dma_start(d["proj"][bass.ds(t * P, r), :], proj[p][0:r, :]).then_inc(p_stored[p], 16)

                each_tile(sp, body)
                for p in range(2):
                    for stored in (xn_stored, xT_stored, p_stored):
                        sp.wait_ge(stored[p], 16 * ((NT + 1 - p) // 2))

            @block.vector
            def _(dve):
                for p in range(2):
                    nc.vector.memset(v1[p][:, :, :], 0.0).then_inc(v1_cleared, 1)
                dve.wait_ge(v1_cleared, 2)
                for p in range(2):
                    nc.vector.memset(v1[p][:, :, ZN:ZN + 1], 1.0)
                    last = nc.vector.memset(feat[p][:, :, FW - 1:FW], SCALE ** 4)
                last.then_inc(const_made, 1)
                dve.wait_ge(const_made, 1)

                def node_norm(t, i, p, r):
                    link = Chain(dve, norm_step, t, 2)
                    dve.wait_ge(x_loaded[p], 16 * (i + 1))
                    link(nc.vector.bn_stats(stats[0:r, :], x_in[p][0:r, :]))
                    carry_wait(dve, c["carrier_dve"])
                    nc.vector.bn_aggr(mv[0:r, :], stats[0:r, :]).then_inc(var_ready, 1)
                    dve.wait_ge(std_ready, t + 1)
                    link(nc.vector.reciprocal(rstd[0:r, :], rstd[0:r, :]))
                    if known(t, 2):
                        dve.wait_ge(xn_stored[p], 16 * i)
                        dve.wait_ge(turned, t - 1)
                    nc.vector.tensor_scalar(xn[p][0:r, :], x_in[p][0:r, :], mv[0:r, 0:1], rstd[0:r, :],
                                            ALU.subtract, ALU.mult).then_inc(xn_ready, 1)
                    dve.wait_ge(xn_ready, t + 1)
                    link.end()

                def keys(t, i, p, r):
                    link = Chain(dve, key_step, t, 8)
                    dve.wait_ge(p_done, t + 1)
                    if known(t, 2):
                        dve.wait_ge(p_stored[p], 16 * i)
                    nc.vector.tensor_tensor(proj[p][0:r, :], ps_p[p][0:r, :], b1_all[0:r, :], ALU.add).then_inc(p_ready, 1)
                    dve.wait_ge(kv_done, t + 1)
                    link(nc.vector.tensor_tensor(k_raw[0:r, :, :], ps_k[p][0:r, 0:D].rearrange("n (h e) -> n h e", h=H),
                                                 bkv_all[0:r, 0:D].rearrange("n (h e) -> n h e", h=H), ALU.add))
                    link(nc.vector.tensor_tensor(k_sq[0:r, :, :], k_raw[0:r, :, :], k_raw[0:r, :, :], ALU.mult))
                    nc.vector.tensor_reduce(ssq[0:r, :], k_sq[0:r, :, :], X, ALU.add).then_inc(ssq_ready, 1)
                    if known(t, 2):
                        dve.wait_ge(feat_used, t - 1)
                    link(nc.vector.tensor_tensor(v1[p][0:r, :, ZN + 1:ZN + VW], ps_k[p][0:r, D:2 * D].rearrange("n (h e) -> n h e", h=H),
                                                 bkv_all[0:r, D:2 * D].rearrange("n (h e) -> n h e", h=H), ALU.add))
                    dve.wait_ge(norm_ready, t + 1)
                    link(nc.vector.tensor_scalar(norm[0:r, :], norm[0:r, :], NORM_EPS, None, ALU.max))
                    link(nc.vector.reciprocal(norm[0:r, :], norm[0:r, :]))
                    link(nc.vector.scalar_tensor_tensor(kk[0:r, :, 0:HD], k_raw[0:r, :, :], SCALE * SCALE,
                                                        norm[0:r, :].unsqueeze(2).to_broadcast([r, H, HD]), ALU.mult, ALU.mult))
                    link(nc.vector.tensor_copy(kk[0:r, :, HD:HD + HQ], kk[0:r, :, 0:HQ]))
                    products(nc, kk, feat[p], r)
                    nc.vector.tensor_scalar(feat[p][0:r, :, NF:NF + HD], kk[0:r, :, 0:HD], SCALE ** 2, None, ALU.mult)
                    link(nc.vector.tensor_tensor(feat[p][0:r, :, NF + HD:NF + HD + HQ], kk[0:r, :, 0:HQ], kk[0:r, :, HQ:HD], ALU.mult))
                    nc.vector.tensor_scalar(feat[p][0:r, :, 0:HD], feat[p][0:r, :, 0:HD], 0.5, None, ALU.mult).then_inc(feat_ready, 1)
                    dve.wait_ge(feat_ready, t + 1)
                    link.end()

                node_norm(0, 0, 0, P)
                node_norm(1, 0, 1, P)
                dve.wait_ge(weights_in, 64)

                def body(t, i, p, r, nr):
                    keys(t, i, p, r)
                    if known_before(t, NT - 2):
                        node_norm(t + 2, i + 1, p, tile_rows(t + 2))

                each_tile(dve, body)

            @block.scalar
            def _(act):
                def root(t, i, p, r):
                    act.wait_ge(var_ready, t + 1)
                    nc.scalar.activation(rstd[0:r, :], mv[0:r, 1:2], ACT.Sqrt, bias=c["eps"][0:r, :]).then_inc(std_ready, 1)

                def copy_xT(t, i, p, r):
                    act.wait_ge(turned, t + 1)
                    if known(t, 2):
                        act.wait_ge(xT_stored[p], 16 * i)
                        act.wait_ge(kv_done, t - 1)
                    nc.scalar.activation(xT[p][:, :, 0:r], ps_t[:, p, :, 0:r], ACT.Copy).then_inc(xT_ready, 1)

                root(0, 0, 0, P)
                root(1, 0, 1, P)
                copy_xT(0, 0, 0, P)

                def body(t, i, p, r, nr):
                    if nr:
                        copy_xT(t + 1, i + p, 1 - p, nr)
                    act.wait_ge(ssq_ready, t + 1)
                    nc.scalar.activation(norm[0:r, :], ssq[0:r, :], ACT.Sqrt, scale=SCALE * SCALE).then_inc(norm_ready, 1)
                    if known_before(t, NT - 2):
                        root(t + 2, i + 1, p, tile_rows(t + 2))

                each_tile(act, body)
                act.wait_ge(feat_used, NT)
                for j in range(3):
                    n = min(3, H - 3 * j)
                    last = nc.scalar.activation(c["sums"][:, :, 3 * j:3 * j + n, :].rearrange("f b h e -> f h b e"),
                                                ps_kv[j][:, 0:n * (FB + 1) * VW].rearrange("f (h b e) -> f h b e", h=n, e=VW), ACT.Copy, scale=1.0 / N)
                last.then_inc(sums_read, 1)
                act.wait_ge(sums_read, 1)

            @block.tensor
            def _(pe):
                for j in range(3):
                    nc.tensor.matmul(ps_kv[j][:, :], c["zeros"][:, 0:P], c["zeros"][:, :], start=True, stop=False, skip_group_check=True)

                def turn(t, i, p, r):
                    pe.wait_ge(xn_ready, t + 1)
                    if known(t, 1):
                        pe.wait_ge(xT_ready, t)
                    for k in range(2):
                        last = nc.tensor.transpose(ps_t[:, p, k, 0:r], xn[p][0:r, k * P:(k + 1) * P], c["ident"][0:r, 0:r])
                    last.then_inc(turned, 1)

                def sums(t, i, p, r):
                    pe.wait_ge(feat_ready, t + 1)
                    for h in range(H):
                        for b in range(FB + 1):
                            w = P if b < FB else FT
                            at = ((h % 3) * (FB + 1) + b) * VW
                            back = max(0, at + VN - 512)
                            last = nc.tensor.matmul(ps_kv[h // 3][0:w, at - back:at - back + VN], feat[p][0:r, h, b * P:b * P + w],
                                                    v1[p][0:r, h, ZN - back:ZN - back + VN],
                                                    start=False, stop=False, skip_group_check=True)
                    last.then_inc(feat_used, 1)

                turn(0, 0, 0, P)

                def body(t, i, p, r, nr):
                    if isinstance(t, int) and t == 0:
                        pe.wait_ge(weights_in, 64)
                    pe.wait_ge(xT_ready, t + 1)
                    if known(t, 2):
                        pe.wait_ge(p_ready, t - 1)
                        pe.wait_ge(feat_ready, t - 1)
                    for k in range(2):
                        last = nc.tensor.matmul(ps_p[p][0:r, :], xT[p][:, k, 0:r], w1a[:, k, :], start=(k == 0), stop=(k == 1))
                    last.then_inc(p_done, 1)
                    for k in range(2):
                        last = nc.tensor.matmul(ps_k[p][0:r, :], xT[p][:, k, 0:r], wkv[:, k, :], start=(k == 0), stop=(k == 1))
                    last.then_inc(kv_done, 1)
                    if nr:
                        turn(t + 1, i + p, 1 - p, nr)
                    if known(t, 1):
                        sums(t - 1, None, 1 - p, P)

                each_tile(pe, body)
                sums(NT - 1, NT // 2, 0, LAST)


def products(nc, kk, feat, r):
    one = kk[0:r, :, :]
    step = [list(x) for x in one.ap]
    shifted = bass.AP(tensor=one.tensor, offset=one.offset, ap=[step[0], step[1], [1, NF // HD], [1, HD]])
    return nc.vector.tensor_tensor(feat[0:r, :, 0:NF].rearrange("n h (d i) -> n h d i", i=HD),
                                   kk[0:r, :, 0:HD].unsqueeze(2).to_broadcast([r, H, NF // HD, HD]), shifted, ALU.mult)


def edge_phase(nc, m, c, a, d):
    with Memory(nc, "e_") as l:
        w1b = l.sb("w1b", [P, HID])
        attr = [l.sb(f"attr{p}", [P, G * P]) for p in range(2)]
        idx = [l.sb(f"idx{p}", [P, G], I32) for p in range(2)]
        hid = [l.sb(f"hid{s}", [P, HID]) for s in range(2 * G)]
        high = [l.sb(f"high{u}", [P, HID], F32R) for u in range(G)]
        low = [l.sb(f"low{u}", [P, HID], F32R) for u in range(G)]
        hot = [l.sb(f"hot{p}", [P, G, W], F32R) for p in range(2)]
        hot_sum = [l.sb(f"hot_sum{p}", [P, W], BF16) for p in range(2)]
        window = [l.sb(f"window{p}", [W, HID]) for p in range(2)]
        ones = l.sb("ones", [P, P], BF16)
        ps_h = [l.ps(f"ps_h{b}", [P, 512]) for b in range(4)]
        ps_w = [l.ps(f"ps_w{p}", [W, 512]) for p in range(2)]
        ps_s = [l.ps(f"ps_s{p}", [P, FB + 1, W]) for p in range(2)]
        w_in = l.sem("w_in")
        ones_made = l.sem("ones_made")

        with nc.Block() as block:
            @block.sync
            def _(sp):
                sp.dma_start(w1b[:, :], a["W1"][D:D + ED, :]).then_inc(w_in, 16)
                sp.wait_ge(w_in, 16)

            @block.vector
            def _(dve):
                nc.vector.memset(ones[:, :], 1.0).then_inc(ones_made, 1)
                dve.wait_ge(ones_made, 1)

        sems = {k: l.sem(k) for k in ("idx_ready", "prod_done", "added", "high_ready", "low_ready", "seg_done", "hot_ready",
                                      "hot_summed", "window_ready", "sum_done", "acc_done")}
        attr_in = [l.sem(f"attr_in{p}") for p in range(2)]
        rows_in = [l.sem(f"rows_in{s}") for s in range(2 * G)]

        everything = (nc, c, a, d, w1b, attr, idx, hid, high, low, hot, hot_sum, window, ones, ps_h, ps_w, ps_s,
                      sems, attr_in, rows_in)
        passes = nc.values_load(c["passes"][0:1, 0:1], min_val=1, max_val=(N + W - 1) // W + 1)
        edge_pass(*everything)
        with nc.If(passes > 1):
            with nc.Fori(1, passes):
                with nc.Block() as block:
                    @block.gpsimd
                    def _(pool):
                        pool.dma_reset()
                        for s in rows_in:
                            pool.sem_clear(s)

                    @block.sync
                    def _(sp):
                        for s in list(sems.values()) + attr_in:
                            sp.sem_clear(s)

                    @block.vector
                    def _(dve):
                        nc.vector.tensor_scalar(c["dst_rel"][:, 0:ET], c["dst_rel"][:, 0:ET], float(W), None, ALU.subtract)
                        nc.vector.tensor_scalar(c["dst_rel"][0:EL, ET:ET + 1], c["dst_rel"][0:EL, ET:ET + 1], float(W), None, ALU.subtract)
                        nc.vector.tensor_scalar(c["base"][0:1, :], c["base"][0:1, :], float(W), float(N), ALU.add, ALU.min).then_inc(c["base_moved"], 1)
                        dve.wait_ge(c["base_moved"], 1)
                        nc.vector.tensor_copy(c["base_i"][:, :], c["base"][0:1, :]).then_inc(c["base_moved"], 1)
                        dve.wait_ge(c["base_moved"], 2)
                        dve.sem_clear(c["base_moved"])

                edge_pass(*everything)
        nc.end_ifs()


def edge_pass(nc, c, a, d, w1b, attr, idx, hid, high, low, hot, hot_sum, window, ones, ps_h, ps_w, ps_s,
              sems, attr_in, rows_in):
    idx_ready, prod_done, added, high_ready = sems["idx_ready"], sems["prod_done"], sems["added"], sems["high_ready"]
    low_ready, seg_done, hot_ready, hot_summed = sems["low_ready"], sems["seg_done"], sems["hot_ready"], sems["hot_summed"]
    window_ready, sum_done, acc_done = sems["window_ready"], sems["sum_done"], sems["acc_done"]

    def each_group(eng, body):
        body(0, 0, 0, G, P)
        body(1, 0, 1, G, P)
        with eng.Fori(1, NG // 2) as i:
            body(2 * i, i, 0, G, P)
            body(2 * i + 1, i, 1, G, P)
        body(NG - 1, NG // 2, 0, G, P)
        body(NG, NG // 2, 1, 1, EL)

    banks = [0, 1, 2, 3, 0, 1, 2, 3, 1, 2]
    assert len(banks) == 2 * G
    back = [next(k for k in range(1, 2 * G + 1) if banks[s - k] == banks[s]) for s in range(2 * G)]

    with nc.Block() as block:
        @block.sync
        def _(sp):
            def body(g, i, p, n, r):
                if known(g, 2):
                    sp.wait_ge(prod_done, G * (g - 1))
                sp.dma_start(attr[p][:, 0:(n - 1) * P + r], a["attrT"][:, bass.ds(g * (G * P), (n - 1) * P + r)]).then_inc(attr_in[p], 16)

            each_group(sp, body)

        @block.gpsimd
        def _(pool):
            def body(g, i, p, n, r):
                if known(g, 2):
                    for u in range(G):
                        pool.wait_ge(rows_in[p * G + u], 16 * i)
                nc.gpsimd.tensor_copy(idx[p][0:r, 0:n], c["src"][0:r, bass.ds(g * G, n)]).then_inc(idx_ready, 1)
                pool.wait_ge(idx_ready, g + 1)
                for u in range(n):
                    if known(g, 2):
                        pool.wait_ge(low_ready, (g - 2) * G + u + 1)
                    carry_wait(pool, c["carrier_pool"])
                    nc.gpsimd.indirect_dma_start(
                        out=hid[p * G + u][0:r, :], out_offset=None, in_=d["proj"][:, :],
                        in_offset=bass.IndirectOffsetOnAxis(ap=idx[p][0:r, u:u + 1].bitcast(U32), axis=0)).then_inc(rows_in[p * G + u], 16)

            each_group(pool, body)

        @block.tensor
        def _(pe):
            def segment(g, p, u, n, r):
                pe.wait_ge(low_ready, g * G + u + 1)
                if u == 0:
                    pe.wait_ge(hot_ready, g + 1)
                    if known(g, 2):
                        pe.wait_ge(window_ready, g - 1)
                nc.tensor.matmul(ps_w[p][:, :], hot[p][0:r, u, :], high[u][0:r, :], start=(u == 0), stop=False)
                nc.tensor.matmul(ps_w[p][:, :], hot[p][0:r, u, :], low[u][0:r, :], start=False, stop=(u == n - 1)).then_inc(seg_done, 1)

            def turn_window(g, p, r):
                pe.wait_ge(window_ready, g + 1)
                pe.wait_ge(hot_summed, g + 1)
                if known(g, 2):
                    pe.wait_ge(acc_done, g - 1)
                    carry_wait(pe, c["carrier_pe"])
                for k in range(FB):
                    nc.tensor.transpose(ps_s[p][:, k, :], window[p][:, k * P:(k + 1) * P], c["ident"][0:W, 0:W])
                nc.tensor.matmul(ps_s[p][:, FB, :], ones[0:r, :], hot_sum[p][0:r, :], start=True, stop=True).then_inc(sum_done, 1)

            def body(g, i, p, n, r):
                for u in range(n):
                    if u == 0:
                        pe.wait_ge(attr_in[p], 16 * (i + 1))
                    s = p * G + u
                    if known(g * G + u, back[s]):
                        pe.wait_ge(added, g * G + u - back[s] + 1)
                    nc.tensor.matmul(ps_h[banks[s]][0:r, :], attr[p][:, u * P:u * P + r], w1b[:, :], start=True, stop=True).then_inc(prod_done, 1)
                    if u >= LAG:
                        segment(g, p, u - LAG, n, r)
                    elif known(g, 1):
                        segment(g - 1, 1 - p, u + G - LAG, G, P)
                    if u == G - 1 and known(g, 1):
                        turn_window(g - 1, 1 - p, P)

            each_group(pe, body)
            for u in range(G - LAG + 1, G):
                segment(NG - 1, 0, u, G, P)
            segment(NG, 1, 0, 1, EL)
            turn_window(NG - 1, 0, P)
            turn_window(NG, 1, EL)

        @block.vector
        def _(dve):
            def add_window(g, p):
                at = dve.value_load(c["base_i"][0:1, bass.ds(g, 1)], min_val=0, max_val=N)
                dve.wait_ge(sum_done, g + 1)
                if known(g, 1):
                    dve.wait_ge(acc_done, g)
                nodes = c["acc"][:, :, bass.ds(at, W)]
                nc.vector.tensor_tensor(nodes, ps_s[p][:, :, :], nodes, ALU.add).then_inc(acc_done, 1)

            def split(g, p, u, r):
                dve.wait_ge(high_ready, g * G + u + 1)
                nc.vector.scalar_tensor_tensor(low[u][0:r, :], hid[p * G + u][0:r, :], 0.0, high[u][0:r, :],
                                               ALU.max, ALU.subtract).then_inc(low_ready, 1)

            def body(g, i, p, n, r):
                if known(g, 2):
                    dve.wait_ge(seg_done, G * (g - 1))
                    dve.wait_ge(sum_done, g - 1)
                nc.vector.tensor_tensor(hot[p][0:r, 0:n, :], c["dst_rel"][0:r, bass.ds(g * G, n)].unsqueeze(2).to_broadcast([r, n, W]),
                                        c["iota"][0:r, :].unsqueeze(1).to_broadcast([r, n, W]), ALU.is_equal).then_inc(hot_ready, 1)
                for u in range(n):
                    s = p * G + u
                    dve.wait_ge(prod_done, g * G + u + 1)
                    dve.wait_ge(rows_in[s], 16 * (i + 1))
                    nc.vector.tensor_tensor(hid[s][0:r, :], ps_h[banks[s]][0:r, :], hid[s][0:r, :], ALU.add).then_inc(added, 1)
                    if u >= 1:
                        split(g, p, u - 1, r)
                    elif known(g, 1):
                        split(g - 1, 1 - p, G - 1, P)
                    if u == 0:
                        dve.wait_ge(hot_ready, g + 1)
                        with nc.allow_low_precision("counts up to G are exact"):
                            nc.vector.tensor_reduce(hot_sum[p][0:r, :], hot[p][0:r, 0:n, :].rearrange("e u w -> e w u"), X, ALU.add).then_inc(hot_summed, 1)
                        if known(g, 2):
                            add_window(g - 2, p)

            each_group(dve, body)
            split(NG, 1, 0, EL)
            add_window(NG - 1, 0)
            add_window(NG, 1)
            dve.wait_ge(acc_done, NG + 1)

        @block.scalar
        def _(act):
            def copy_window(g, p, n):
                act.wait_ge(seg_done, g * G + n)
                if known(g, 2):
                    act.wait_ge(sum_done, g - 1)
                nc.scalar.activation(window[p][:, :], ps_w[p][:, :], ACT.Copy).then_inc(window_ready, 1)

            def body(g, i, p, n, r):
                for u in range(n):
                    act.wait_ge(added, g * G + u + 1)
                    if known(g, 1):
                        act.wait_ge(seg_done, (g - 1) * G + u + 1)
                    nc.scalar.activation(high[u][0:r, :], hid[p * G + u][0:r, :], ACT.Relu).then_inc(high_ready, 1)
                    if u == 2 and known(g, 1):
                        copy_window(g - 1, 1 - p, G)

            each_group(act, body)
            copy_window(NG - 1, 0, G)
            copy_window(NG, 1, 1)


def update_phase(nc, m, c, a, d):
    with Memory(nc, "u_") as l:
        w2 = l.sb("w2", [P, FB, ED])
        w3 = l.sb("w3", [P, 3, FH])
        w3u = l.sb("w3u", [64, FH])
        u_col = l.sb("u_col", [64, 1])
        w4 = l.sb("w4", [P, FH // P, D])
        wq = l.sb("wq", [P, 2, D])
        wproj = l.sb("wproj", [P, 2, D])
        gate_w = l.sb("gate_w", [P, 2, VN])
        b2 = l.sb("b2", [ED, 1])
        b3 = l.sb("b3", [P, FH // P])
        bq_all = l.sb("bq_all", [P, D])
        b4_all = l.sb("b4_all", [P, D])
        gamma_all = l.sb("gamma_all", [P, D])
        shift_all = l.sb("shift_all", [P, D])
        bproj_all = l.sb("bproj_all", [P, D])
        gate_b_all = l.sb("gate_b_all", [P, NE])
        temp_all = l.sb("temp_all", [P, H])
        x_in = [l.sb(f"x{p}", [P, D]) for p in range(2)]
        xn = [l.sb(f"xn{p}", [P, D]) for p in range(2)]
        xT = [l.sb(f"xT{p}", [P, 2, P]) for p in range(2)]
        q_raw = l.sb("q_raw", [P, H, HD])
        q_sq = l.sb("q_sq", [P, H, HD])
        qq = l.sb("qq", [P, H, HD + HQ])
        feat = [l.sb(f"feat{p}", [P, H, FW]) for p in range(2)]
        featT = l.sb("featT", [P, H + 2, 4, P])
        ssq = l.sb("ssq", [P, H])
        norm = l.sb("norm", [P, H])
        y_inv = l.sb("y_inv", [P, H])
        o = l.sb("o", [P, D])
        oT = l.sb("oT", [P, 2, P])
        cnt = l.sb("cnt", [P, P])
        aggT = [l.sb(f"aggT{p}", [P, P]) for p in range(2)]
        hT = l.sb("hT", [P, FH // P, P])
        y = l.sb("y", [P, D])
        xr = [l.sb(f"xr{p}", [P, D]) for p in range(2)]
        z = [l.sb(f"z{p}", [P, D]) for p in range(2)]
        zT = l.sb("zT", [P, 2, P])
        stats = l.sb("stats", [P, 6])
        mv = l.sb("mv", [P, 2])
        rstd = l.sb("rstd", [P, 1])
        logits = l.sb("logits", [P, NE])
        top_v = l.sb("top_v", [P, 8])
        top_i = l.sb("top_i", [P, 8], U32)
        top_f = l.sb("top_f", [P, 2])
        ps_q = l.ps("ps_q", [P, 512])
        ps_f = [l.ps(f"ps_f{j}", [P, 4, P]) for j in range(2)]
        ps_y = l.ps("ps_y", [P, 512])
        ps_h = [l.ps(f"ps_h{j}", [P, 4, P]) for j in range(2)]
        ps_o = l.ps("ps_o", [P, 512])
        ps_s = l.ps("ps_s", [P, 512])
        ps_turn = ps_s[:, 0:2 * P].rearrange("f (k n) -> f k n", k=2)
        ps_agg = ps_y[:, 3 * P:4 * P]
        assert (H + 2) * VW <= 3 * P
        ps_gate = ps_s[:, 3 * P:3 * P + VN]
        s = {k: l.sem(k) for k in (
            "weights_in", "b3_done", "b3_ready", "consts_ready", "setup_step", "agg_done", "agg_ready", "mlp1_done", "hT_ready", "q_done", "ssq_ready",
            "norm_ready", "feat_ready", "batch_turned", "batch_copied", "y_done", "o_ready", "o_turned", "oT_ready",
            "mlp2_done", "proj_done", "var1_ready", "std1_ready", "var2_ready", "std2_ready", "z_ready", "z_turned", "zT_ready",
            "gate_done", "routed", "agg_step", "q_step", "o_step", "final_step", "route_step")}
        loaded = [l.sem(f"loaded{p}") for p in range(2)]
        stored = [l.sem(f"stored{p}") for p in range(2)]
        NB = H + 2

        with nc.Block() as block:
            @block.sync
            def _(sp):
                def load(t, p, r):
                    sp.dma_start(x_in[p][0:r, :], a["x"][bass.ds(t * P, r), :]).then_inc(loaded[p], 16)
                    sp.dma_start(xn[p][0:r, :], d["xn"][bass.ds(t * P, r), :]).then_inc(loaded[p], 16)
                    sp.dma_start(xT[p][:, :, 0:r], d["xT"][bass.ds(t * P, P), :].rearrange("k (c n) -> k c n", c=2)[:, :, 0:r]).then_inc(loaded[p], 16)

                w = [
                    (w2[:, :, :], a["W2"].rearrange("(k f) e -> f k e", f=P)),
                    (w3[:, :, :], a["W3"][0:3 * P, :].rearrange("(k f) e -> f k e", f=P)),
                    (w3u[:, :], a["W3"][3 * P:3 * P + 64, :]),
                    (u_col[:, :], a["u"][0:1, :].rearrange("a k -> k a")),
                    (w4[:, :, :], a["W4"].rearrange("(k f) e -> f k e", f=P)),
                    (wq[:, :, :], a["wqkvT"][:, 0:D].rearrange("(k f) e -> f k e", f=P)),
                    (wproj[:, :, :], a["wprojT"].rearrange("(k f) e -> f k e", f=P)),
                    (gate_w[:, :, 0:NE], a["gate_w"].rearrange("(k f) e -> f k e", f=P)),
                    (b2[:, :], a["b2"].rearrange("(f a) -> f a", a=1)),
                    (b3[:, :], a["b3"].rearrange("(k f) -> f k", f=P)),
                    (bq_all[:, :], rows(a["bqkv"], P, D)),
                    (b4_all[:, :], rows(a["b4"], P, D)),
                    (gamma_all[:, :], rows(a["gnn_gamma"], P, D)),
                    (shift_all[:, :], rows(a["gnn_beta"], P, D)),
                    (bproj_all[:, :], rows(a["bproj"], P, D)),
                    (gate_b_all[:, :], rows(a["gate_b"], P, NE)),
                    (temp_all[:, :], rows(a["temperature"], P, H)),
                ]
                with nc.allow_non_contiguous_dma(reason="a few bias columns"):
                    for to, frm in w:
                        sp.dma_start(to, frm).then_inc(s["weights_in"], 16)
                sp.wait_ge(s["weights_in"], 16 * len(w))
                sp.sem_inc(s["b3_done"], 1)
                load(0, 0, P)
                load(1, 1, P)

                def body(t, i, p, r, nr):
                    sp.wait_ge(s["z_ready"], t + 1)
                    sp.dma_start(d["xr"][bass.ds(t * P, r), :], xr[p][0:r, :]).then_inc(stored[p], 16)
                    sp.dma_start(d["z"][bass.ds(t * P, r), :], z[p][0:r, :]).then_inc(stored[p], 16)
                    if not isinstance(t, int) or t + 2 < NT:
                        n = LAST if isinstance(t, int) and t == NT - 3 else P
                        load(t + 2, p, n)

                each_tile(sp, body)
                for p in range(2):
                    sp.wait_ge(stored[p], 32 * ((NT + 1 - p) // 2))

            @block.tensor
            def _(pe):
                pe.wait_ge(s["b3_done"], 1)
                for j in range(FH // P):
                    last = nc.tensor.matmul(ps_s[:, j:j + 1], w3u[:, j * P:(j + 1) * P], u_col[:, :], start=(j == 0), stop=(j == FH // P - 1), skip_group_check=True)
                last.then_inc(s["b3_done"], 1)
                pe.wait_ge(s["consts_ready"], 1)

                def query(t, i, p, r):
                    pe.wait_ge(loaded[p], 48 * (i + 1))
                    if known(t, 2):
                        pe.wait_ge(s["z_ready"], t - 1)
                    for k in range(2):
                        last = nc.tensor.matmul(ps_q[0:r, 0:D], xT[p][:, k, 0:r], wq[:, k, :], start=(k == 0), stop=(k == 1))
                    last.then_inc(s["q_done"], 1)

                def turn_z(t, p, r):
                    pe.wait_ge(s["z_ready"], t + 1)
                    for k in range(2):
                        last = nc.tensor.transpose(ps_turn[:, k, 0:r], z[p][0:r, k * P:(k + 1) * P], c["ident"][0:r, 0:r])
                    last.then_inc(s["z_turned"], 1)

                def gate(t, r):
                    pe.wait_ge(s["zT_ready"], t + 1)
                    for k in range(2):
                        last = nc.tensor.matmul(ps_gate[0:r, :], zT[:, k, 0:r], gate_w[:, k, :], start=(k == 0), stop=(k == 1))
                    last.then_inc(s["gate_done"], 1)

                def turn_batch(t, p, r, b):
                    g = t * NB + b
                    if known(t, 1) or b >= 2:
                        pe.wait_ge(s["batch_copied"], g - 1)
                    if b < 2:
                        carry_wait(pe, c["carrier_pe"])
                    for j in range(4):
                        if b < 2:
                            last = nc.tensor.transpose(ps_f[b % 2][0:FT, j, 0:r], feat[p][0:r, 4 * b + j, NF:FW], c["ident"][0:r, 0:r])
                        else:
                            last = nc.tensor.transpose(ps_f[b % 2][:, j, 0:r], feat[p][0:r, b - 2, j * P:(j + 1) * P], c["ident"][0:r, 0:r])
                    last.then_inc(s["batch_turned"], 1)

                def attend(t, r, h):
                    pe.wait_ge(s["batch_copied"], t * NB + h + 3)
                    for b in range(FB + 1):
                        if b < FB:
                            lhs, rhs = featT[:, h + 2, b, 0:r], c["sums"][:, b, h:h + 3, :]
                        else:
                            lhs, rhs = featT[0:FT, h // 4, h % 4, 0:r], c["sums"][0:FT, b, h:h + 3, :]
                        last = nc.tensor.matmul(ps_y[0:r, h * VW:(h + 3) * VW], lhs, rhs, start=(b == 0), stop=(b == FB))
                    return last

                def aggregate(t, i, p, r):
                    if known(t, 1):
                        pe.wait_ge(s["o_ready"], t)
                    for k in range(FB):
                        last = nc.tensor.matmul(ps_agg[:, 0:r], w2[:, k, :], c["acc"][:, k, bass.ds(t * P, r)], start=(k == 0), stop=(k == FB - 1))
                    last.then_inc(s["agg_done"], 1)

                query(0, 0, 0, P)
                aggregate(0, 0, 0, P)

                def body(t, i, p, r, nr):
                    pe.wait_ge(s["agg_ready"], t + 1)
                    if known(t, 1):
                        pe.wait_ge(s["hT_ready"], 2 * t)
                    for j in range(FH // P):
                        for k in range(3):
                            last = nc.tensor.matmul(ps_h[j // 4][:, j % 4, 0:r], w3[:, k, j * P:(j + 1) * P],
                                                    xT[p][:, k, 0:r] if k < 2 else aggT[p][:, 0:r], start=(k == 0), stop=(k == 2))
                        if j % 4 == 3:
                            last.then_inc(s["mlp1_done"], 1)
                    pe.wait_ge(s["feat_ready"], t + 1)
                    for b in range(NB):
                        turn_batch(t, p, r, b)
                        if b == 3 and known(t, 1):
                            pe.wait_ge(s["o_ready"], t)
                        if b >= 3:
                            attend(t, r, b - 3)
                        if b == 5:
                            if nr:
                                query(t + 1, i + p, 1 - p, nr)
                        if b == 8 and known(t, 1):
                            turn_z(t - 1, 1 - p, P)
                    attend(t, r, H - 1).then_inc(s["y_done"], 1)
                    if known(t, 1):
                        gate(t - 1, P)
                    pe.wait_ge(s["hT_ready"], 2 * t + 2)
                    if known(t, 1):
                        pe.wait_ge(s["z_ready"], t)
                    for j in range(FH // P):
                        last = nc.tensor.matmul(ps_o[0:r, 0:D], hT[:, j, 0:r], w4[:, j, :], start=(j == 0), stop=(j == FH // P - 1))
                    last.then_inc(s["mlp2_done"], 1)
                    pe.wait_ge(s["o_ready"], t + 1)
                    if known(t, 1):
                        pe.wait_ge(s["routed"], t)
                    for k in range(2):
                        last = nc.tensor.transpose(ps_turn[:, k, 0:r], o[0:r, k * P:(k + 1) * P], c["ident"][0:r, 0:r])
                    last.then_inc(s["o_turned"], 1)
                    if nr:
                        aggregate(t + 1, None, None, nr)
                    pe.wait_ge(s["oT_ready"], t + 1)
                    if nr:
                        pe.wait_ge(s["ssq_ready"], t + 2)
                    for k in range(2):
                        last = nc.tensor.matmul(ps_q[0:r, D:2 * D], oT[:, k, 0:r], wproj[:, k, :], start=(k == 0), stop=(k == 1))
                    last.then_inc(s["proj_done"], 1)

                each_tile(pe, body)
                turn_z(NT - 1, 0, LAST)
                gate(NT - 1, LAST)

            @block.scalar
            def _(act):
                def root(t, i, p, r):
                    act.wait_ge(s["ssq_ready"], t + 1)
                    nc.scalar.activation(norm[0:r, :], ssq[0:r, :], ACT.Sqrt, scale=SCALE * SCALE).then_inc(s["norm_ready"], 1)

                def copy_zT(t, r):
                    act.wait_ge(s["z_turned"], t + 1)
                    if known(t, 1):
                        act.wait_ge(s["gate_done"], t)
                    nc.scalar.activation(zT[:, :, 0:r], ps_turn[:, :, 0:r], ACT.Copy).then_inc(s["zT_ready"], 1)

                root(0, 0, 0, P)

                def relu(t, r, half):
                    act.wait_ge(s["mlp1_done"], 2 * t + half + 1)
                    if known(t, 1):
                        act.wait_ge(s["mlp2_done"], t)
                    for j in range(4 * half, 4 * half + 4):
                        last = nc.scalar.activation(hT[:, j, 0:r], ps_h[half][:, j % 4, 0:r], ACT.Relu, bias=b3[:, j:j + 1])
                    last.then_inc(s["hT_ready"], 1)

                def body(t, i, p, r, nr):
                    for b in range(NB):
                        act.wait_ge(s["batch_turned"], t * NB + b + 1)
                        if known(t, 1) and b == 0:
                            act.wait_ge(s["y_done"], t)
                        w = FT if b < 2 else P
                        nc.scalar.activation(featT[0:w, b, :, 0:r], ps_f[b % 2][0:w, :, 0:r], ACT.Copy).then_inc(s["batch_copied"], 1)
                        if b == 3:
                            relu(t, r, 1)
                        if b == 6 and nr:
                            root(t + 1, i + p, 1 - p, nr)
                    if known(t, 1):
                        copy_zT(t - 1, P)
                    act.wait_ge(s["o_turned"], t + 1)
                    if known(t, 1):
                        act.wait_ge(s["proj_done"], t)
                    nc.scalar.activation(oT[:, :, 0:r], ps_turn[:, :, 0:r], ACT.Copy).then_inc(s["oT_ready"], 1)
                    for k in ("1", "2"):
                        act.wait_ge(s[f"var{k}_ready"], t + 1)
                        nc.scalar.activation(rstd[0:r, :], mv[0:r, 1:2], ACT.Sqrt, bias=c["eps"][0:r, :]).then_inc(s[f"std{k}_ready"], 1)
                        if k == "1" and nr:
                            relu(t + 1, nr, 0)

                relu(0, P, 0)
                each_tile(act, body)
                copy_zT(NT - 1, LAST)

            @block.vector
            def _(dve):
                link = Chain(dve, s["setup_step"], 0, 4)
                dve.wait_ge(s["b3_done"], 2)
                link(nc.vector.tensor_tensor(b3[:, :], ps_s[:, 0:FH // P], b3[:, :], ALU.add))
                link(nc.vector.tensor_tensor(shift_all[:, :], shift_all[:, :], bproj_all[:, :], ALU.add))
                link(nc.vector.tensor_scalar(temp_all[:, :], temp_all[:, :], SCALE * SCALE, None, ALU.mult))
                link(nc.vector.memset(c["chosen"][:, :, :, :], 0.0))
                nc.vector.memset(c["gate_v"][:, :, :], 0.0)
                nc.vector.memset(gate_w[:, :, NE:VN], 0.0)
                for p in range(2):
                    last = nc.vector.memset(feat[p][:, :, FW - 1:FW], 1.0)
                last.then_inc(s["consts_ready"], 1)
                dve.wait_ge(s["consts_ready"], 1)

                def queries(t, i, p, r):
                    link = Chain(dve, s["q_step"], t, 7)
                    dve.wait_ge(s["q_done"], t + 1)
                    link(nc.vector.tensor_tensor(q_raw[0:r, :, :], ps_q[0:r, 0:D].rearrange("n (h e) -> n h e", h=H),
                                                 bq_all[0:r, :].rearrange("n (h e) -> n h e", h=H), ALU.add))
                    link(nc.vector.tensor_tensor(q_sq[0:r, :, :], q_raw[0:r, :, :], q_raw[0:r, :, :], ALU.mult))
                    nc.vector.tensor_reduce(ssq[0:r, :], q_sq[0:r, :, :], X, ALU.add).then_inc(s["ssq_ready"], 1)
                    dve.wait_ge(s["norm_ready"], t + 1)
                    link(nc.vector.tensor_scalar(norm[0:r, :], norm[0:r, :], NORM_EPS, None, ALU.max))
                    link(nc.vector.reciprocal(norm[0:r, :], norm[0:r, :]))
                    link(nc.vector.tensor_tensor(norm[0:r, :], norm[0:r, :], temp_all[0:r, :], ALU.mult))
                    link(nc.vector.tensor_tensor(qq[0:r, :, 0:HD], q_raw[0:r, :, :], norm[0:r, :].unsqueeze(2).to_broadcast([r, H, HD]), ALU.mult))
                    link(nc.vector.tensor_copy(qq[0:r, :, HD:HD + HQ], qq[0:r, :, 0:HQ]))
                    if known(t, 2):
                        dve.wait_ge(s["batch_turned"], (t - 1) * NB)
                    products(nc, qq, feat[p], r)
                    nc.vector.tensor_copy(feat[p][0:r, :, NF:NF + HD], qq[0:r, :, 0:HD])
                    nc.vector.tensor_tensor(feat[p][0:r, :, NF + HD:NF + HD + HQ], qq[0:r, :, 0:HQ], qq[0:r, :, HQ:HD], ALU.mult).then_inc(s["feat_ready"], 1)
                    dve.wait_ge(s["feat_ready"], t + 1)
                    link.end()

                def route(t, p, r):
                    link = Chain(dve, s["route_step"], t, 4)
                    dve.wait_ge(s["gate_done"], t + 1)
                    link(nc.vector.tensor_tensor(logits[0:r, :], ps_gate[0:r, 0:NE], gate_b_all[0:r, :], ALU.add))
                    carry_wait(dve, c["carrier_dve"])
                    link(nc.vector.max(top_v[0:r, :], logits[0:r, :]))
                    carry_wait(dve, c["carrier_dve"])
                    link(nc.vector.max_index(top_i[0:r, :], top_v[0:r, :], logits[0:r, :]))
                    link(nc.vector.tensor_copy(top_f[0:r, :], top_i[0:r, 0:2]))
                    nc.vector.tensor_copy(c["gate_v"][0:r, bass.ds(t, 1), :], top_v[0:r, 0:2].unsqueeze(1))
                    for k in range(2):
                        last = nc.vector.tensor_scalar(c["chosen"][0:r, k, bass.ds(t, 1), :], c["iota"][0:r, 0:NE].unsqueeze(1), top_f[0:r, k:k + 1], None, ALU.is_equal)
                    last.then_inc(s["routed"], 1)
                    dve.wait_ge(s["routed"], t + 1)
                    link.end()

                def mean(t, i, p, r):
                    link = Chain(dve, s["agg_step"], t, 3)
                    counts = c["acc"][:, FB, bass.ds(t * P, r)]
                    link(nc.vector.tensor_scalar(cnt[:, 0:r], counts, 1.0, None, ALU.max))
                    link(nc.vector.reciprocal(cnt[:, 0:r], cnt[:, 0:r]))
                    dve.wait_ge(s["agg_done"], t + 1)
                    link(nc.vector.scalar_tensor_tensor(aggT[p][:, 0:r], counts, b2[:, 0:1], ps_agg[:, 0:r], ALU.mult, ALU.add))
                    nc.vector.tensor_tensor(aggT[p][:, 0:r], aggT[p][:, 0:r], cnt[:, 0:r], ALU.mult).then_inc(s["agg_ready"], 1)
                    link.end()

                queries(0, 0, 0, P)
                mean(0, 0, 0, P)

                def body(t, i, p, r, nr):
                    if nr:
                        queries(t + 1, i + p, 1 - p, nr)
                    link = Chain(dve, s["o_step"], t, 1)
                    dve.wait_ge(s["y_done"], t + 1)
                    heads = ps_y[0:r, 0:H * VW].rearrange("n (h e) -> n h e", h=H)
                    link(nc.vector.reciprocal(y_inv[0:r, :].unsqueeze(2), heads[:, :, 0:1]))
                    if known(t, 1):
                        dve.wait_ge(s["o_turned"], t)
                    nc.vector.tensor_tensor(o[0:r, :].rearrange("n (h e) -> n h e", h=H), heads[:, :, 1:VW],
                                            y_inv[0:r, :].unsqueeze(2).to_broadcast([r, H, HD]), ALU.mult).then_inc(s["o_ready"], 1)
                    link.end()
                    if known(t, 1):
                        route(t - 1, 1 - p, P)
                    if nr:
                        mean(t + 1, None, 1 - p, nr)
                    link = Chain(dve, s["final_step"], t, 11)
                    dve.wait_ge(s["mlp2_done"], t + 1)
                    link(nc.vector.tensor_tensor(y[0:r, :], ps_o[0:r, 0:D], xn[p][0:r, :], ALU.add))
                    link(nc.vector.tensor_tensor(y[0:r, :], y[0:r, :], b4_all[0:r, :], ALU.add))
                    link(nc.vector.bn_stats(stats[0:r, :], y[0:r, :]))
                    carry_wait(dve, c["carrier_dve"])
                    nc.vector.bn_aggr(mv[0:r, :], stats[0:r, :]).then_inc(s["var1_ready"], 1)
                    dve.wait_ge(s["std1_ready"], t + 1)
                    link(nc.vector.reciprocal(rstd[0:r, :], rstd[0:r, :]))
                    link(nc.vector.tensor_scalar(y[0:r, :], y[0:r, :], mv[0:r, 0:1], rstd[0:r, :], ALU.subtract, ALU.mult))
                    link(nc.vector.tensor_tensor(y[0:r, :], y[0:r, :], gamma_all[0:r, :], ALU.mult))
                    link(nc.vector.tensor_tensor(y[0:r, :], y[0:r, :], shift_all[0:r, :], ALU.add))
                    link(nc.vector.tensor_tensor(y[0:r, :], y[0:r, :], x_in[p][0:r, :], ALU.add))
                    dve.wait_ge(s["proj_done"], t + 1)
                    if known(t, 2):
                        dve.wait_ge(stored[p], 32 * i)
                    link(nc.vector.tensor_tensor(xr[p][0:r, :], ps_q[0:r, D:2 * D], y[0:r, :], ALU.add))
                    link(nc.vector.bn_stats(stats[0:r, :], xr[p][0:r, :]))
                    carry_wait(dve, c["carrier_dve"])
                    nc.vector.bn_aggr(mv[0:r, :], stats[0:r, :]).then_inc(s["var2_ready"], 1)
                    dve.wait_ge(s["std2_ready"], t + 1)
                    link(nc.vector.reciprocal(rstd[0:r, :], rstd[0:r, :]))
                    nc.vector.tensor_scalar(z[p][0:r, :], xr[p][0:r, :], mv[0:r, 0:1], rstd[0:r, :], ALU.subtract, ALU.mult).then_inc(s["z_ready"], 1)
                    dve.wait_ge(s["z_ready"], t + 1)
                    link.end()

                each_tile(dve, body)
                route(NT - 1, 0, LAST)


def route_phase(nc, m, c, a, d, w):
    with Memory(nc, "r_") as l:
        both = l.sb("both", [P, NT, NE])
        rank = l.sb("rank", [P, NT, NE])
        total = l.sb("total", [P, NT, NE])
        run = l.sb("run", [P, NE])
        tiles_i = l.sb("tiles_i", [P, NE], I32)
        tiles = l.sb("tiles", [P, NE])
        ends = l.sb("ends", [P, NE])
        begins = l.sb("begins", [P, NE])
        prod = l.sb("prod", [P, NT, NE])
        slot_f = l.sb("slot_f", [P, 2, NT])
        over = l.sb("over", [1, MT, NE])
        tile_no = l.sb("tile_no", [1, MT])
        owner = l.sb("owner", [1, MT])
        gap = l.sb("gap", [P, NT])
        z_all = l.sb("z_all", [P, NT, D])
        ps_rank = l.ps("ps_rank", [P, 512])
        ps_total = l.ps("ps_total", [P, 512])
        step = l.sem("step")
        both_ready = l.sem("both_ready")
        ranked = l.sem("ranked")
        gap_ready = l.sem("gap_ready")
        exp_ready = l.sem("exp_ready")
        slots_ready = l.sem("slots_ready")
        z_in = l.sem("z_in")
        placed = [l.sem(f"placed{j}") for j in range(4)]
        iota_made = l.sem("iota_made")
        assert NT * NE <= 512

        with nc.Block() as block:
            @block.sync
            def _(sp):
                sp.dma_start(z_all[:, 0:NT - 1, :], d["z"][0:(NT - 1) * P, :].rearrange("(t n) e -> n t e", n=P)).then_inc(z_in, 16)
                sp.dma_start(z_all[0:LAST, NT - 1, :], d["z"][(NT - 1) * P:N, :]).then_inc(z_in, 16)
                for e in range(NE):
                    sp.dma_start(w["w1"][:, e, :, :], a["ew1"][e * D:(e + 1) * D, :].rearrange("(k f) n -> f k n", f=P)).then_inc(w["in"][e // SET], 16)
                    sp.dma_start(w["w2"][:, e, :, :], a["ew2"][e * FE:(e + 1) * FE, :].rearrange("(k f) n -> f k n", f=P)).then_inc(w["in"][e // SET], 16)
                    sp.dma_start(w["b1"][:, e, :], a["eb1"][:, e * (FE // P):(e + 1) * (FE // P)]).then_inc(w["in"][e // SET], 16)
                sp.wait_ge(z_in, 32)

            @block.tensor
            def _(pe):
                pe.wait_ge(both_ready, 1)
                flat = both[:, :, :].rearrange("n t e -> n (t e)")
                nc.tensor.matmul(ps_rank[:, 0:NT * NE], c["before"][:, :], flat, start=True, stop=True).then_inc(ranked, 1)
                nc.tensor.matmul(ps_total[:, 0:NT * NE], c["ones"][:, :], flat, start=True, stop=True).then_inc(ranked, 1)

            @block.scalar
            def _(act):
                act.wait_ge(gap_ready, 1)
                nc.scalar.activation(gap[:, :], gap[:, :], ACT.Exp).then_inc(exp_ready, 1)

            @block.vector
            def _(dve):
                n = [0]

                def link(ins):
                    n[0] += 1
                    ins.then_inc(step, 1)
                    dve.wait_ge(step, n[0])

                nc.vector.tensor_tensor(both[:, :, :], c["chosen"][:, 0, :, :], c["chosen"][:, 1, :, :], ALU.add).then_inc(both_ready, 1)
                nc.vector.tensor_tensor(gap[:, :].unsqueeze(2), c["gate_v"][:, :, 1:2], c["gate_v"][:, :, 0:1], ALU.subtract).then_inc(gap_ready, 1)
                dve.wait_ge(exp_ready, 1)
                link(nc.vector.tensor_scalar(c["mix_w"][:, 0, :], gap[:, :], 1.0, None, ALU.add))
                link(nc.vector.reciprocal(c["mix_w"][:, 0, :], c["mix_w"][:, 0, :]))
                link(nc.vector.tensor_tensor(c["mix_w"][:, 1, :], gap[:, :], c["mix_w"][:, 0, :], ALU.mult))
                dve.wait_ge(ranked, 2)
                link(nc.vector.tensor_copy(rank[:, :, :].rearrange("n t e -> n (t e)"), ps_rank[:, 0:NT * NE]))
                link(nc.vector.tensor_copy(total[:, :, :].rearrange("n t e -> n (t e)"), ps_total[:, 0:NT * NE]))
                link(nc.vector.tensor_copy(run[:, :], total[:, 0, :]))
                for t in range(1, NT):
                    link(nc.vector.tensor_tensor(rank[:, t, :], rank[:, t, :], run[:, :], ALU.add))
                    link(nc.vector.tensor_tensor(run[:, :], run[:, :], total[:, t, :], ALU.add))
                link(nc.vector.tensor_scalar(run[:, :], run[:, :], float(P - 1), None, ALU.add))
                link(nc.vector.tensor_copy(tiles_i[:, :], run[:, :]))
                link(nc.vector.tensor_scalar(tiles_i[:, :], tiles_i[:, :], P.bit_length() - 1, None, ALU.arith_shift_right))
                link(nc.vector.tensor_copy(tiles[:, :], tiles_i[:, :]))
                link(nc.vector.tensor_copy(ends[:, 0:1], tiles[:, 0:1]))
                for e in range(1, NE):
                    link(nc.vector.tensor_tensor(ends[:, e:e + 1], ends[:, e - 1:e], tiles[:, e:e + 1], ALU.add))
                link(nc.vector.tensor_tensor(begins[:, :], ends[:, :], tiles[:, :], ALU.subtract))
                link(nc.vector.tensor_scalar(begins[:, :], begins[:, :], float(P), None, ALU.mult))
                link(nc.vector.tensor_tensor(rank[:, :, :], rank[:, :, :], begins[:, :].unsqueeze(1).to_broadcast([P, NT, NE]), ALU.add))
                for k in range(2):
                    link(nc.vector.tensor_tensor(prod[:, :, :], rank[:, :, :], c["chosen"][:, k, :, :], ALU.mult))
                    link(nc.vector.tensor_reduce(slot_f[:, k, :], prod[:, :, :], X, ALU.add))
                nc.vector.tensor_copy(c["slots"][:, :, :], slot_f[:, :, :]).then_inc(slots_ready, 1)
                dve.wait_ge(iota_made, 1)
                link(nc.vector.tensor_tensor(over[:, :, :], ends[0:1, :].unsqueeze(1).to_broadcast([1, MT, NE]),
                                             tile_no[:, :].unsqueeze(2).to_broadcast([1, MT, NE]), ALU.is_le))
                link(nc.vector.tensor_reduce(owner[:, :], over[:, :, :], X, ALU.add))
                link(nc.vector.tensor_scalar(c["owner"][:, :], owner[:, :], float(NE - 1), None, ALU.min))
                for k in range(2):
                    link(nc.vector.tensor_tensor(prod[:, :, :], c["chosen"][:, k, :, :], c["mix_w"][:, k, :].unsqueeze(2).to_broadcast([P, NT, NE]), ALU.mult))
                    if k == 0:
                        link(nc.vector.tensor_copy(c["share"][:, :, :], prod[:, :, :]))
                    else:
                        link(nc.vector.tensor_tensor(c["share"][:, :, :], c["share"][:, :, :], prod[:, :, :], ALU.add))

            @block.gpsimd
            def _(pool):
                nc.gpsimd.iota(tile_no[:, :], pattern=[[1, MT]], base=0, channel_multiplier=0,
                               allow_small_or_imprecise_dtypes=True).then_inc(iota_made, 1)
                pool.wait_ge(slots_ready, 1)
                pool.wait_ge(z_in, 32)
                for t in range(NT):
                    r = P if t < NT - 1 else LAST
                    for k in range(2):
                        j = (2 * t + k) % 4
                        nc.gpsimd.indirect_dma_start(
                            out=d["rows"][:, :], out_offset=bass.IndirectOffsetOnAxis(ap=c["slots"][0:r, k, t:t + 1].bitcast(U32), axis=0),
                            in_=z_all[0:r, t, :], in_offset=None).then_inc(placed[j], 16)
                for j in range(4):
                    pool.wait_ge(placed[j], 16 * ((2 * NT - j + 3) // 4))


def expert_phase(nc, m, c, a, d, w):
    with Memory(nc, "m_") as l:
        w1_tile = [l.sb(f"w1_tile{p}", [P, 2, FE]) for p in range(2)] * 2
        z = [l.sb(f"z{p}", [P, D]) for p in range(DEEP)]
        zT = [l.sb(f"zT{p}", [P, 2, P]) for p in range(DEEP)]
        hT = [l.sb(f"hT{p}", [P, FE // P, P]) for p in range(DEEP)]
        y = [l.sb(f"y{p}", [P, D]) for p in range(DEEP)]
        ps_t = [l.ps(f"ps_t{p}", [P, 2, P]) for p in range(2)] * 2
        ps_h = [l.ps(f"ps_h{p}", [P, FE // P, P]) for p in range(2)] * 2
        ps_y = [l.ps(f"ps_y{p}", [P, D]) for p in range(2)] * 2
        w1, w2, b1, w_in = w["w1"], w["w2"], w["b1"], w["in"]
        z_in = [l.sem(f"z_in{p}") for p in range(DEEP)]
        y_out = [l.sem(f"y_out{p}") for p in range(DEEP)]
        weights_ready = l.sem("weights_ready")
        turned = l.sem("turned")
        zT_ready = l.sem("zT_ready")
        w1_placed = l.sem("w1_placed")
        up_done = l.sem("up_done")
        hT_ready = l.sem("hT_ready")
        down_done = l.sem("down_done")
        y_ready = l.sem("y_ready")

        def each(eng, body):
            for p in range(DEEP):
                body(p, 0, p)
            with eng.Fori(1, MT // DEEP - 1) as i:
                for p in range(DEEP):
                    body(DEEP * i + p, i, p)
            for p in range(DEEP):
                body(MT - DEEP + p, MT // DEEP - 1, p)

        with nc.Block() as block:
            @block.sync
            def _(sp):
                for j in range(NE // SET):
                    sp.wait_ge(w_in[j], 48 * SET)
                    sp.sem_inc(weights_ready, SET)

            @block.tensor
            def _(pe):
                def turn(t, i, p):
                    pe.wait_ge(z_in[p], 16 * (i + 1))
                    if known(t, 2):
                        pe.wait_ge(zT_ready, t - 1)
                    for k in range(2):
                        last = nc.tensor.transpose(ps_t[p][:, k, :], z[p][:, k * P:(k + 1) * P], c["ident"][:, :])
                    last.then_inc(turned, 1)

                def up(t, i, p):
                    pe.wait_ge(zT_ready, t + 1)
                    pe.wait_ge(w1_placed, t + 1)
                    if known(t, 2):
                        pe.wait_ge(hT_ready, t - 1)
                    for f in range(FE // P):
                        for k in range(2):
                            last = nc.tensor.matmul(ps_h[p][:, f, :], w1_tile[p][:, k, f * P:(f + 1) * P], zT[p][:, k, :], start=(k == 0), stop=(k == 1))
                    last.then_inc(up_done, 1)

                def down(t, p):
                    e = pe.value_load(c["owner"][0:1, bass.ds(t, 1)], min_val=0, max_val=NE - 1)
                    pe.wait_ge(hT_ready, t + 1)
                    if known(t, 2):
                        pe.wait_ge(y_ready, t - 1)
                    for f in range(FE // P):
                        last = nc.tensor.matmul(ps_y[p][:, :], hT[p][:, f, :], w2[:, bass.ds(e, 1), f, :].rearrange("f a n -> f (a n)"), start=(f == 0), stop=(f == FE // P - 1))
                    last.then_inc(down_done, 1)

                turn(0, 0, 0)

                def body(t, i, p):
                    up(t, i, p)
                    if known_before(t, MT - 1):
                        turn(t + 1, i + (p + 1) // DEEP, (p + 1) % DEEP)
                    if known(t, 1):
                        down(t - 1, (p - 1) % DEEP)

                each(pe, body)
                down(MT - 1, DEEP - 1)

            @block.scalar
            def _(act):
                for p in range(DEEP):
                    act.dma_start(z[p][:, :], d["rows"][p * P:(p + 1) * P, :]).then_inc(z_in[p], 16)

                def body(t, i, p):
                    e = act.value_load(c["owner"][0:1, bass.ds(t, 1)], min_val=0, max_val=NE - 1)
                    act.wait_ge(up_done, t + 1)
                    if known(t, 2):
                        act.wait_ge(down_done, t - 1)
                    for f in range(FE // P):
                        last = nc.scalar.activation(hT[p][:, f, :], ps_h[p][:, f, :], ACT.Relu, bias=b1[:, bass.ds(e, 1), f])
                    last.then_inc(hT_ready, 1)
                    if not isinstance(i, int) or i + 1 < MT // DEEP:
                        act.dma_start(z[p][:, :], d["rows"][bass.ds((t + DEEP) * P, P), :]).then_inc(z_in[p], 16)

                each(act, body)

            @block.vector
            def _(dve):
                def take(t, p, i):
                    dve.wait_ge(down_done, t + 1)
                    if known(t, DEEP):
                        dve.wait_ge(y_out[p], 16 * i)
                    nc.vector.tensor_copy(y[p][:, :], ps_y[p][:, :]).then_inc(y_ready, 1)

                def place(t, p):
                    e = dve.value_load(c["owner"][0:1, bass.ds(t, 1)], min_val=0, max_val=NE - 1)
                    dve.wait_ge(weights_ready, e + 1)
                    if known(t, 2):
                        dve.wait_ge(up_done, t - 1)
                    nc.vector.tensor_copy(w1_tile[p][:, :, :].unsqueeze(1), w1[:, bass.ds(e, 1), :, :]).then_inc(w1_placed, 1)

                def copy_zT(t, p):
                    dve.wait_ge(turned, t + 1)
                    if known(t, DEEP):
                        dve.wait_ge(up_done, t - DEEP + 1)
                    nc.vector.tensor_copy(zT[p][:, :, :], ps_t[p][:, :, :]).then_inc(zT_ready, 1)

                place(0, 0)
                copy_zT(0, 0)

                def body(t, i, p):
                    if known_before(t, MT - 1):
                        place(t + 1, (p + 1) % DEEP)
                        copy_zT(t + 1, (p + 1) % DEEP)
                    if known(t, 1):
                        take(t - 1, (p - 1) % DEEP, i if p else i - 1)

                each(dve, body)
                take(MT - 1, DEEP - 1, MT // DEEP - 1)

            @block.gpsimd
            def _(pool):
                def body(t, i, p):
                    pool.wait_ge(y_ready, t + 1)
                    pool.dma_start(d["outs"][bass.ds(t * P, P), :], y[p][:, :]).then_inc(y_out[p], 16)

                each(pool, body)
                for p in range(DEEP):
                    pool.wait_ge(y_out[p], 16 * (MT // DEEP))


def combine_phase(nc, m, c, a, d, out):
    with Memory(nc, "c_") as l:
        eb2 = l.sb("eb2", [NE, D])
        gamma_all = l.sb("gamma_all", [P, D])
        beta_all = l.sb("beta_all", [P, D])
        xr = [l.sb(f"xr{p}", [P, D]) for p in range(2)]
        z = [l.sb(f"z{p}", [P, D]) for p in range(2)]
        y1 = [l.sb(f"y1{p}", [P, D]) for p in range(2)]
        y2 = [l.sb(f"y2{p}", [P, D]) for p in range(2)]
        idx = [l.sb(f"idx{p}", [P, 2], I32) for p in range(2)]
        mix = [l.sb(f"mix{p}", [P, 2]) for p in range(2)]
        share = [l.sb(f"share{p}", [P, NE]) for p in range(2)]
        shareT = [l.sb(f"shareT{p}", [NE, P]) for p in range(2)]
        y = l.sb("y", [P, D])
        res = [l.sb(f"res{p}", [P, D]) for p in range(2)]
        stats = l.sb("stats", [P, 6])
        mv = l.sb("mv", [P, 2])
        rstd = l.sb("rstd", [P, 1])
        ps_t = [l.ps(f"ps_t{p}", [NE, P]) for p in range(2)]
        ps_b = [l.ps(f"ps_b{p}", [P, D]) for p in range(2)]
        weights_in = l.sem("weights_in")
        loaded = [l.sem(f"loaded{p}") for p in range(2)]
        got1 = [l.sem(f"got1{p}") for p in range(2)]
        got2 = [l.sem(f"got2{p}") for p in range(2)]
        stored = [l.sem(f"stored{p}") for p in range(2)]
        picked = l.sem("picked")
        turned = l.sem("turned")
        shareT_ready = l.sem("shareT_ready")
        bias_done = l.sem("bias_done")
        step = l.sem("step")
        var_ready = l.sem("var_ready")
        std_ready = l.sem("std_ready")
        res_ready = l.sem("res_ready")

        with nc.Block() as block:
            @block.sync
            def _(sp):
                def load(t, p, r):
                    sp.dma_start(xr[p][0:r, :], d["xr"][bass.ds(t * P, r), :]).then_inc(loaded[p], 16)
                    sp.dma_start(z[p][0:r, :], d["z"][bass.ds(t * P, r), :]).then_inc(loaded[p], 16)

                sp.dma_start(eb2[:, :], a["eb2"]).then_inc(weights_in, 16)
                sp.dma_start(gamma_all[:, :], rows(a["ffn_gamma"], P, D)).then_inc(weights_in, 16)
                sp.dma_start(beta_all[:, :], rows(a["ffn_beta"], P, D)).then_inc(weights_in, 16)
                load(0, 0, P)
                load(1, 1, P)

                def body(t, i, p, r, nr):
                    sp.wait_ge(res_ready, t + 1)
                    sp.dma_start(out[bass.ds(t * P, r), :], res[p][0:r, :]).then_inc(stored[p], 16)
                    if not isinstance(t, int) or t + 2 < NT:
                        load(t + 2, p, LAST if isinstance(t, int) and t == NT - 3 else P)

                each_tile(sp, body)
                for p in range(2):
                    sp.wait_ge(stored[p], 16 * ((NT + 1 - p) // 2))

            @block.gpsimd
            def _(pool):
                def body(t, i, p, r, nr):
                    if known(t, 2):
                        pool.wait_ge(res_ready, t - 1)
                        pool.wait_ge(turned, t - 1)
                        pool.wait_ge(got1[p], 16 * i)
                        pool.wait_ge(got2[p], 16 * i)
                    nc.gpsimd.tensor_copy(idx[p][0:r, :].unsqueeze(2), c["slots"][0:r, :, bass.ds(t, 1)])
                    nc.gpsimd.tensor_copy(mix[p][0:r, :].unsqueeze(2), c["mix_w"][0:r, :, bass.ds(t, 1)])
                    nc.gpsimd.tensor_copy(share[p][0:r, :].unsqueeze(1), c["share"][0:r, bass.ds(t, 1), :]).then_inc(picked, 1)
                    pool.wait_ge(picked, t + 1)
                    carry_wait(pool, c["carrier_pool"])
                    for k, (to, got) in enumerate(((y1[p], got1[p]), (y2[p], got2[p]))):
                        nc.gpsimd.indirect_dma_start(
                            out=to[0:r, :], out_offset=None, in_=d["outs"][:, :],
                            in_offset=bass.IndirectOffsetOnAxis(ap=idx[p][0:r, k:k + 1].bitcast(U32), axis=0)).then_inc(got, 16)

                each_tile(pool, body)

            @block.tensor
            def _(pe):
                def body(t, i, p, r, nr):
                    pe.wait_ge(picked, t + 1)
                    if known(t, 2):
                        pe.wait_ge(shareT_ready, t - 1)
                        pe.wait_ge(res_ready, t - 1)
                    nc.tensor.transpose(ps_t[p][:, 0:r], share[p][0:r, :], c["ident"][0:r, 0:r]).then_inc(turned, 1)
                    if isinstance(t, int) and t == 0:
                        pe.wait_ge(weights_in, 48)
                    pe.wait_ge(shareT_ready, t + 1)
                    nc.tensor.matmul(ps_b[p][0:r, :], shareT[p][:, 0:r], eb2[:, :], start=True, stop=True).then_inc(bias_done, 1)

                each_tile(pe, body)

            @block.scalar
            def _(act):
                def copy_share(t, i, p, r):
                    act.wait_ge(turned, t + 1)
                    if known(t, 2):
                        act.wait_ge(bias_done, t - 1)
                    nc.scalar.activation(shareT[p][:, 0:r], ps_t[p][:, 0:r], ACT.Copy).then_inc(shareT_ready, 1)

                def body(t, i, p, r, nr):
                    copy_share(t, i, p, r)
                    act.wait_ge(var_ready, t + 1)
                    nc.scalar.activation(rstd[0:r, :], mv[0:r, 1:2], ACT.Sqrt, bias=c["eps"][0:r, :]).then_inc(std_ready, 1)

                each_tile(act, body)

            @block.vector
            def _(dve):
                def body(t, i, p, r, nr):
                    if isinstance(t, int) and t == 0:
                        dve.wait_ge(weights_in, 48)
                    link = Chain(dve, step, t, 8)
                    dve.wait_ge(loaded[p], 32 * (i + 1))
                    dve.wait_ge(bias_done, t + 1)
                    link(nc.vector.tensor_tensor(y[0:r, :], ps_b[p][0:r, :], z[p][0:r, :], ALU.add))
                    for k, (frm, got) in enumerate(((y1[p], got1[p]), (y2[p], got2[p]))):
                        dve.wait_ge(got, 16 * (i + 1))
                        link(nc.vector.scalar_tensor_tensor(y[0:r, :], frm[0:r, :], mix[p][0:r, k:k + 1], y[0:r, :], ALU.mult, ALU.add))
                    link(nc.vector.bn_stats(stats[0:r, :], y[0:r, :]))
                    carry_wait(dve, c["carrier_dve"])
                    nc.vector.bn_aggr(mv[0:r, :], stats[0:r, :]).then_inc(var_ready, 1)
                    dve.wait_ge(std_ready, t + 1)
                    link(nc.vector.reciprocal(rstd[0:r, :], rstd[0:r, :]))
                    link(nc.vector.tensor_scalar(y[0:r, :], y[0:r, :], mv[0:r, 0:1], rstd[0:r, :], ALU.subtract, ALU.mult))
                    link(nc.vector.tensor_tensor(y[0:r, :], y[0:r, :], gamma_all[0:r, :], ALU.mult))
                    if known(t, 2):
                        dve.wait_ge(stored[p], 16 * i)
                    link(nc.vector.tensor_tensor(y[0:r, :], y[0:r, :], beta_all[0:r, :], ALU.add))
                    nc.vector.tensor_tensor(res[p][0:r, :], y[0:r, :], xr[p][0:r, :], ALU.add).then_inc(res_ready, 1)
                    dve.wait_ge(res_ready, t + 1)
                    link.end()

                each_tile(dve, body)


def gps_layer_kernel(nc, a, out):
    with Memory(nc, "k_") as m:
        c = {
            "ident": m.sb("ident", [P, P]),
            "ones": m.sb("ones", [P, P]),
            "before": m.sb("before", [P, P]),
            "zeros": m.sb("zeros", [P, 512]),
            "iota": m.sb("iota", [P, W]),
            "eps": m.sb("eps", [P, 1]),
            "src": m.sb("src", [P, ET + 1], I32),
            "dst_rel": m.sb("dst_rel", [P, ET + 1]),
            "base": m.sb("base", [P, NG + 1]),
            "base_i": m.sb("base_i", [1, NG + 1], I32),
            "passes": m.sb("passes", [1, 1], I32),
            "sums": m.sb("sums", [P, FB + 1, H + 2, VW]),
            "chosen": m.sb("chosen", [P, 2, NT, NE]),
            "gate_v": m.sb("gate_v", [P, NT, 2]),
            "mix_w": m.sb("mix_w", [P, 2, NT]),
            "slots": m.sb("slots", [P, 2, NT], I32),
            "share": m.sb("share", [P, NT, NE]),
            "owner": m.sb("owner", [1, MT], I32),
            "base_moved": m.sem("base_moved"),
            "carrier_dve": m.sem("carrier_dve"),
            "carrier_pool": m.sem("carrier_pool"),
            "carrier_pe": m.sem("carrier_pe"),
        }
        d = {
            "xn": nc.dram_tensor("xn_kept", [N, D], F32, kind="Internal").ap(),
            "xT": nc.dram_tensor("xT_kept", [NT * P, 2 * P], F32, kind="Internal").ap(),
            "proj": nc.dram_tensor("proj_kept", [N, HID], F32, kind="Internal").ap(),
            "xr": nc.dram_tensor("xr_kept", [N, D], F32, kind="Internal").ap(),
            "z": nc.dram_tensor("z_kept", [N, D], F32, kind="Internal").ap(),
            "rows": nc.dram_tensor("rows_kept", [MT * P, D], F32, kind="Internal").ap(),
            "outs": nc.dram_tensor("outs_kept", [MT * P, D], F32, kind="Internal").ap(),
        }
        setup_phase(nc, m, c, a)
        with Memory(nc, "n_") as n:
            c["acc"] = n.sb("acc", [P, FB + 1, N + W])
            node_phase(nc, m, c, a, d)
            edge_phase(nc, m, c, a, d)
            update_phase(nc, m, c, a, d)
        with Memory(nc, "w_") as k:
            w = {
                "w1": k.sb("w1", [P, NE, 2, FE]),
                "w2": k.sb("w2", [P, NE, FE // P, D]),
                "b1": k.sb("b1", [P, NE, FE // P]),
                "in": [k.sem(f"in{j}") for j in range(NE // SET)],
            }
            route_phase(nc, m, c, a, d, w)
            expert_phase(nc, m, c, a, d, w)
        combine_phase(nc, m, c, a, d, out)


def _layout(inputs):
    import numpy as np

    def arr(k):
        return np.asarray(inputs[k])

    src, dst = arr("src"), arr("dst")
    whole = ET * P
    return {
        "x": arr("x"),
        "dst": dst,
        "dst_cols": dst[:whole].reshape(ET, P).T,
        "dst_tail": dst[whole:].reshape(EL, 1),
        "src_cols": src[:whole].reshape(ET, P).T,
        "src_tail": src[whole:].reshape(EL, 1),
        "attrT": arr("edge_attr_128").T,
        "u": arr("L0_gnn_u"),
        "W1": arr("L0_gnn_W1"), "b1": arr("L0_gnn_b1"), "W2": arr("L0_gnn_W2"), "b2": arr("L0_gnn_b2"),
        "W3": arr("L0_gnn_W3"), "b3": arr("L0_gnn_b3"), "W4": arr("L0_gnn_W4"), "b4": arr("L0_gnn_b4"),
        "gnn_gamma": arr("L0_gnn_gamma"), "gnn_beta": arr("L0_gnn_beta"),
        "wqkvT": arr("L0_mix_Wqkv").T, "bqkv": arr("L0_mix_bqkv"),
        "wprojT": arr("L0_mix_Wproj").T, "bproj": arr("L0_mix_bproj"),
        "temperature": arr("L0_mix_temperature").reshape(H),
        "gate_w": arr("L0_ffn_gate_w"), "gate_b": arr("L0_ffn_gate_b"),
        "ew1": arr("L0_ffn_w1").reshape(NE * D, FE),
        "eb1": arr("L0_ffn_b1").reshape(NE * (FE // P), P).T,
        "ew2": arr("L0_ffn_w2").reshape(NE * FE, D),
        "eb2": arr("L0_ffn_b2"),
        "ffn_gamma": arr("L0_ffn_gamma"), "ffn_beta": arr("L0_ffn_beta"),
    }


def kernel(**inputs):
    import numpy as np
    import concourse.bacc as bacc
    from concourse.bass_utils import run_bass_kernel_spmd

    nc = bacc.Bacc("TRN2", target_bir_lowering=False, num_devices=1)
    arrays, aps = {}, {}
    for name, value in _layout(inputs).items():
        value = np.ascontiguousarray(value)
        arrays[f"in_{name}"] = value
        aps[name] = nc.dram_tensor(f"in_{name}", value.shape, mybir.dt.from_np(value.dtype), kind="ExternalInput").ap()
    out = nc.dram_tensor("out_0", (N, D), F32, kind="ExternalOutput").ap()
    gps_layer_kernel(nc, aps, out)
    r = run_bass_kernel_spmd(nc, [arrays], core_ids=[0])
    return r.results[0]["out_0"]
```

```python
import concourse.bass as bass
from concourse import mybir
from contextlib import ExitStack

F32 = mybir.dt.float32
F32R = mybir.dt.float32r
BF16 = mybir.dt.bfloat16
I32 = mybir.dt.int32
U32 = mybir.dt.uint32
ALU = mybir.AluOpType
ACT = mybir.ActivationFunctionType
X = mybir.AxisListType.X

P = 128
N = 3125
D = 256
ED = 128
HID = 512
E = 53125
NT = (N + P - 1) // P
LAST = N - (NT - 1) * P
ET = E // P
EL = E - ET * P
G = 5
NG = ET // G
assert NG * G == ET and NG % 2 == 1 and NT % 2 == 1
W = 64
LAG = 4
H = 8
HD = D // H
HQ = HD // 2
NF = 16 * HD
FT = HD + HQ + 1
TW = 64
assert FT <= TW and 2 * TW == P
FB = NF // P
VW = HD + 1
FH = 4 * D
NE = 16
FE = 512
MT = (2 * N + NE * (P - 1)) // P
DEEP = 4
SET = 2
CAP = N + P
assert MT % DEEP == 0 and NE % SET == 0
SCALE = float(HD) ** 0.25
VN = 96
PW = VN // 2
ZN = VN - VW
LN_EPS = 1e-5
NORM_EPS = 1e-12


def rows(ap, n, width, start=0):
    return bass.AP(tensor=ap.tensor, offset=ap.offset + start, ap=[[0, n], [1, width]])


class Chain:

    def __init__(self, eng, sem, turn, per):
        self.eng, self.sem, self.start, self.per, self.n = eng, sem, turn * per, per, 0

    def __call__(self, ins):
        self.n += 1
        assert self.n <= self.per
        ins.then_inc(self.sem, 1)
        self.eng.wait_ge(self.sem, self.start + self.n)

    def end(self):
        assert self.n == self.per, (self.n, self.per)


def each_tile(eng, body):
    body(0, 0, 0, P, P)
    body(1, 0, 1, P, P)
    half = NT // 2
    with eng.Fori(1, half - 1) as i:
        body(2 * i, i, 0, P, P)
        body(2 * i + 1, i, 1, P, P)
    body(NT - 3, half - 1, 0, P, P)
    body(NT - 2, half - 1, 1, P, LAST)
    body(NT - 1, half, 0, LAST, 0)


def known(t, least):
    return not isinstance(t, int) or t >= least


def known_before(t, end):
    return not isinstance(t, int) or t < end


def tile_rows(t):
    return LAST if isinstance(t, int) and t == NT - 1 else P


def carry_wait(eng, carrier):
    eng.sem_inc(carrier, 1)


class Memory:

    def __init__(self, nc, tag):
        self.nc, self.tag, self.ctx, self.sems = nc, tag, ExitStack(), []

    def __enter__(self):
        self.ctx.__enter__()
        return self

    def __exit__(self, *a):
        return self.ctx.__exit__(*a)

    def sb(self, name, shape, dt=F32):
        return self.ctx.enter_context(self.nc.sbuf_tensor(self.tag + name, shape, dt))

    def ps(self, name, shape):
        return self.ctx.enter_context(self.nc.psum_tensor(self.tag + name, shape, F32))

    def sem(self, name):
        self.sems.append(self.ctx.enter_context(self.nc.semaphore(self.tag + name)))
        return self.sems[-1]

    def clear_sems(self):
        with self.nc.Block() as block:
            @block.sync
            def _(sp):
                for sem in self.sems:
                    sp.sem_clear(sem)


def setup_phase(nc, m, c, a):
    with Memory(nc, "s_") as l:
        groups_i = l.sb("groups_i", [NG + 1, G * P], I32)
        lohi = l.sb("lohi", [NG + 1, 2])
        lo_rows = l.sb("lo_rows", [NG + 1, P])
        hi_rows = l.sb("hi_rows", [NG + 1, P])
        dst_i = l.sb("dst_i", [P, ET + 1], I32)
        span = l.sb("span", [P, NG + 1])
        widest = l.sb("widest", [1, 1])
        windows_i = l.sb("windows_i", [1, 1], I32)
        ps_lo = l.ps("ps_lo", [P, 512])
        ps_hi = l.ps("ps_hi", [P, 512])
        dst_in = l.sem("dst_in")
        src_in = l.sem("src_in")
        filled = l.sem("filled")
        ident_made = l.sem("ident_made")
        masks_made = l.sem("masks_made")
        step = l.sem("step")
        lohi_made = l.sem("lohi_made")
        spread = l.sem("spread")

        with nc.Block() as block:
            @block.sync
            def _(sp):
                sp.dma_start(groups_i[0:NG, :], a["dst"][0:NG * G * P].rearrange("(g e) -> g e", g=NG)).then_inc(dst_in, 16)
                sp.dma_start(groups_i[NG:NG + 1, :], a["dst"][E - G * P:E].rearrange("(g e) -> g e", g=1)).then_inc(dst_in, 16)
                sp.dma_start(dst_i[:, 0:ET], a["dst_cols"]).then_inc(dst_in, 16)
                sp.dma_start(dst_i[0:EL, ET:ET + 1], a["dst_tail"]).then_inc(dst_in, 16)
                sp.dma_start(c["src"][:, 0:ET], a["src_cols"]).then_inc(src_in, 16)
                sp.dma_start(c["src"][0:EL, ET:ET + 1], a["src_tail"]).then_inc(src_in, 16)
                sp.dma_start(c["w1b"][:, :], a["W1"][D:D + ED, :]).then_inc(src_in, 16)
                sp.wait_ge(src_in, 48)

            @block.gpsimd
            def _(pool):
                nc.gpsimd.memset(c["ident"][:, :], 0.0).then_inc(filled, 1)
                nc.gpsimd.memset(c["ones"][:, :], 1.0).then_inc(filled, 1)
                nc.gpsimd.memset(c["before"][:, :], 1.0).then_inc(filled, 1)
                nc.gpsimd.memset(c["zeros"][:, :], 0.0).then_inc(filled, 1)
                pool.wait_ge(filled, 4)
                nc.gpsimd.affine_select(out=c["ident"][:, :], in_=c["ident"][:, :], compare_op=ALU.not_equal,
                                        fill=1.0, base=0, pattern=[[-1, P]], channel_multiplier=1).then_inc(ident_made, 1)
                nc.gpsimd.tensor_copy(c["ones_bf16"][:, :], c["ones"][:, :])
                nc.gpsimd.affine_select(out=c["before"][:, :], in_=c["before"][:, :], compare_op=ALU.is_gt,
                                        fill=0.0, base=0, pattern=[[1, P]], channel_multiplier=-1).then_inc(masks_made, 1)
                nc.gpsimd.iota(c["iota"][:, :], pattern=[[1, W]], base=0, channel_multiplier=0,
                               allow_small_or_imprecise_dtypes=True).then_inc(masks_made, 1)
                pool.wait_ge(masks_made, 2)
                nc.gpsimd.tensor_copy(c["before_bf16"][:, :], c["before"][:, :]).then_inc(masks_made, 1)
                pool.wait_ge(masks_made, 3)

            @block.vector
            def _(dve):
                n = [0]

                def link(ins):
                    n[0] += 1
                    ins.then_inc(step, 1)
                    dve.wait_ge(step, n[0])

                link(nc.vector.memset(c["eps"][:, :], LN_EPS))
                link(nc.vector.memset(c["sums"][:, :, :, :], 0.0))
                link(nc.vector.memset(c["tail_sums"][:, :, :], 0.0))
                link(nc.vector.memset(lo_rows[:, :], 1.0))
                dve.wait_ge(dst_in, 64)
                link(nc.vector.tensor_reduce(lohi[:, 0:1], groups_i[:, :], X, ALU.min))
                link(nc.vector.tensor_reduce(lohi[:, 1:2], groups_i[:, :], X, ALU.max))
                link(nc.vector.tensor_scalar(hi_rows[:, :], lo_rows[:, :], lohi[:, 1:2], None, ALU.mult))
                link(nc.vector.tensor_scalar(lo_rows[:, :], lo_rows[:, :], lohi[:, 0:1], None, ALU.mult))
                nc.vector.tensor_copy(c["to_base"][:, 0:ET], dst_i[:, 0:ET]).then_inc(lohi_made, 1)
                dve.wait_ge(lohi_made, 1)
                link(nc.vector.tensor_copy(c["to_base"][0:EL, ET:ET + 1], dst_i[0:EL, ET:ET + 1]))
                dve.wait_ge(spread, 2)
                link(nc.vector.tensor_copy(c["base"][:, :], ps_lo[:, 0:NG + 1]))
                link(nc.vector.tensor_tensor(span[:, :], ps_hi[:, 0:NG + 1], c["base"][:, :], ALU.subtract))
                link(nc.vector.tensor_reduce(widest[:, :], span[0:1, :], X, ALU.max))
                link(nc.vector.tensor_copy(windows_i[:, :], widest[:, :]))
                link(nc.vector.tensor_scalar(windows_i[:, :], windows_i[:, :], W.bit_length() - 1, None, ALU.arith_shift_right))
                link(nc.vector.tensor_scalar(c["passes"][:, :], windows_i[:, :], 1, None, ALU.add))
                link(nc.vector.tensor_copy(c["base_i"][:, :], c["base"][0:1, :]))
                view = c["to_base"][:, 0:ET].rearrange("p (g u) -> p g u", u=G)
                link(nc.vector.tensor_tensor(view, c["base"][:, 0:NG].unsqueeze(2).to_broadcast([P, NG, G]), view, ALU.subtract))
                link(nc.vector.tensor_tensor(c["to_base"][0:EL, ET:ET + 1], c["base"][0:EL, NG:NG + 1],
                                             c["to_base"][0:EL, ET:ET + 1], ALU.subtract))

            @block.tensor
            def _(pe):
                pe.wait_ge(ident_made, 1)
                pe.wait_ge(lohi_made, 1)
                nc.tensor.matmul(ps_lo[:, 0:NG + 1], lo_rows[:, :], c["ident"][0:NG + 1, 0:NG + 1], start=True, stop=True).then_inc(spread, 1)
                nc.tensor.matmul(ps_hi[:, 0:NG + 1], hi_rows[:, :], c["ident"][0:NG + 1, 0:NG + 1], start=True, stop=True).then_inc(spread, 1)

        l.clear_sems()


def node_phase(nc, m, c, a, d):
    with Memory(nc, "a_") as l:
        w1a = l.sb("w1a", [P, 2, HID])
        wkv = l.sb("wkv", [P, 2, 2 * D])
        b1_all = l.sb("b1_all", [P, HID])
        bkv_all = l.sb("bkv_all", [P, 2 * D])
        x_in = [l.sb(f"x{p}", [P, D]) for p in range(2)]
        xn = [l.sb(f"xn{p}", [P, D]) for p in range(2)]
        xT = [l.sb(f"xT{p}", [P, 2, P]) for p in range(2)]
        proj = [l.sb(f"proj{p}", [P, HID]) for p in range(2)]
        v1 = [l.sb(f"v1{p}", [P, H, VN + ZN]) for p in range(2)]
        feat = [l.sb(f"feat{p}", [P, H, NF]) for p in range(2)]
        tail = [l.sb(f"tail{p}", [P, H, TW]) for p in range(2)]
        k_raw = l.sb("k_raw", [P, H, HD])
        k_sq = l.sb("k_sq", [P, H, HD])
        kk = l.sb("kk", [P, H, HD + HQ])
        stats = l.sb("stats", [P, 6])
        mv = l.sb("mv", [P, 2])
        rstd = l.sb("rstd", [P, 1])
        ssq = l.sb("ssq", [P, H])
        norm = l.sb("norm", [P, H])
        ps_kv = [l.ps(f"ps_sum{j}", [P, 512]) for j in range(3)]
        tail_place = [(0, 3 * FB * VW), (1, 3 * FB * VW), (2, 2 * FB * VW), (2, 2 * FB * VW + VN)]
        assert 3 * FB * VW + VN <= 512 and 2 * FB * VW + 2 * VN <= 512
        ps_t = l.ps("ps_t", [P, 2, 2, P])
        ps_p = [l.ps(f"ps_p{p}", [P, 512]) for p in range(2)]
        ps_k = [l.ps(f"ps_k{p}", [P, 512]) for p in range(2)]
        weights_in = l.sem("weights_in")
        x_loaded = [l.sem(f"x_loaded{p}") for p in range(2)]
        xn_stored = [l.sem(f"xn_stored{p}") for p in range(2)]
        xT_stored = [l.sem(f"xT_stored{p}") for p in range(2)]
        p_stored = [l.sem(f"p_stored{p}") for p in range(2)]
        const_made = l.sem("const_made")
        v1_cleared = l.sem("v1_cleared")
        var_ready = l.sem("var_ready")
        std_ready = l.sem("std_ready")
        xn_ready = l.sem("xn_ready")
        turned = l.sem("turned")
        xT_ready = l.sem("xT_ready")
        p_done = l.sem("p_done")
        kv_done = l.sem("kv_done")
        p_ready = l.sem("p_ready")
        ssq_ready = l.sem("ssq_ready")
        norm_ready = l.sem("norm_ready")
        feat_ready = l.sem("feat_ready")
        feat_used = l.sem("feat_used")
        sums_read = l.sem("sums_read")
        norm_step = l.sem("norm_step")
        key_step = l.sem("key_step")
        acc_cleared = l.sem("acc_cleared")
        x_d, wkv_d = a["x"], a["wqkvT"]

        with nc.Block() as block:
            @block.gpsimd
            def _(pool):
                for k in range(FB + 1):
                    nc.gpsimd.memset(c["acc"][:, k, :], 0.0).then_inc(acc_cleared, 1)
                pool.wait_ge(acc_cleared, FB + 1)

            @block.sync
            def _(sp):
                for p in range(2):
                    sp.dma_start(x_in[p][:, :], x_d[p * P:(p + 1) * P, :]).then_inc(x_loaded[p], 16)
                sp.dma_start(w1a[:, :, :], a["W1"][0:D, :].rearrange("(c k) f -> k c f", c=2)).then_inc(weights_in, 16)
                sp.dma_start(wkv[:, :, :], wkv_d[:, D:3 * D].rearrange("(c k) f -> k c f", c=2)).then_inc(weights_in, 16)
                sp.dma_start(b1_all[:, :], rows(a["b1"], P, HID)).then_inc(weights_in, 16)
                sp.dma_start(bkv_all[:, :], rows(a["bqkv"], P, 2 * D, D)).then_inc(weights_in, 16)

                def body(t, i, p, r, nr):
                    sp.wait_ge(xn_ready, t + 1)
                    ahead = t + 2 if not isinstance(t, int) or t + 2 < NT else None
                    if ahead is not None:
                        n = LAST if isinstance(t, int) and t == NT - 3 else P
                        sp.dma_start(x_in[p][0:n, :], x_d[bass.ds(ahead * P, n), :]).then_inc(x_loaded[p], 16)
                    sp.dma_start(d["xn"][bass.ds(t * P, r), :], xn[p][0:r, :]).then_inc(xn_stored[p], 16)
                    sp.wait_ge(xT_ready, t + 1)
                    sp.dma_start(d["xT"][bass.ds(t * P, P), :].rearrange("k (c n) -> k c n", c=2)[:, :, 0:r],
                                 xT[p][:, :, 0:r]).then_inc(xT_stored[p], 16)
                    sp.wait_ge(p_ready, t + 1)
                    sp.dma_start(d["proj"][bass.ds(t * P, r), :], proj[p][0:r, :]).then_inc(p_stored[p], 16)

                each_tile(sp, body)
                for p in range(2):
                    for stored in (xn_stored, xT_stored, p_stored):
                        sp.wait_ge(stored[p], 16 * ((NT + 1 - p) // 2))

            @block.vector
            def _(dve):
                for p in range(2):
                    nc.vector.memset(tail[p][:, :, :], 0.0)
                    nc.vector.memset(v1[p][:, :, :], 0.0).then_inc(v1_cleared, 1)
                dve.wait_ge(v1_cleared, 2)
                for p in range(2):
                    nc.vector.memset(v1[p][:, :, ZN:ZN + 1], 1.0)
                    last = nc.vector.memset(tail[p][:, :, FT - 1:FT], SCALE ** 4)
                last.then_inc(const_made, 1)
                dve.wait_ge(const_made, 1)

                def node_norm(t, i, p, r):
                    link = Chain(dve, norm_step, t, 2)
                    dve.wait_ge(x_loaded[p], 16 * (i + 1))
                    link(nc.vector.bn_stats(stats[0:r, :], x_in[p][0:r, :]))
                    carry_wait(dve, c["carrier_dve"])
                    nc.vector.bn_aggr(mv[0:r, :], stats[0:r, :]).then_inc(var_ready, 1)
                    dve.wait_ge(std_ready, t + 1)
                    link(nc.vector.reciprocal(rstd[0:r, :], rstd[0:r, :]))
                    if known(t, 2):
                        dve.wait_ge(xn_stored[p], 16 * i)
                        dve.wait_ge(turned, t - 1)
                    nc.vector.tensor_scalar(xn[p][0:r, :], x_in[p][0:r, :], mv[0:r, 0:1], rstd[0:r, :],
                                            ALU.subtract, ALU.mult).then_inc(xn_ready, 1)
                    dve.wait_ge(xn_ready, t + 1)
                    link.end()

                def keys(t, i, p, r):
                    link = Chain(dve, key_step, t, 8)
                    dve.wait_ge(p_done, t + 1)
                    if known(t, 2):
                        dve.wait_ge(p_stored[p], 16 * i)
                    nc.vector.tensor_tensor(proj[p][0:r, :], ps_p[p][0:r, :], b1_all[0:r, :], ALU.add).then_inc(p_ready, 1)
                    dve.wait_ge(kv_done, t + 1)
                    link(nc.vector.tensor_tensor(k_raw[0:r, :, :], ps_k[p][0:r, 0:D].rearrange("n (h e) -> n h e", h=H),
                                                 bkv_all[0:r, 0:D].rearrange("n (h e) -> n h e", h=H), ALU.add))
                    link(nc.vector.tensor_tensor(k_sq[0:r, :, :], k_raw[0:r, :, :], k_raw[0:r, :, :], ALU.mult))
                    nc.vector.tensor_reduce(ssq[0:r, :], k_sq[0:r, :, :], X, ALU.add).then_inc(ssq_ready, 1)
                    if known(t, 2):
                        dve.wait_ge(feat_used, t - 1)
                    link(nc.vector.tensor_tensor(v1[p][0:r, :, ZN + 1:ZN + VW], ps_k[p][0:r, D:2 * D].rearrange("n (h e) -> n h e", h=H),
                                                 bkv_all[0:r, D:2 * D].rearrange("n (h e) -> n h e", h=H), ALU.add))
                    dve.wait_ge(norm_ready, t + 1)
                    link(nc.vector.tensor_scalar(norm[0:r, :], norm[0:r, :], NORM_EPS, None, ALU.max))
                    link(nc.vector.reciprocal(norm[0:r, :], norm[0:r, :]))
                    link(nc.vector.scalar_tensor_tensor(kk[0:r, :, 0:HD], k_raw[0:r, :, :], SCALE * SCALE,
                                                        norm[0:r, :].unsqueeze(2).to_broadcast([r, H, HD]), ALU.mult, ALU.mult))
                    link(nc.vector.tensor_copy(kk[0:r, :, HD:HD + HQ], kk[0:r, :, 0:HQ]))
                    products(nc, kk, feat[p], r)
                    nc.vector.tensor_scalar(tail[p][0:r, :, 0:HD], kk[0:r, :, 0:HD], SCALE ** 2, None, ALU.mult)
                    link(nc.vector.tensor_tensor(tail[p][0:r, :, HD:HD + HQ], kk[0:r, :, 0:HQ], kk[0:r, :, HQ:HD], ALU.mult))
                    nc.vector.tensor_scalar(feat[p][0:r, :, 0:HD], feat[p][0:r, :, 0:HD], 0.5, None, ALU.mult).then_inc(feat_ready, 1)
                    dve.wait_ge(feat_ready, t + 1)
                    link.end()

                node_norm(0, 0, 0, P)
                node_norm(1, 0, 1, P)
                dve.wait_ge(weights_in, 64)

                def body(t, i, p, r, nr):
                    keys(t, i, p, r)
                    if known_before(t, NT - 2):
                        node_norm(t + 2, i + 1, p, tile_rows(t + 2))

                each_tile(dve, body)

            @block.scalar
            def _(act):
                def root(t, i, p, r):
                    act.wait_ge(var_ready, t + 1)
                    nc.scalar.activation(rstd[0:r, :], mv[0:r, 1:2], ACT.Sqrt, bias=c["eps"][0:r, :]).then_inc(std_ready, 1)

                def copy_xT(t, i, p, r):
                    act.wait_ge(turned, t + 1)
                    if known(t, 2):
                        act.wait_ge(xT_stored[p], 16 * i)
                        act.wait_ge(kv_done, t - 1)
                    nc.scalar.activation(xT[p][:, :, 0:r], ps_t[:, p, :, 0:r], ACT.Copy).then_inc(xT_ready, 1)

                root(0, 0, 0, P)
                root(1, 0, 1, P)
                copy_xT(0, 0, 0, P)

                def body(t, i, p, r, nr):
                    if nr:
                        copy_xT(t + 1, i + p, 1 - p, nr)
                    act.wait_ge(ssq_ready, t + 1)
                    nc.scalar.activation(norm[0:r, :], ssq[0:r, :], ACT.Sqrt, scale=SCALE * SCALE).then_inc(norm_ready, 1)
                    if known_before(t, NT - 2):
                        root(t + 2, i + 1, p, tile_rows(t + 2))

                each_tile(act, body)
                act.wait_ge(feat_used, NT)
                for j in range(3):
                    n = min(3, H - 3 * j)
                    nc.scalar.activation(c["sums"][:, :, 3 * j:3 * j + n, 0:VW].rearrange("f b h e -> f h b e"),
                                         ps_kv[j][:, 0:n * FB * VW].rearrange("f (h b e) -> f h b e", h=n, e=VW), ACT.Copy, scale=1.0 / N)
                for m, (j, at) in enumerate(tail_place):
                    for k in range(2):
                        last = nc.scalar.activation(c["tail_sums"][k * TW:(k + 1) * TW, m, k * VW:(k + 1) * VW],
                                                    ps_kv[j][k * TW:(k + 1) * TW, at + k * PW:at + k * PW + VW], ACT.Copy, scale=1.0 / N)
                last.then_inc(sums_read, 1)
                act.wait_ge(sums_read, 1)

            @block.tensor
            def _(pe):
                for j in range(3):
                    nc.tensor.matmul(ps_kv[j][:, :], c["zeros"][:, 0:P], c["zeros"][:, :], start=True, stop=False, skip_group_check=True)

                def turn(t, i, p, r):
                    pe.wait_ge(xn_ready, t + 1)
                    if known(t, 1):
                        pe.wait_ge(xT_ready, t)
                    for k in range(2):
                        last = nc.tensor.transpose(ps_t[:, p, k, 0:r], xn[p][0:r, k * P:(k + 1) * P], c["ident"][0:r, 0:r])
                    last.then_inc(turned, 1)

                def sums(t, i, p, r):
                    pe.wait_ge(feat_ready, t + 1)
                    for h in range(H):
                        for b in range(FB):
                            at = ((h % 3) * FB + b) * VW
                            nc.tensor.matmul(ps_kv[h // 3][:, at:at + VN], feat[p][0:r, h, b * P:(b + 1) * P], v1[p][0:r, h, ZN:ZN + VN],
                                             start=False, stop=False, skip_group_check=True)
                    for m, (j, at) in enumerate(tail_place):
                        last = nc.tensor.matmul(ps_kv[j][:, at:at + VN], tail[p][0:r, 2 * m:2 * m + 2, :].rearrange("n h e -> n (h e)"),
                                                v1[p][0:r, 2 * m:2 * m + 2, ZN:ZN + PW], start=False, stop=False, skip_group_check=True)
                    last.then_inc(feat_used, 1)

                turn(0, 0, 0, P)

                def body(t, i, p, r, nr):
                    if isinstance(t, int) and t == 0:
                        pe.wait_ge(weights_in, 64)
                    pe.wait_ge(xT_ready, t + 1)
                    if known(t, 2):
                        pe.wait_ge(p_ready, t - 1)
                        pe.wait_ge(feat_ready, t - 1)
                    for k in range(2):
                        last = nc.tensor.matmul(ps_p[p][0:r, :], xT[p][:, k, 0:r], w1a[:, k, :], start=(k == 0), stop=(k == 1))
                    last.then_inc(p_done, 1)
                    for k in range(2):
                        last = nc.tensor.matmul(ps_k[p][0:r, :], xT[p][:, k, 0:r], wkv[:, k, :], start=(k == 0), stop=(k == 1))
                    last.then_inc(kv_done, 1)
                    if nr:
                        turn(t + 1, i + p, 1 - p, nr)
                    if known(t, 1):
                        sums(t - 1, None, 1 - p, P)

                each_tile(pe, body)
                sums(NT - 1, NT // 2, 0, LAST)

        l.clear_sems()


def products(nc, kk, feat, r):
    one = kk[0:r, :, :]
    step = [list(x) for x in one.ap]
    shifted = bass.AP(tensor=one.tensor, offset=one.offset, ap=[step[0], step[1], [1, NF // HD], [1, HD]])
    return nc.vector.tensor_tensor(feat[0:r, :, 0:NF].rearrange("n h (d i) -> n h d i", i=HD),
                                   kk[0:r, :, 0:HD].unsqueeze(2).to_broadcast([r, H, NF // HD, HD]), shifted, ALU.mult)


def edge_phase(nc, m, c, a, d, w):
    with Memory(nc, "e_") as l:
        w1b, ones = c["w1b"], c["ones_bf16"]
        attr = [l.sb(f"attr{p}", [P, G * P]) for p in range(2)]
        idx = [l.sb(f"idx{p}", [P, G], I32) for p in range(2)]
        hid = [l.sb(f"hid{s}", [P, HID]) for s in range(2 * G)]
        high = [l.sb(f"high{u}", [P, HID], F32R) for u in range(G)]
        low = [l.sb(f"low{u}", [P, HID], F32R) for u in range(G)]
        away = l.sb("away", [P, G, W])
        hot = [l.sb(f"hot{p}", [P, G, W], F32R) for p in range(2)]
        hot_sum = [l.sb(f"hot_sum{p}", [P, W], BF16) for p in range(2)]
        window = [l.sb(f"window{p}", [W, HID]) for p in range(2)]
        ps_h = [l.ps(f"ps_h{b}", [P, 512]) for b in range(4)]
        ps_w = [l.ps(f"ps_w{p}", [W, 512]) for p in range(2)]
        ps_s = [l.ps(f"ps_s{p}", [P, FB + 1, W]) for p in range(2)]
        sems = {k: l.sem(k) for k in ("idx_ready", "prod_done", "added", "high_ready", "low_ready", "seg_done", "away_ready", "hot_ready",
                                      "hot_summed", "window_ready", "sum_done", "acc_done")}
        attr_in = [l.sem(f"attr_in{p}") for p in range(2)]
        rows_in = [l.sem(f"rows_in{s}") for s in range(2 * G)]

        everything = (nc, c, a, d, w1b, attr, idx, hid, high, low, away, hot, hot_sum, window, ones, ps_h, ps_w, ps_s,
                      sems, attr_in, rows_in)
        passes = nc.values_load(c["passes"][0:1, 0:1], min_val=1, max_val=(N + W - 1) // W + 1)
        edge_pass(True, w, *everything)
        with nc.If(passes > 1):
            with nc.Fori(1, passes):
                with nc.Block() as block:
                    @block.gpsimd
                    def _(pool):
                        pool.dma_reset()
                        for s in rows_in:
                            pool.sem_clear(s)

                    @block.sync
                    def _(sp):
                        for s in list(sems.values()) + attr_in:
                            sp.sem_clear(s)

                    @block.vector
                    def _(dve):
                        nc.vector.tensor_scalar(c["to_base"][:, 0:ET], c["to_base"][:, 0:ET], float(W), None, ALU.add)
                        nc.vector.tensor_scalar(c["to_base"][0:EL, ET:ET + 1], c["to_base"][0:EL, ET:ET + 1], float(W), None, ALU.add)
                        nc.vector.tensor_scalar(c["base"][0:1, :], c["base"][0:1, :], float(W), float(N), ALU.add, ALU.min).then_inc(c["base_moved"], 1)
                        dve.wait_ge(c["base_moved"], 1)
                        nc.vector.tensor_copy(c["base_i"][:, :], c["base"][0:1, :]).then_inc(c["base_moved"], 1)
                        dve.wait_ge(c["base_moved"], 2)
                        dve.sem_clear(c["base_moved"])

                edge_pass(False, w, *everything)
        nc.end_ifs()


def edge_pass(first, weights, nc, c, a, d, w1b, attr, idx, hid, high, low, away, hot, hot_sum, window, ones, ps_h, ps_w, ps_s,
              sems, attr_in, rows_in):
    idx_ready, prod_done, added, high_ready = sems["idx_ready"], sems["prod_done"], sems["added"], sems["high_ready"]
    low_ready, seg_done, hot_ready, hot_summed = sems["low_ready"], sems["seg_done"], sems["hot_ready"], sems["hot_summed"]
    away_ready = sems["away_ready"]
    window_ready, sum_done, acc_done = sems["window_ready"], sems["sum_done"], sems["acc_done"]

    def each_group(eng, body):
        body(0, 0, 0, G, P)
        body(1, 0, 1, G, P)
        with eng.Fori(1, NG // 2) as i:
            body(2 * i, i, 0, G, P)
            body(2 * i + 1, i, 1, G, P)
        body(NG - 1, NG // 2, 0, G, P)
        body(NG, NG // 2, 1, 1, EL)

    banks = [0, 1, 2, 3, 0, 1, 2, 3, 1, 2]
    assert len(banks) == 2 * G
    back = [next(k for k in range(1, 2 * G + 1) if banks[s - k] == banks[s]) for s in range(2 * G)]

    with nc.Block() as block:
        @block.sync
        def _(sp):
            def body(g, i, p, n, r):
                if known(g, 2):
                    sp.wait_ge(prod_done, G * (g - 1))
                sp.dma_start(attr[p][:, 0:(n - 1) * P + r], a["attrT"][:, bass.ds(g * (G * P), (n - 1) * P + r)]).then_inc(attr_in[p], 16)

            body(0, 0, 0, G, P)
            body(1, 0, 1, G, P)
            if first:
                weights.load(nc, sp, a)
            with sp.Fori(1, NG // 2) as i:
                body(2 * i, i, 0, G, P)
                body(2 * i + 1, i, 1, G, P)
            body(NG - 1, NG // 2, 0, G, P)
            body(NG, NG // 2, 1, 1, EL)

        @block.gpsimd
        def _(pool):
            def body(g, i, p, n, r):
                if known(g, 2):
                    for u in range(G):
                        pool.wait_ge(rows_in[p * G + u], 16 * i)
                nc.gpsimd.tensor_copy(idx[p][0:r, 0:n], c["src"][0:r, bass.ds(g * G, n)]).then_inc(idx_ready, 1)
                pool.wait_ge(idx_ready, g + 1)
                for u in range(n):
                    if known(g, 2):
                        pool.wait_ge(low_ready, (g - 2) * G + u + 1)
                    carry_wait(pool, c["carrier_pool"])
                    nc.gpsimd.indirect_dma_start(
                        out=hid[p * G + u][0:r, :], out_offset=None, in_=d["proj"][:, :],
                        in_offset=bass.IndirectOffsetOnAxis(ap=idx[p][0:r, u:u + 1].bitcast(U32), axis=0)).then_inc(rows_in[p * G + u], 16)

            each_group(pool, body)

        @block.tensor
        def _(pe):
            def segment(g, p, u, n, r):
                pe.wait_ge(low_ready, g * G + u + 1)
                if u == 0:
                    pe.wait_ge(hot_ready, g + 1)
                    if known(g, 2):
                        pe.wait_ge(window_ready, g - 1)
                nc.tensor.matmul(ps_w[p][:, :], hot[p][0:r, u, :], high[u][0:r, :], start=(u == 0), stop=False)
                nc.tensor.matmul(ps_w[p][:, :], hot[p][0:r, u, :], low[u][0:r, :], start=False, stop=(u == n - 1)).then_inc(seg_done, 1)

            def turn_window(g, p, r):
                pe.wait_ge(window_ready, g + 1)
                pe.wait_ge(hot_summed, g + 1)
                if known(g, 2):
                    pe.wait_ge(acc_done, g - 1)
                    carry_wait(pe, c["carrier_pe"])
                for k in range(FB):
                    nc.tensor.transpose(ps_s[p][:, k, :], window[p][:, k * P:(k + 1) * P], c["ident"][0:W, 0:W])
                nc.tensor.matmul(ps_s[p][:, FB, :], ones[0:r, :], hot_sum[p][0:r, :], start=True, stop=True).then_inc(sum_done, 1)

            def body(g, i, p, n, r):
                for u in range(n):
                    if u == 0:
                        pe.wait_ge(attr_in[p], 16 * (i + 1))
                    s = p * G + u
                    if known(g * G + u, back[s]):
                        pe.wait_ge(added, g * G + u - back[s] + 1)
                    nc.tensor.matmul(ps_h[banks[s]][0:r, :], attr[p][:, u * P:u * P + r], w1b[:, :], start=True, stop=True).then_inc(prod_done, 1)
                    if u >= LAG:
                        segment(g, p, u - LAG, n, r)
                    elif known(g, 1):
                        segment(g - 1, 1 - p, u + G - LAG, G, P)
                    if u == G - 1 and known(g, 1):
                        turn_window(g - 1, 1 - p, P)

            each_group(pe, body)
            for u in range(G - LAG + 1, G):
                segment(NG - 1, 0, u, G, P)
            segment(NG, 1, 0, 1, EL)
            turn_window(NG - 1, 0, P)
            turn_window(NG, 1, EL)

        @block.vector
        def _(dve):
            def add_window(g, p):
                at = dve.value_load(c["base_i"][0:1, bass.ds(g, 1)], min_val=0, max_val=N)
                dve.wait_ge(sum_done, g + 1)
                if known(g, 1):
                    dve.wait_ge(acc_done, g)
                nodes = c["acc"][:, :, bass.ds(at, W)]
                nc.vector.tensor_tensor(nodes, ps_s[p][:, :, :], nodes, ALU.add).then_inc(acc_done, 1)

            def split(g, p, u, r):
                dve.wait_ge(high_ready, g * G + u + 1)
                nc.vector.scalar_tensor_tensor(low[u][0:r, :], hid[p * G + u][0:r, :], 0.0, high[u][0:r, :],
                                               ALU.max, ALU.subtract).then_inc(low_ready, 1)

            def body(g, i, p, n, r):
                for u in range(n):
                    s = p * G + u
                    dve.wait_ge(prod_done, g * G + u + 1)
                    dve.wait_ge(rows_in[s], 16 * (i + 1))
                    nc.vector.tensor_tensor(hid[s][0:r, :], ps_h[banks[s]][0:r, :], hid[s][0:r, :], ALU.add).then_inc(added, 1)
                    if u >= 1:
                        split(g, p, u - 1, r)
                    elif known(g, 1):
                        split(g - 1, 1 - p, G - 1, P)
                    if u == min(2, n - 1):
                        dve.wait_ge(hot_ready, g + 1)
                        if known(g, 2):
                            dve.wait_ge(sum_done, g - 1)
                        with nc.allow_low_precision("counts up to G are exact"):
                            nc.vector.tensor_reduce(hot_sum[p][0:r, :], hot[p][0:r, 0:n, :].rearrange("e u w -> e w u"), X, ALU.add).then_inc(hot_summed, 1)
                    if u == 0 and known(g, 2):
                        add_window(g - 2, p)

            each_group(dve, body)
            split(NG, 1, 0, EL)
            add_window(NG - 1, 0)
            add_window(NG, 1)
            dve.wait_ge(acc_done, NG + 1)

        @block.scalar
        def _(act):
            def copy_window(g, p, n):
                act.wait_ge(seg_done, g * G + n)
                if known(g, 2):
                    act.wait_ge(sum_done, g - 1)
                nc.scalar.activation(window[p][:, :], ps_w[p][:, :], ACT.Copy).then_inc(window_ready, 1)

            def one_hot(g, p, n, r):
                act.wait_ge(away_ready, g + 1)
                if known(g, 2):
                    act.wait_ge(seg_done, G * (g - 1))
                nc.scalar.activation(hot[p][0:r, 0:n, :], away[0:r, 0:n, :], ACT.Relu, scale=-1.0, bias=c["ones"][0:r, 0:1]).then_inc(hot_ready, 1)

            def square(g, u, n, r):
                if known(g, 1) and u == 0:
                    act.wait_ge(hot_ready, g)
                ins = nc.scalar.activation(away[0:r, u:u + 1, :], c["iota"][0:r, :].unsqueeze(1), ACT.Square,
                                           bias=c["to_base"][0:r, bass.ds(g * G + u, 1)])
                if u == n - 1:
                    ins.then_inc(away_ready, 1)

            for u in range(G):
                square(0, u, G, P)
            one_hot(0, 0, G, P)

            def body(g, i, p, n, r):
                for u in range(n):
                    act.wait_ge(added, g * G + u + 1)
                    if known(g, 1):
                        act.wait_ge(seg_done, (g - 1) * G + u + 1)
                    nc.scalar.activation(high[u][0:r, :], hid[p * G + u][0:r, :], ACT.Relu).then_inc(high_ready, 1)
                    if known_before(g, NG):
                        nn, nr = (1, EL) if isinstance(g, int) and g == NG - 1 else (G, P)
                        if u < nn:
                            square(g + 1, u, nn, nr)
                        if u == n - 1:
                            one_hot(g + 1, 1 - p, nn, nr)
                    if u == 2 and known(g, 1):
                        copy_window(g - 1, 1 - p, G)

            each_group(act, body)
            copy_window(NG - 1, 0, G)
            copy_window(NG, 1, 1)


class UpdateWeights(dict):

    def __init__(self, l):
        self.update({
            "w2": l.sb("w2", [P, FB, ED]),
            "w3": l.sb("w3", [P, 3, FH]),
            "w3u": l.sb("w3u", [64, FH]),
            "u_col": l.sb("u_col", [64, 1]),
            "w4": l.sb("w4", [P, FH // P, D]),
            "wq": l.sb("wq", [P, 2, D]),
            "wproj": l.sb("wproj", [P, 2, D]),
            "gate_w": l.sb("gate_w", [P, 2, VN]),
            "b2": l.sb("b2", [ED, 1]),
            "b3": l.sb("b3", [P, FH // P]),
            "bq_all": l.sb("bq_all", [P, D]),
            "b4_all": l.sb("b4_all", [P, D]),
            "gamma_all": l.sb("gamma_all", [P, D]),
            "shift_all": l.sb("shift_all", [P, D]),
            "bproj_all": l.sb("bproj_all", [P, D]),
            "beta_all": l.sb("beta_all", [P, D]),
            "gate_b_all": l.sb("gate_b_all", [P, NE]),
            "temp_all": l.sb("temp_all", [P, H]),
            "in": l.sem("in"),
        })

    def load(self, nc, sp, a):
        pairs = [
            (self["w2"][:, :, :], a["W2"].rearrange("(k f) e -> f k e", f=P)),
            (self["w3"][:, :, :], a["W3"][0:3 * P, :].rearrange("(k f) e -> f k e", f=P)),
            (self["w3u"][:, :], a["W3"][3 * P:3 * P + 64, :]),
            (self["u_col"][:, :], a["u"][0:1, :].rearrange("a k -> k a")),
            (self["w4"][:, :, :], a["W4"].rearrange("(k f) e -> f k e", f=P)),
            (self["wq"][:, :, :], a["wqkvT"][:, 0:D].rearrange("(k f) e -> f k e", f=P)),
            (self["wproj"][:, :, :], a["wprojT"].rearrange("(k f) e -> f k e", f=P)),
            (self["gate_w"][:, :, 0:NE], a["gate_w"].rearrange("(k f) e -> f k e", f=P)),
            (self["b2"][:, :], a["b2"].rearrange("(f a) -> f a", a=1)),
            (self["b3"][:, :], a["b3"].rearrange("(k f) -> f k", f=P)),
            (self["bq_all"][:, :], rows(a["bqkv"], P, D)),
            (self["b4_all"][:, :], rows(a["b4"], P, D)),
            (self["gamma_all"][:, :], rows(a["gnn_gamma"], P, D)),
            (self["shift_all"][:, :], rows(a["gnn_beta"], P, D)),
            (self["bproj_all"][:, :], rows(a["bproj"], P, D)),
            (self["beta_all"][:, :], rows(a["ffn_beta"], P, D)),
            (self["gate_b_all"][:, :], rows(a["gate_b"], P, NE)),
            (self["temp_all"][:, :], rows(a["temperature"], P, H)),
        ]
        with nc.allow_non_contiguous_dma(reason="a few bias columns"):
            for to, frm in pairs:
                sp.dma_start(to, frm).then_inc(self["in"], 16)
        self["loads"] = len(pairs)


def update_phase(nc, m, c, a, d, w):
    with Memory(nc, "u_") as l:
        w2, w3, w3u, u_col, w4, wq, wproj, gate_w = (w[k] for k in ("w2", "w3", "w3u", "u_col", "w4", "wq", "wproj", "gate_w"))
        b2, b3, bq_all, b4_all, gamma_all, shift_all = (w[k] for k in ("b2", "b3", "bq_all", "b4_all", "gamma_all", "shift_all"))
        bproj_all, beta_all, gate_b_all, temp_all = (w[k] for k in ("bproj_all", "beta_all", "gate_b_all", "temp_all"))
        x_in = [l.sb(f"x{p}", [P, D]) for p in range(2)]
        xn = [l.sb(f"xn{p}", [P, D]) for p in range(2)]
        xT = [l.sb(f"xT{p}", [P, 2, P]) for p in range(2)]
        q_raw = l.sb("q_raw", [P, H, HD])
        q_sq = l.sb("q_sq", [P, H, HD])
        qq = l.sb("qq", [P, H, HD + HQ])
        feat = [l.sb(f"feat{p}", [P, H, NF]) for p in range(2)]
        tail = [l.sb(f"tail{p}", [P, H, TW]) for p in range(2)]
        featT = l.sb("featT", [P, H + 1, 4, P])
        ssq = l.sb("ssq", [P, H])
        norm = l.sb("norm", [P, H])
        y_inv = l.sb("y_inv", [P, H])
        o = l.sb("o", [P, D])
        oT = l.sb("oT", [P, 2, P])
        cnt = l.sb("cnt", [P, P])
        aggT = [l.sb(f"aggT{p}", [P, P]) for p in range(2)]
        hT = l.sb("hT", [P, FH // P, P])
        y = l.sb("y", [P, D])
        xr = [l.sb(f"xr{p}", [P, D]) for p in range(2)]
        z = [l.sb(f"z{p}", [P, D]) for p in range(2)]
        zT = l.sb("zT", [P, 2, P])
        stats = l.sb("stats", [P, 6])
        mv = l.sb("mv", [P, 2])
        rstd = l.sb("rstd", [P, 1])
        logits = l.sb("logits", [P, NE])
        top_v = l.sb("top_v", [P, 8])
        top_i = l.sb("top_i", [P, 8], U32)
        top_f = l.sb("top_f", [P, 2])
        both = l.sb("both", [P, NE], BF16)
        before, ones = c["before_bf16"], c["ones_bf16"]
        pos = l.sb("pos", [P, NE])
        pick = l.sb("pick", [P, 2, NE])
        row_f = l.sb("row_f", [P, 2])
        row = [l.sb(f"row{p}", [P, 2], I32) for p in range(2)]
        ps_q = l.ps("ps_q", [P, 512])
        ps_f = [l.ps(f"ps_f{j}", [P, 4, P]) for j in range(2)]
        ps_y = l.ps("ps_y", [P, 512])
        ps_h = [l.ps(f"ps_h{j}", [P, 4, P]) for j in range(2)]
        ps_o = l.ps("ps_o", [P, 512])
        ps_s = l.ps("ps_s", [P, 512])
        ps_turn = ps_s[:, 0:2 * P].rearrange("f (k n) -> f k n", k=2)
        ps_agg = ps_y[:, 3 * P:4 * P]
        heads_end = (H - 1) * VW + VN
        ps_pos = ps_y[:, heads_end:heads_end + 2 * NE]
        assert heads_end + 2 * NE <= 3 * P
        ps_gate = ps_s[:, 3 * P:3 * P + VN]
        s = {k: l.sem(k) for k in (
            "b3_done", "consts_ready", "setup_step", "agg_done", "agg_ready", "mlp1_done", "hT_ready", "q_done", "ssq_ready",
            "norm_ready", "feat_ready", "batch_turned", "batch_copied", "y_done", "o_ready", "o_turned", "oT_ready",
            "mlp2_done", "proj_done", "var1_ready", "std1_ready", "var2_ready", "std2_ready", "z_ready", "xr_ready", "z_turned", "zT_ready",
            "gate_done", "routed", "fill_made", "counted", "filled", "row_ready", "row_step", "agg_step", "q_step", "o_step", "final_step", "route_step")}
        loaded = [l.sem(f"loaded{p}") for p in range(2)]
        xT_in = [l.sem(f"xT_in{p}") for p in range(2)]
        stored = [l.sem(f"stored{p}") for p in range(2)]
        placed = [l.sem(f"placed{p}") for p in range(2)]
        NB = H + 1
        assert NB % 2 == 1 and H // 2 == 4 == FB

        with nc.Block() as block:
            @block.sync
            def _(sp):
                def load(t, p, r):
                    sp.dma_start(x_in[p][0:r, :], a["x"][bass.ds(t * P, r), :]).then_inc(loaded[p], 16)
                    sp.dma_start(xn[p][0:r, :], d["xn"][bass.ds(t * P, r), :]).then_inc(loaded[p], 16)

                def load_xT(t, p, r):
                    sp.dma_start(xT[p][:, :, 0:r], d["xT"][bass.ds(t * P, P), :].rearrange("k (c n) -> k c n", c=2)[:, :, 0:r]).then_inc(xT_in[p], 16)

                sp.wait_ge(w["in"], 16 * w["loads"])
                sp.sem_inc(s["b3_done"], 1)
                for p in range(2):
                    load_xT(p, p, P)
                    load(p, p, P)

                def body(t, i, p, r, nr):
                    ahead = None if isinstance(t, int) and t + 2 >= NT else LAST if isinstance(t, int) and t == NT - 3 else P
                    if ahead:
                        sp.wait_ge(s["mlp1_done"], 2 * t + 2)
                        load_xT(t + 2, p, ahead)
                    sp.wait_ge(s["z_ready"], t + 1)
                    sp.dma_start(d["z"][bass.ds(t * P, r), :], z[p][0:r, :]).then_inc(stored[p], 16)
                    sp.wait_ge(s["xr_ready"], t + 1)
                    sp.dma_start(d["xr"][bass.ds(t * P, r), :], xr[p][0:r, :]).then_inc(stored[p], 16)
                    if ahead:
                        load(t + 2, p, ahead)

                each_tile(sp, body)
                for p in range(2):
                    sp.wait_ge(stored[p], 32 * ((NT + 1 - p) // 2))

            @block.tensor
            def _(pe):
                pe.wait_ge(s["b3_done"], 1)
                for j in range(FH // P):
                    last = nc.tensor.matmul(ps_s[:, j:j + 1], w3u[:, j * P:(j + 1) * P], u_col[:, :], start=(j == 0), stop=(j == FH // P - 1), skip_group_check=True)
                last.then_inc(s["b3_done"], 1)
                pe.wait_ge(s["consts_ready"], 1)

                def query(t, i, p, r):
                    pe.wait_ge(xT_in[p], 16 * (i + 1))
                    if known(t, 2):
                        pe.wait_ge(s["var2_ready"], t - 1)
                    for k in range(2):
                        last = nc.tensor.matmul(ps_q[0:r, 0:D], xT[p][:, k, 0:r], wq[:, k, :], start=(k == 0), stop=(k == 1))
                    last.then_inc(s["q_done"], 1)

                def turn_z(t, p, r):
                    pe.wait_ge(s["z_ready"], t + 1)
                    for k in range(2):
                        last = nc.tensor.transpose(ps_turn[:, k, 0:r], z[p][0:r, k * P:(k + 1) * P], c["ident"][0:r, 0:r])
                    last.then_inc(s["z_turned"], 1)

                def gate(t, r):
                    pe.wait_ge(s["zT_ready"], t + 1)
                    for k in range(2):
                        last = nc.tensor.matmul(ps_gate[0:r, :], zT[:, k, 0:r], gate_w[:, k, :], start=(k == 0), stop=(k == 1))
                    last.then_inc(s["gate_done"], 1)

                def turn_batch(t, p, r, b):
                    g = t * NB + b
                    if known(t, 1) or b >= 2:
                        pe.wait_ge(s["batch_copied"], g - 1)
                    for j in range(4):
                        if b == 0:
                            frm = tail[p][0:r, 2 * j:2 * j + 2, :].rearrange("n h e -> n (h e)")
                        else:
                            frm = feat[p][0:r, b - 1, j * P:(j + 1) * P]
                        last = nc.tensor.transpose(ps_f[(p + b) % 2][:, j, 0:r], frm, c["ident"][0:r, 0:r])
                    last.then_inc(s["batch_turned"], 1)

                def attend(t, r, h):
                    pe.wait_ge(s["batch_copied"], t * NB + h + 2)
                    for b in range(FB):
                        last = nc.tensor.matmul(ps_y[0:r, h * VW:h * VW + VN], featT[:, h + 1, b, 0:r], c["sums"][:, b, h, :],
                                                start=(h == 0 and b == 0), stop=False, skip_group_check=True)
                    if h % 2 == 1:
                        last = nc.tensor.matmul(ps_y[0:r, (h - 1) * VW:(h - 1) * VW + VN], featT[:, 0, h // 2, 0:r], c["tail_sums"][:, h // 2, :],
                                                start=False, stop=(h == H - 1), skip_group_check=True)
                    return last

                def aggregate(t, i, p, r):
                    if known(t, 1):
                        pe.wait_ge(s["o_ready"], t)
                    for k in range(FB):
                        last = nc.tensor.matmul(ps_agg[:, 0:r], w2[:, k, :], c["acc"][:, k, bass.ds(t * P, r)], start=(k == 0), stop=(k == FB - 1))
                    last.then_inc(s["agg_done"], 1)

                def count(t):
                    pe.wait_ge(s["routed"], t + 1)
                    nc.tensor.matmul(ps_pos[:, 0:NE], before[:, :], both[:, :], start=True, stop=True)
                    nc.tensor.matmul(ps_pos[:, NE:2 * NE], ones[:, :], both[:, :], start=True, stop=True).then_inc(s["counted"], 1)

                query(0, 0, 0, P)
                aggregate(0, 0, 0, P)

                def body(t, i, p, r, nr):
                    pe.wait_ge(s["agg_ready"], t + 1)
                    if known(t, 1):
                        pe.wait_ge(s["hT_ready"], 2 * t)
                    for j in range(FH // P):
                        for k in range(3):
                            last = nc.tensor.matmul(ps_h[j // 4][:, j % 4, 0:r], w3[:, k, j * P:(j + 1) * P],
                                                    xT[p][:, k, 0:r] if k < 2 else aggT[p][:, 0:r], start=(k == 0), stop=(k == 2))
                        if j % 4 == 3:
                            last.then_inc(s["mlp1_done"], 1)
                            if j == 3:
                                pe.wait_ge(s["feat_ready"], t + 1)
                            turn_batch(t, p, r, j // 4)
                    for b in range(2, NB):
                        turn_batch(t, p, r, b)
                        if b == 2 and known(t, 1):
                            pe.wait_ge(s["o_ready"], t)
                        if b == 2 and known(t, 2):
                            pe.wait_ge(s["filled"], 2 * (t - 1))
                        if b >= 2:
                            attend(t, r, b - 2)
                        if b == 4:
                            if nr:
                                query(t + 1, i + p, 1 - p, nr)
                        if b == 7 and known(t, 1):
                            turn_z(t - 1, 1 - p, P)
                    attend(t, r, H - 1).then_inc(s["y_done"], 1)
                    if known(t, 1):
                        gate(t - 1, P)
                    pe.wait_ge(s["hT_ready"], 2 * t + 2)
                    if known(t, 1):
                        pe.wait_ge(s["z_ready"], t)
                    for j in range(FH // P):
                        last = nc.tensor.matmul(ps_o[0:r, 0:D], hT[:, j, 0:r], w4[:, j, :], start=(j == 0), stop=(j == FH // P - 1))
                    last.then_inc(s["mlp2_done"], 1)
                    pe.wait_ge(s["o_ready"], t + 1)
                    if known(t, 1):
                        pe.wait_ge(s["routed"], t)
                    for k in range(2):
                        last = nc.tensor.transpose(ps_turn[:, k, 0:r], o[0:r, k * P:(k + 1) * P], c["ident"][0:r, 0:r])
                    last.then_inc(s["o_turned"], 1)
                    if known(t, 1):
                        count(t - 1)
                    if nr:
                        aggregate(t + 1, None, None, nr)
                    pe.wait_ge(s["oT_ready"], t + 1)
                    if nr:
                        pe.wait_ge(s["ssq_ready"], t + 2)
                    for k in range(2):
                        last = nc.tensor.matmul(ps_q[0:r, D:2 * D], oT[:, k, 0:r], wproj[:, k, :], start=(k == 0), stop=(k == 1))
                    last.then_inc(s["proj_done"], 1)

                each_tile(pe, body)
                turn_z(NT - 1, 0, LAST)
                gate(NT - 1, LAST)
                pe.wait_ge(s["filled"], 2 * (NT - 1))
                count(NT - 1)

            @block.scalar
            def _(act):
                def root(t, i, p, r):
                    act.wait_ge(s["ssq_ready"], t + 1)
                    nc.scalar.activation(norm[0:r, :], ssq[0:r, :], ACT.Sqrt, scale=SCALE * SCALE).then_inc(s["norm_ready"], 1)

                def copy_zT(t, r):
                    act.wait_ge(s["z_turned"], t + 1)
                    if known(t, 1):
                        act.wait_ge(s["gate_done"], t)
                    nc.scalar.activation(zT[:, :, 0:r], ps_turn[:, :, 0:r], ACT.Copy).then_inc(s["zT_ready"], 1)

                root(0, 0, 0, P)

                def relu(t, r, half):
                    act.wait_ge(s["mlp1_done"], 2 * t + half + 1)
                    if known(t, 1):
                        act.wait_ge(s["mlp2_done"], t)
                    for j in range(4 * half, 4 * half + 4):
                        last = nc.scalar.activation(hT[:, j, 0:r], ps_h[half][:, j % 4, 0:r], ACT.Relu, bias=b3[:, j:j + 1])
                    last.then_inc(s["hT_ready"], 1)

                def body(t, i, p, r, nr):
                    for b in range(NB):
                        act.wait_ge(s["batch_turned"], t * NB + b + 1)
                        if known(t, 1) and b == 0:
                            act.wait_ge(s["y_done"], t)
                        nc.scalar.activation(featT[:, b, :, 0:r], ps_f[(p + b) % 2][:, :, 0:r], ACT.Copy).then_inc(s["batch_copied"], 1)
                        if b == 1 and known(t, 1):
                            deviation(t - 1, P, "2")
                        if b == 3:
                            relu(t, r, 1)
                        if b == 5 and nr:
                            root(t + 1, i + p, 1 - p, nr)
                    if known(t, 1):
                        copy_zT(t - 1, P)
                    act.wait_ge(s["o_turned"], t + 1)
                    if known(t, 1):
                        act.wait_ge(s["proj_done"], t)
                    nc.scalar.activation(oT[:, :, 0:r], ps_turn[:, :, 0:r], ACT.Copy).then_inc(s["oT_ready"], 1)
                    deviation(t, r, "1")
                    if nr:
                        relu(t + 1, nr, 0)

                def deviation(t, r, k):
                    act.wait_ge(s[f"var{k}_ready"], t + 1)
                    nc.scalar.activation(rstd[0:r, :], mv[0:r, 1:2], ACT.Sqrt, bias=c["eps"][0:r, :]).then_inc(s[f"std{k}_ready"], 1)

                relu(0, P, 0)
                each_tile(act, body)
                deviation(NT - 1, LAST, "2")
                copy_zT(NT - 1, LAST)

            @block.vector
            def _(dve):
                link = Chain(dve, s["setup_step"], 0, 6)
                dve.wait_ge(s["b3_done"], 2)
                link(nc.vector.tensor_tensor(b3[:, :], ps_s[:, 0:FH // P], b3[:, :], ALU.add))
                link(nc.vector.tensor_tensor(shift_all[:, :], shift_all[:, :], bproj_all[:, :], ALU.add))
                link(nc.vector.tensor_scalar(temp_all[:, :], temp_all[:, :], SCALE * SCALE, None, ALU.mult))
                link(nc.vector.memset(c["chosen"][:, :, :, :], 0.0))
                nc.vector.memset(c["gate_v"][:, :, :], 0.0)
                nc.vector.memset(gate_w[:, :, NE:VN], 0.0)
                for p in range(2):
                    link(nc.vector.memset(tail[p][:, :, :], 0.0))
                    last = nc.vector.memset(tail[p][:, :, FT - 1:FT], 1.0)
                last.then_inc(s["consts_ready"], 1)
                dve.wait_ge(s["consts_ready"], 1)
                dve.wait_ge(s["fill_made"], 1)

                def queries(t, i, p, r):
                    link = Chain(dve, s["q_step"], t, 7)
                    dve.wait_ge(s["q_done"], t + 1)
                    link(nc.vector.tensor_tensor(q_raw[0:r, :, :], ps_q[0:r, 0:D].rearrange("n (h e) -> n h e", h=H),
                                                 bq_all[0:r, :].rearrange("n (h e) -> n h e", h=H), ALU.add))
                    link(nc.vector.tensor_tensor(q_sq[0:r, :, :], q_raw[0:r, :, :], q_raw[0:r, :, :], ALU.mult))
                    nc.vector.tensor_reduce(ssq[0:r, :], q_sq[0:r, :, :], X, ALU.add).then_inc(s["ssq_ready"], 1)
                    dve.wait_ge(s["norm_ready"], t + 1)
                    link(nc.vector.tensor_scalar(norm[0:r, :], norm[0:r, :], NORM_EPS, None, ALU.max))
                    link(nc.vector.reciprocal(norm[0:r, :], norm[0:r, :]))
                    link(nc.vector.tensor_tensor(norm[0:r, :], norm[0:r, :], temp_all[0:r, :], ALU.mult))
                    link(nc.vector.tensor_tensor(qq[0:r, :, 0:HD], q_raw[0:r, :, :], norm[0:r, :].unsqueeze(2).to_broadcast([r, H, HD]), ALU.mult))
                    link(nc.vector.tensor_copy(qq[0:r, :, HD:HD + HQ], qq[0:r, :, 0:HQ]))
                    if known(t, 2):
                        dve.wait_ge(s["batch_turned"], (t - 1) * NB)
                    products(nc, qq, feat[p], r)
                    nc.vector.tensor_copy(tail[p][0:r, :, 0:HD], qq[0:r, :, 0:HD])
                    nc.vector.tensor_tensor(tail[p][0:r, :, HD:HD + HQ], qq[0:r, :, 0:HQ], qq[0:r, :, HQ:HD], ALU.mult).then_inc(s["feat_ready"], 1)
                    dve.wait_ge(s["feat_ready"], t + 1)
                    link.end()

                def route(t, p, r):
                    link = Chain(dve, s["route_step"], t, 5)
                    dve.wait_ge(s["gate_done"], t + 1)
                    link(nc.vector.tensor_tensor(logits[0:r, :], ps_gate[0:r, 0:NE], gate_b_all[0:r, :], ALU.add))
                    carry_wait(dve, c["carrier_dve"])
                    link(nc.vector.max(top_v[0:r, :], logits[0:r, :]))
                    carry_wait(dve, c["carrier_dve"])
                    link(nc.vector.max_index(top_i[0:r, :], top_v[0:r, :], logits[0:r, :]))
                    link(nc.vector.tensor_copy(top_f[0:r, :], top_i[0:r, 0:2]))
                    nc.vector.tensor_copy(c["gate_v"][0:r, bass.ds(t, 1), :], top_v[0:r, 0:2].unsqueeze(1))
                    for k in range(2):
                        last = nc.vector.tensor_scalar(c["chosen"][0:r, k, bass.ds(t, 1), :], c["iota"][0:r, 0:NE].unsqueeze(1), top_f[0:r, k:k + 1], None, ALU.is_equal)
                    link(last)
                    with nc.allow_low_precision("zeros and ones are exact"):
                        nc.vector.tensor_tensor(both[:, :].unsqueeze(1), c["chosen"][:, 0, bass.ds(t, 1), :], c["chosen"][:, 1, bass.ds(t, 1), :],
                                                ALU.add).then_inc(s["routed"], 1)
                    link.end()

                def fill(t):
                    dve.wait_ge(s["counted"], t + 1)
                    nc.vector.tensor_tensor(pos[:, :], ps_pos[:, 0:NE], c["fill"][:, :], ALU.add).then_inc(s["filled"], 1)
                    dve.wait_ge(s["filled"], 2 * t + 1)
                    nc.vector.tensor_tensor(c["fill"][:, :], ps_pos[:, NE:2 * NE], c["fill"][:, :], ALU.add).then_inc(s["filled"], 1)
                    dve.wait_ge(s["filled"], 2 * t + 2)

                def place(t, i, p, r):
                    link = Chain(dve, s["row_step"], t, 2)
                    link(nc.vector.tensor_tensor(pick[:, :, :], pos[:, :].unsqueeze(1).to_broadcast([P, 2, NE]),
                                                 c["chosen"][:, :, bass.ds(t, 1), :].rearrange("n k a e -> n (k a) e"), ALU.mult))
                    link(nc.vector.tensor_reduce(row_f[:, :], pick[:, :, :], X, ALU.add))
                    if known(t, 2):
                        dve.wait_ge(placed[p], 32 * i)
                    nc.vector.tensor_copy(row[p][:, :], row_f[:, :]).then_inc(s["row_ready"], 1)
                    link.end()

                def mean(t, i, p, r):
                    link = Chain(dve, s["agg_step"], t, 3)
                    counts = c["acc"][:, FB, bass.ds(t * P, r)]
                    link(nc.vector.tensor_scalar(cnt[:, 0:r], counts, 1.0, None, ALU.max))
                    link(nc.vector.reciprocal(cnt[:, 0:r], cnt[:, 0:r]))
                    dve.wait_ge(s["agg_done"], t + 1)
                    link(nc.vector.scalar_tensor_tensor(aggT[p][:, 0:r], counts, b2[:, 0:1], ps_agg[:, 0:r], ALU.mult, ALU.add))
                    nc.vector.tensor_tensor(aggT[p][:, 0:r], aggT[p][:, 0:r], cnt[:, 0:r], ALU.mult).then_inc(s["agg_ready"], 1)
                    link.end()

                mean(0, 0, 0, P)
                queries(0, 0, 0, P)

                def body(t, i, p, r, nr):
                    if nr:
                        queries(t + 1, i + p, 1 - p, nr)
                    link = Chain(dve, s["o_step"], t, 1)
                    dve.wait_ge(s["y_done"], t + 1)
                    heads = ps_y[0:r, 0:H * VW].rearrange("n (h e) -> n h e", h=H)
                    link(nc.vector.reciprocal(y_inv[0:r, :].unsqueeze(2), heads[:, :, 0:1]))
                    if known(t, 1):
                        dve.wait_ge(s["o_turned"], t)
                    nc.vector.tensor_tensor(o[0:r, :].rearrange("n (h e) -> n h e", h=H), heads[:, :, 1:VW],
                                            y_inv[0:r, :].unsqueeze(2).to_broadcast([r, H, HD]), ALU.mult).then_inc(s["o_ready"], 1)
                    link.end()
                    if known(t, 1):
                        route(t - 1, 1 - p, P)
                    if nr:
                        mean(t + 1, None, 1 - p, nr)
                    if known(t, 1):
                        fill(t - 1)
                    link = Chain(dve, s["final_step"], t, 11)
                    dve.wait_ge(s["mlp2_done"], t + 1)
                    dve.wait_ge(loaded[p], 32 * (i + 1))
                    link(nc.vector.tensor_tensor(y[0:r, :], ps_o[0:r, 0:D], xn[p][0:r, :], ALU.add))
                    link(nc.vector.tensor_tensor(y[0:r, :], y[0:r, :], b4_all[0:r, :], ALU.add))
                    link(nc.vector.bn_stats(stats[0:r, :], y[0:r, :]))
                    carry_wait(dve, c["carrier_dve"])
                    nc.vector.bn_aggr(mv[0:r, :], stats[0:r, :]).then_inc(s["var1_ready"], 1)
                    dve.wait_ge(s["std1_ready"], t + 1)
                    link(nc.vector.reciprocal(rstd[0:r, :], rstd[0:r, :]))
                    link(nc.vector.tensor_scalar(y[0:r, :], y[0:r, :], mv[0:r, 0:1], rstd[0:r, :], ALU.subtract, ALU.mult))
                    link(nc.vector.tensor_tensor(y[0:r, :], y[0:r, :], gamma_all[0:r, :], ALU.mult))
                    link(nc.vector.tensor_tensor(y[0:r, :], y[0:r, :], shift_all[0:r, :], ALU.add))
                    link(nc.vector.tensor_tensor(y[0:r, :], y[0:r, :], x_in[p][0:r, :], ALU.add))
                    dve.wait_ge(s["proj_done"], t + 1)
                    if known(t, 2):
                        dve.wait_ge(stored[p], 32 * i)
                        dve.wait_ge(placed[p], 32 * i)
                    link(nc.vector.tensor_tensor(xr[p][0:r, :], ps_q[0:r, D:2 * D], y[0:r, :], ALU.add))
                    link(nc.vector.bn_stats(stats[0:r, :], xr[p][0:r, :]))
                    carry_wait(dve, c["carrier_dve"])
                    nc.vector.bn_aggr(mv[0:r, :], stats[0:r, :]).then_inc(s["var2_ready"], 1)
                    dve.wait_ge(s["std2_ready"], t + 1)
                    link(nc.vector.reciprocal(rstd[0:r, :], rstd[0:r, :]))
                    nc.vector.tensor_scalar(z[p][0:r, :], xr[p][0:r, :], mv[0:r, 0:1], rstd[0:r, :], ALU.subtract, ALU.mult).then_inc(s["z_ready"], 1)
                    dve.wait_ge(s["z_ready"], t + 1)
                    nc.vector.tensor_tensor(xr[p][0:r, :], xr[p][0:r, :], beta_all[0:r, :], ALU.add).then_inc(s["xr_ready"], 1)
                    link.end()
                    if known(t, 1):
                        place(t - 1, i if p else i - 1, 1 - p, P)

                each_tile(dve, body)
                route(NT - 1, 0, LAST)
                fill(NT - 1)
                place(NT - 1, NT // 2, 0, LAST)

            @block.gpsimd
            def _(pool):
                nc.gpsimd.iota(c["fill"][:, :], pattern=[[CAP, NE]], base=0, channel_multiplier=0,
                               allow_small_or_imprecise_dtypes=True).then_inc(s["fill_made"], 1)

                def body(t, i, p, r, nr):
                    pool.wait_ge(s["row_ready"], t + 1)
                    pool.wait_ge(s["z_ready"], t + 1)
                    carry_wait(pool, c["carrier_pool"])
                    for k in range(2):
                        nc.gpsimd.indirect_dma_start(
                            out=d["rows"][:, :], out_offset=bass.IndirectOffsetOnAxis(ap=row[p][0:r, k:k + 1].bitcast(U32), axis=0),
                            in_=z[p][0:r, :], in_offset=None).then_inc(placed[p], 16)

                each_tile(pool, body)
                for p in range(2):
                    pool.wait_ge(placed[p], 32 * ((NT + 1 - p) // 2))


def route_phase(nc, m, c, a, d, w):
    with Memory(nc, "r_") as l:
        both = l.sb("both", [P, NT, NE])
        rank = l.sb("rank", [P, NT, NE])
        total = l.sb("total", [P, NT, NE])
        spare = l.sb("spare", [P, NT, NE])
        tiles_i = l.sb("tiles_i", [P, NE], I32)
        tiles = l.sb("tiles", [P, NE])
        ends_a = l.sb("ends_a", [P, NE])
        ends_b = l.sb("ends_b", [P, NE])
        begins = l.sb("begins", [P, NE])
        prod = l.sb("prod", [P, NT, NE])
        slot_f = l.sb("slot_f", [P, 2, NT])
        over = l.sb("over", [1, MT, NE])
        tile_no = l.sb("tile_no", [1, MT])
        owner = l.sb("owner", [1, MT])
        gap = l.sb("gap", [P, NT])
        node_no = l.sb("node_no", [P, 1])
        first_row = l.sb("first_row", [1, NE])
        start_f = l.sb("start_f", [1, MT])
        real = l.sb("real", [1, MT])
        unfilled = l.sb("unfilled", [P, NE], I32)
        zeros = l.sb("zeros", [P, D])
        share = c["share"]
        ps_rank = l.ps("ps_rank", [P, 512])
        ps_total = l.ps("ps_total", [P, 512])
        step = l.sem("step")
        both_ready = l.sem("both_ready")
        ranked = l.sem("ranked")
        gap_ready = l.sem("gap_ready")
        exp_ready = l.sem("exp_ready")
        unfilled_ready = l.sem("unfilled_ready")
        zeros_made = l.sem("zeros_made")
        filled = l.sem("filled")
        iota_made = l.sem("iota_made")
        assert NT * NE <= 512

        with nc.Block() as block:
            @block.sync
            def _(sp):
                load_set(sp, a, w, 0)

            @block.tensor
            def _(pe):
                pe.wait_ge(both_ready, 1)
                flat = both[:, :, :].rearrange("n t e -> n (t e)")
                nc.tensor.matmul(ps_rank[:, 0:NT * NE], c["before"][:, :], flat, start=True, stop=True).then_inc(ranked, 1)
                nc.tensor.matmul(ps_total[:, 0:NT * NE], c["ones"][:, :], flat, start=True, stop=True).then_inc(ranked, 1)

            @block.scalar
            def _(act):
                act.wait_ge(gap_ready, 1)
                nc.scalar.activation(gap[:, :], gap[:, :], ACT.Exp).then_inc(exp_ready, 1)

            @block.vector
            def _(dve):
                n = [0]

                def link(ins):
                    n[0] += 1
                    ins.then_inc(step, 1)
                    dve.wait_ge(step, n[0])

                nc.vector.tensor_tensor(both[:, :, :], c["chosen"][:, 0, :, :], c["chosen"][:, 1, :, :], ALU.add).then_inc(both_ready, 1)
                nc.vector.memset(zeros[:, :], 0.0).then_inc(zeros_made, 1)
                dve.wait_ge(iota_made, 2)
                nc.vector.tensor_scalar(unfilled[:, :], c["fill"][:, :], node_no[:, :], None, ALU.add).then_inc(unfilled_ready, 1)
                nc.vector.tensor_tensor(gap[:, :].unsqueeze(2), c["gate_v"][:, :, 1:2], c["gate_v"][:, :, 0:1], ALU.subtract).then_inc(gap_ready, 1)
                dve.wait_ge(exp_ready, 1)
                link(nc.vector.tensor_scalar(c["mix_w"][:, 0, :], gap[:, :], 1.0, None, ALU.add))
                link(nc.vector.reciprocal(c["mix_w"][:, 0, :], c["mix_w"][:, 0, :]))
                link(nc.vector.tensor_tensor(c["mix_w"][:, 1, :], gap[:, :], c["mix_w"][:, 0, :], ALU.mult))
                dve.wait_ge(ranked, 2)
                link(nc.vector.tensor_copy(rank[:, :, :].rearrange("n t e -> n (t e)"), ps_rank[:, 0:NT * NE]))
                link(nc.vector.tensor_copy(total[:, :, :].rearrange("n t e -> n (t e)"), ps_total[:, 0:NT * NE]))
                now, then, gone = total, spare, 1
                while gone < NT:
                    nc.vector.tensor_copy(then[:, 0:gone, :], now[:, 0:gone, :])
                    link(nc.vector.tensor_tensor(then[:, gone:NT, :], now[:, gone:NT, :], now[:, 0:NT - gone, :], ALU.add))
                    now, then, gone = then, now, 2 * gone
                link(nc.vector.tensor_tensor(rank[:, 1:NT, :], rank[:, 1:NT, :], now[:, 0:NT - 1, :], ALU.add))
                run = now[:, NT - 1, :]
                link(nc.vector.tensor_scalar(tiles[:, :], run, float(P - 1), None, ALU.add))
                link(nc.vector.tensor_copy(tiles_i[:, :], tiles[:, :]))
                link(nc.vector.tensor_scalar(tiles_i[:, :], tiles_i[:, :], P.bit_length() - 1, None, ALU.arith_shift_right))
                link(nc.vector.tensor_copy(tiles[:, :], tiles_i[:, :]))
                now, then, gone = tiles, ends_a, 1
                while gone < NE:
                    nc.vector.tensor_copy(then[:, 0:gone], now[:, 0:gone])
                    link(nc.vector.tensor_tensor(then[:, gone:NE], now[:, gone:NE], now[:, 0:NE - gone], ALU.add))
                    now, then, gone = then, (ends_b if then is ends_a else ends_a), 2 * gone
                ends = now
                link(nc.vector.tensor_tensor(begins[:, :], ends[:, :], tiles[:, :], ALU.subtract))
                link(nc.vector.tensor_scalar(begins[:, :], begins[:, :], float(P), None, ALU.mult))
                link(nc.vector.tensor_tensor(rank[:, :, :], rank[:, :, :], begins[:, :].unsqueeze(1).to_broadcast([P, NT, NE]), ALU.add))
                for k in range(2):
                    link(nc.vector.tensor_tensor(prod[:, :, :], rank[:, :, :], c["chosen"][:, k, :, :], ALU.mult))
                    link(nc.vector.tensor_reduce(slot_f[:, k, :], prod[:, :, :], X, ALU.add))
                link(nc.vector.tensor_copy(c["slots"][:, :, :], slot_f[:, :, :]))
                link(nc.vector.tensor_tensor(over[:, :, :], ends[0:1, :].unsqueeze(1).to_broadcast([1, MT, NE]),
                                             tile_no[:, :].unsqueeze(2).to_broadcast([1, MT, NE]), ALU.is_le))
                link(nc.vector.tensor_reduce(owner[:, :], over[:, :, :], X, ALU.add))
                link(nc.vector.tensor_scalar(real[:, :], owner[:, :], float(NE - 1), None, ALU.is_le))
                link(nc.vector.tensor_scalar(first_row[:, :], c["iota"][0:1, 0:NE], float(CAP), None, ALU.mult))
                link(nc.vector.tensor_tensor(first_row[:, :], first_row[:, :], begins[0:1, :], ALU.subtract))
                link(nc.vector.tensor_tensor(over[:, :, :], owner[:, :].unsqueeze(2).to_broadcast([1, MT, NE]),
                                             c["iota"][0:1, 0:NE].unsqueeze(1).to_broadcast([1, MT, NE]), ALU.is_equal))
                link(nc.vector.tensor_tensor(over[:, :, :], over[:, :, :], first_row[:, :].unsqueeze(1).to_broadcast([1, MT, NE]), ALU.mult))
                link(nc.vector.tensor_reduce(start_f[:, :], over[:, :, :], X, ALU.add))
                link(nc.vector.scalar_tensor_tensor(start_f[:, :], tile_no[:, :], float(P), start_f[:, :], ALU.mult, ALU.add))
                link(nc.vector.tensor_tensor(c["start"][:, :], start_f[:, :], real[:, :], ALU.mult))
                link(nc.vector.tensor_tensor(c["owner"][:, :], owner[:, :], real[:, :], ALU.mult))
                for k in range(2):
                    link(nc.vector.tensor_tensor(prod[:, :, :], c["chosen"][:, k, :, :], c["mix_w"][:, k, :].unsqueeze(2).to_broadcast([P, NT, NE]), ALU.mult))
                    if k == 0:
                        link(nc.vector.tensor_copy(share[:, 0:NT, :], prod[:, :, :]))
                nc.vector.memset(share[:, NT:NT + 1, :], 0.0)
                link(nc.vector.tensor_tensor(share[:, 0:NT, :], share[:, 0:NT, :], prod[:, :, :], ALU.add))

            @block.gpsimd
            def _(pool):
                nc.gpsimd.iota(tile_no[:, :], pattern=[[1, MT]], base=0, channel_multiplier=0,
                               allow_small_or_imprecise_dtypes=True).then_inc(iota_made, 1)
                nc.gpsimd.iota(node_no[:, :], pattern=[[1, 1]], base=0, channel_multiplier=1,
                               allow_small_or_imprecise_dtypes=True).then_inc(iota_made, 1)
                pool.wait_ge(zeros_made, 1)
                pool.wait_ge(unfilled_ready, 1)
                for e in range(NE):
                    nc.gpsimd.indirect_dma_start(
                        out=d["rows"][:, :], out_offset=bass.IndirectOffsetOnAxis(ap=unfilled[:, e:e + 1].bitcast(U32), axis=0),
                        in_=zeros[:, :], in_offset=None).then_inc(filled, 16)
                pool.wait_ge(filled, 16 * NE)


def load_set(sp, a, w, j):
    for e in range(j * SET, (j + 1) * SET):
        sp.dma_start(w["w1"][:, e, :, :], a["ew1"][e * D:(e + 1) * D, :].rearrange("(k f) n -> f k n", f=P)).then_inc(w["in"][j], 16)
        sp.dma_start(w["w2"][:, e, :, :], a["ew2"][e * FE:(e + 1) * FE, :].rearrange("(k f) n -> f k n", f=P)).then_inc(w["in"][j], 16)
        sp.dma_start(w["b1"][:, e, :], a["eb1"][:, e * (FE // P):(e + 1) * (FE // P)]).then_inc(w["in"][j], 16)


def expert_phase(nc, m, c, a, d, w):
    with Memory(nc, "m_") as l:
        w1_tile = [l.sb(f"w1_tile{p}", [P, 2, FE]) for p in range(2)] * 2
        z = [l.sb(f"z{p}", [P, D]) for p in range(DEEP)]
        zT = [l.sb(f"zT{p}", [P, 2, P]) for p in range(DEEP)]
        hT = [l.sb(f"hT{p}", [P, FE // P, P]) for p in range(DEEP)]
        y = [l.sb(f"y{p}", [P, D]) for p in range(DEEP)]
        ps_t = [l.ps(f"ps_t{p}", [P, 2, P]) for p in range(2)] * 2
        ps_h = [l.ps(f"ps_h{p}", [P, FE // P, P]) for p in range(2)] * 2
        ps_y = [l.ps(f"ps_y{p}", [P, D]) for p in range(2)] * 2
        w1, w2, b1, w_in = w["w1"], w["w2"], w["b1"], w["in"]
        z_in = [l.sem(f"z_in{p}") for p in range(DEEP)]
        y_out = [l.sem(f"y_out{p}") for p in range(DEEP)]
        z_all_in = l.sem("z_all_in")
        weights_ready = l.sem("weights_ready")
        turned = l.sem("turned")
        zT_ready = l.sem("zT_ready")
        w1_placed = l.sem("w1_placed")
        up_done = l.sem("up_done")
        hT_ready = l.sem("hT_ready")
        down_done = l.sem("down_done")
        y_ready = l.sem("y_ready")

        def each(eng, body):
            for p in range(DEEP):
                body(p, 0, p)
            with eng.Fori(1, MT // DEEP - 1) as i:
                for p in range(DEEP):
                    body(DEEP * i + p, i, p)
            for p in range(DEEP):
                body(MT - DEEP + p, MT // DEEP - 1, p)

        with nc.Block() as block:
            @block.sync
            def _(sp):
                for j in range(NE // SET):
                    sp.wait_ge(w_in[j], 48 * SET)
                    if j + 1 < NE // SET:
                        load_set(sp, a, w, j + 1)
                    else:
                        sp.dma_start(c["z_all"][:, 0:NT - 1, :], d["z"][0:(NT - 1) * P, :].rearrange("(t n) e -> n t e", n=P)).then_inc(z_all_in, 16)
                        sp.dma_start(c["z_all"][0:LAST, NT - 1, :], d["z"][(NT - 1) * P:N, :]).then_inc(z_all_in, 16)
                    sp.sem_inc(weights_ready, SET)
                sp.wait_ge(z_all_in, 32)

            @block.tensor
            def _(pe):
                def turn(t, i, p):
                    pe.wait_ge(z_in[p], 16 * (i + 1))
                    if known(t, 2):
                        pe.wait_ge(zT_ready, t - 1)
                    for k in range(2):
                        last = nc.tensor.transpose(ps_t[p][:, k, :], z[p][:, k * P:(k + 1) * P], c["ident"][:, :])
                    last.then_inc(turned, 1)

                def up(t, i, p):
                    pe.wait_ge(zT_ready, t + 1)
                    pe.wait_ge(w1_placed, t + 1)
                    if known(t, 2):
                        pe.wait_ge(hT_ready, t - 1)
                    for f in range(FE // P):
                        for k in range(2):
                            last = nc.tensor.matmul(ps_h[p][:, f, :], w1_tile[p][:, k, f * P:(f + 1) * P], zT[p][:, k, :], start=(k == 0), stop=(k == 1))
                    last.then_inc(up_done, 1)

                def down(t, p):
                    e = pe.value_load(c["owner"][0:1, bass.ds(t, 1)], min_val=0, max_val=NE - 1)
                    pe.wait_ge(hT_ready, t + 1)
                    if known(t, 2):
                        pe.wait_ge(y_ready, t - 1)
                    for f in range(FE // P):
                        last = nc.tensor.matmul(ps_y[p][:, :], hT[p][:, f, :], w2[:, bass.ds(e, 1), f, :].rearrange("f a n -> f (a n)"), start=(f == 0), stop=(f == FE // P - 1))
                    last.then_inc(down_done, 1)

                turn(0, 0, 0)

                def body(t, i, p):
                    up(t, i, p)
                    if known_before(t, MT - 1):
                        turn(t + 1, i + (p + 1) // DEEP, (p + 1) % DEEP)
                    if known(t, 1):
                        down(t - 1, (p - 1) % DEEP)

                each(pe, body)
                down(MT - 1, DEEP - 1)

            @block.scalar
            def _(act):
                def load(t, p):
                    start = act.value_load(c["start"][0:1, bass.ds(t, 1)], min_val=0, max_val=NE * CAP - P)
                    act.dma_start(z[p][:, :], d["rows"][bass.ds(start, P), :]).then_inc(z_in[p], 16)

                for p in range(DEEP):
                    load(p, p)

                def body(t, i, p):
                    e = act.value_load(c["owner"][0:1, bass.ds(t, 1)], min_val=0, max_val=NE - 1)
                    act.wait_ge(up_done, t + 1)
                    if known(t, 2):
                        act.wait_ge(down_done, t - 1)
                    for f in range(FE // P):
                        last = nc.scalar.activation(hT[p][:, f, :], ps_h[p][:, f, :], ACT.Relu, bias=b1[:, bass.ds(e, 1), f])
                    last.then_inc(hT_ready, 1)
                    if not isinstance(i, int) or i + 1 < MT // DEEP:
                        load(t + DEEP, p)

                each(act, body)

            @block.vector
            def _(dve):
                def take(t, p, i):
                    dve.wait_ge(down_done, t + 1)
                    if known(t, DEEP):
                        dve.wait_ge(y_out[p], 16 * i)
                    nc.vector.tensor_copy(y[p][:, :], ps_y[p][:, :]).then_inc(y_ready, 1)

                def place(t, p):
                    e = dve.value_load(c["owner"][0:1, bass.ds(t, 1)], min_val=0, max_val=NE - 1)
                    dve.wait_ge(weights_ready, e + 1)
                    if known(t, 2):
                        dve.wait_ge(up_done, t - 1)
                    nc.vector.tensor_copy(w1_tile[p][:, :, :].unsqueeze(1), w1[:, bass.ds(e, 1), :, :]).then_inc(w1_placed, 1)

                def copy_zT(t, p):
                    dve.wait_ge(turned, t + 1)
                    if known(t, DEEP):
                        dve.wait_ge(up_done, t - DEEP + 1)
                    nc.vector.tensor_copy(zT[p][:, :, :], ps_t[p][:, :, :]).then_inc(zT_ready, 1)

                place(0, 0)
                copy_zT(0, 0)

                def body(t, i, p):
                    if known_before(t, MT - 1):
                        place(t + 1, (p + 1) % DEEP)
                        copy_zT(t + 1, (p + 1) % DEEP)
                    if known(t, 1):
                        take(t - 1, (p - 1) % DEEP, i if p else i - 1)

                each(dve, body)
                take(MT - 1, DEEP - 1, MT // DEEP - 1)

            @block.gpsimd
            def _(pool):
                def body(t, i, p):
                    pool.wait_ge(y_ready, t + 1)
                    pool.dma_start(d["outs"][bass.ds(t * P, P), :], y[p][:, :]).then_inc(y_out[p], 16)

                each(pool, body)
                for p in range(DEEP):
                    pool.wait_ge(y_out[p], 16 * (MT // DEEP))


def combine_phase(nc, m, c, a, d, out):
    with Memory(nc, "c_") as l:
        gamma_all = l.sb("gamma_all", [P, D])
        xr = [l.sb(f"xr{b}", [P, D]) for b in range(4)]
        y1 = [l.sb(f"y1{b}", [P, D]) for b in range(4)]
        y2 = [l.sb(f"y2{b}", [P, D]) for b in range(4)]
        y = [l.sb(f"y{b}", [P, D]) for b in range(4)]
        res = [l.sb(f"res{b}", [P, D]) for b in range(4)]
        idx = [l.sb(f"idx{q}", [P, 2, 2], I32) for q in range(2)]
        mix = [l.sb(f"mix{q}", [P, 2, 2]) for q in range(2)]
        stats = l.sb("stats", [P, 2, 6])
        mv = l.sb("mv", [P, 2, 2])
        rstd = [l.sb(f"rstd{q}", [P, 2]) for q in range(2)]
        shift = [l.sb(f"shift{q}", [P, 2]) for q in range(2)]
        eb2 = l.sb("eb2", [NE, D])
        share = [l.sb(f"share{q}", [P, 2, NE]) for q in range(2)]
        shareT = [l.sb(f"shareT{q}", [NE, 2, P]) for q in range(2)]
        ps_t = [l.ps(f"ps_t{q}", [NE, 2, P]) for q in range(2)]
        ps_b = [l.ps(f"ps_b{q}", [P, 2, D]) for q in range(2)]
        share_picked = l.sem("share_picked")
        turned = l.sem("turned")
        shareT_ready = l.sem("shareT_ready")
        bias_done = l.sem("bias_done")
        bias_added = l.sem("bias_added")
        small_in = l.sem("small_in")
        loaded = [l.sem(f"loaded{q}") for q in range(2)]
        got = [l.sem(f"got{q}") for q in range(2)]
        stored = [l.sem(f"stored{q}") for q in range(2)]
        picked = l.sem("picked")
        summed = l.sem("summed")
        step = l.sem("step")
        var_ready = l.sem("var_ready")
        std_ready = l.sem("std_ready")
        scale_ready = l.sem("scale_ready")
        normed = l.sem("normed")
        scaled = l.sem("scaled")
        res_ready = l.sem("res_ready")
        NJ = (NT + 1) // 2
        PAIR = [0, 1]
        assert NT % 2 == 1 and NJ % 2 == 1

        def each_pair(eng, body):
            body(0, 0, 0, PAIR, P)
            body(1, 0, 1, PAIR, P)
            with eng.Fori(1, NJ // 2) as i:
                body(2 * i, i, 0, PAIR, P)
                body(2 * i + 1, i, 1, PAIR, P)
            body(NJ - 1, NJ // 2, 0, [0], LAST)

        with nc.Block() as block:
            @block.sync
            def _(sp):
                def load(j, q, tiles, r):
                    for s in tiles:
                        sp.dma_start(xr[2 * q + s][0:r, :], d["xr"][bass.ds((2 * j + s) * P, r), :]).then_inc(loaded[q], 16)

                sp.dma_start(eb2[:, :], a["eb2"]).then_inc(small_in, 16)
                sp.dma_start(gamma_all[:, :], rows(a["ffn_gamma"], P, D)).then_inc(small_in, 16)
                load(0, 0, PAIR, P)
                load(1, 1, PAIR, P)

                def body(j, i, q, tiles, r):
                    sp.wait_ge(res_ready, j + 1)
                    for s in tiles:
                        sp.dma_start(out[bass.ds((2 * j + s) * P, r), :], res[2 * q + s][0:r, :]).then_inc(stored[q], 16)
                    if isinstance(j, int) and j == NJ - 3:
                        load(j + 2, q, [0], LAST)
                    elif known_before(j, NJ - 2):
                        load(j + 2, q, PAIR, P)

                body(0, 0, 0, PAIR, P)
                body(1, 0, 1, PAIR, P)
                with sp.Fori(1, NJ // 2 - 1) as i:
                    body(2 * i, i, 0, PAIR, P)
                    body(2 * i + 1, i, 1, PAIR, P)
                body(NJ - 3, NJ // 2 - 1, 0, PAIR, P)
                body(NJ - 2, NJ // 2 - 1, 1, PAIR, P)
                body(NJ - 1, NJ // 2, 0, [0], LAST)
                sp.wait_ge(stored[0], 32 * (NJ // 2) + 16)
                sp.wait_ge(stored[1], 32 * (NJ // 2))

            @block.gpsimd
            def _(pool):
                def body(j, i, q, tiles, r):
                    n = len(tiles)
                    if known(j, 2):
                        pool.wait_ge(summed, j - 1)
                        pool.wait_ge(got[q], 64 * i)
                    nc.gpsimd.tensor_copy(mix[q][0:r, :, 0:n], c["mix_w"][0:r, :, bass.ds(2 * j, n)])
                    nc.gpsimd.tensor_copy(idx[q][0:r, :, 0:n], c["slots"][0:r, :, bass.ds(2 * j, n)]).then_inc(picked, 1)
                    pool.wait_ge(picked, j + 1)
                    carry_wait(pool, c["carrier_pool"])
                    for s in tiles:
                        for k, to in enumerate((y1[2 * q + s], y2[2 * q + s])):
                            nc.gpsimd.indirect_dma_start(
                                out=to[0:r, :], out_offset=None, in_=d["outs"][:, :],
                                in_offset=bass.IndirectOffsetOnAxis(ap=idx[q][0:r, k, s:s + 1].bitcast(U32), axis=0)).then_inc(got[q], 16)

                each_pair(pool, body)

            @block.tensor
            def _(pe):
                pe.wait_ge(small_in, 32)

                def body(j, i, q, tiles, r):
                    pe.wait_ge(share_picked, j + 1)
                    if known(j, 2):
                        pe.wait_ge(shareT_ready, j - 1)
                    for s in tiles:
                        last = nc.tensor.transpose(ps_t[q][:, s, 0:r], share[q][0:r, s, :], c["ident"][0:r, 0:r])
                    last.then_inc(turned, 1)
                    pe.wait_ge(shareT_ready, j + 1)
                    if known(j, 2):
                        pe.wait_ge(bias_added, j - 1)
                    for s in tiles:
                        nc.tensor.matmul(ps_b[q][0:r, s, :], c["ident"][0:r, 0:r], c["z_all"][0:r, bass.ds(2 * j + s, 1), :].rearrange("n t e -> n (t e)"),
                                         start=True, stop=False)
                        last = nc.tensor.matmul(ps_b[q][0:r, s, :], shareT[q][:, s, 0:r], eb2[:, :], start=False, stop=True)
                    last.then_inc(bias_done, 1)

                each_pair(pe, body)

            @block.scalar
            def _(act):
                def turn_share(j, q):
                    if known(j, 2):
                        act.wait_ge(bias_done, j - 1)
                    nc.scalar.activation(share[q][:, :, :], c["share"][:, bass.ds(2 * j, 2), :], ACT.Copy).then_inc(share_picked, 1)
                    act.wait_ge(turned, j + 1)
                    nc.scalar.activation(shareT[q][:, :, :], ps_t[q][:, :, :], ACT.Copy).then_inc(shareT_ready, 1)

                turn_share(0, 0)

                def body(j, i, q, tiles, r):
                    n = len(tiles)
                    if known_before(j, NJ - 1):
                        turn_share(j + 1, 1 - q)
                    act.wait_ge(var_ready, j + 1)
                    nc.scalar.activation(rstd[q][0:r, 0:n], mv[0:r, 0:n, 1], ACT.Sqrt, bias=c["eps"][0:r, :]).then_inc(std_ready, 1)
                    act.wait_ge(scale_ready, j + 1)
                    for s in tiles:
                        b = 2 * q + s
                        last = nc.scalar.activation(y[b][0:r, :], y[b][0:r, :], ACT.Identity, bias=shift[q][0:r, s:s + 1], scale=rstd[q][0:r, s:s + 1])
                    last.then_inc(normed, 1)

                each_pair(act, body)

            @block.vector
            def _(dve):
                def finish(j, i, q, tiles, r):
                    dve.wait_ge(normed, j + 1)
                    dve.wait_ge(loaded[q], 32 * i + 16 * len(tiles))
                    if known(j, 2):
                        dve.wait_ge(stored[q], 32 * i)
                    for s in tiles:
                        b = 2 * q + s
                        last = nc.vector.tensor_tensor(res[b][0:r, :], y[b][0:r, :], gamma_all[0:r, :], ALU.mult)
                    last.then_inc(scaled, 1)
                    dve.wait_ge(scaled, j + 1)
                    for s in tiles:
                        b = 2 * q + s
                        last = nc.vector.tensor_tensor(res[b][0:r, :], res[b][0:r, :], xr[b][0:r, :], ALU.add)
                    last.then_inc(res_ready, 1)

                def body(j, i, q, tiles, r):
                    link = Chain(dve, step, j, 2)
                    n = len(tiles)
                    dve.wait_ge(got[q], 64 * i + 32 * n)
                    dve.wait_ge(bias_done, j + 1)
                    for s in tiles:
                        b = 2 * q + s
                        last = nc.vector.scalar_tensor_tensor(y[b][0:r, :], y1[b][0:r, :], mix[q][0:r, 0, s:s + 1], ps_b[q][0:r, s, :], ALU.mult, ALU.add)
                    last.then_inc(bias_added, 1)
                    dve.wait_ge(bias_added, j + 1)
                    for s in tiles:
                        b = 2 * q + s
                        last = nc.vector.scalar_tensor_tensor(y[b][0:r, :], y2[b][0:r, :], mix[q][0:r, 1, s:s + 1], y[b][0:r, :], ALU.mult, ALU.add)
                    last.then_inc(summed, 1)
                    dve.wait_ge(summed, j + 1)
                    for s in tiles:
                        last = nc.vector.bn_stats(stats[0:r, s, :], y[2 * q + s][0:r, :])
                    link(last)
                    carry_wait(dve, c["carrier_dve"])
                    for s in tiles:
                        last = nc.vector.bn_aggr(mv[0:r, s, :], stats[0:r, s, :])
                    last.then_inc(var_ready, 1)
                    if known(j, 1):
                        finish(j - 1, i if q else i - 1, 1 - q, PAIR, P)
                    dve.wait_ge(std_ready, j + 1)
                    link(nc.vector.reciprocal(rstd[q][0:r, 0:n], rstd[q][0:r, 0:n]))
                    nc.vector.scalar_tensor_tensor(shift[q][0:r, 0:n], mv[0:r, 0:n, 0], -1.0, rstd[q][0:r, 0:n], ALU.mult, ALU.mult).then_inc(scale_ready, 1)
                    dve.wait_ge(scale_ready, j + 1)
                    link.end()

                dve.wait_ge(small_in, 32)
                each_pair(dve, body)
                finish(NJ - 1, NJ // 2, 0, [0], LAST)


def gps_layer_kernel(nc, a, out):
    with Memory(nc, "k_") as m:
        c = {
            "ident": m.sb("ident", [P, P]),
            "ones": m.sb("ones", [P, P]),
            "before": m.sb("before", [P, P]),
            "iota": m.sb("iota", [P, W]),
            "eps": m.sb("eps", [P, 1]),
            "base": m.sb("base", [P, NG + 1]),
            "base_i": m.sb("base_i", [1, NG + 1], I32),
            "passes": m.sb("passes", [1, 1], I32),
            "chosen": m.sb("chosen", [P, 2, NT, NE]),
            "gate_v": m.sb("gate_v", [P, NT, 2]),
            "mix_w": m.sb("mix_w", [P, 2, NT]),
            "slots": m.sb("slots", [P, 2, NT], I32),
            "fill": m.sb("fill", [P, NE]),
            "owner": m.sb("owner", [1, MT], I32),
            "start": m.sb("start", [1, MT], I32),
            "base_moved": m.sem("base_moved"),
            "carrier_dve": m.sem("carrier_dve"),
            "carrier_pool": m.sem("carrier_pool"),
            "carrier_pe": m.sem("carrier_pe"),
        }
        d = {
            "xn": nc.dram_tensor("xn_kept", [N, D], F32, kind="Internal").ap(),
            "xT": nc.dram_tensor("xT_kept", [NT * P, 2 * P], F32, kind="Internal").ap(),
            "proj": nc.dram_tensor("proj_kept", [N, HID], F32, kind="Internal").ap(),
            "xr": nc.dram_tensor("xr_kept", [N, D], F32, kind="Internal").ap(),
            "z": nc.dram_tensor("z_kept", [N, D], F32, kind="Internal").ap(),
            "rows": nc.dram_tensor("rows_kept", [NE * CAP, D], F32, kind="Internal").ap(),
            "outs": nc.dram_tensor("outs_kept", [MT * P, D], F32, kind="Internal").ap(),
        }
        with Memory(nc, "n_") as n:
            c |= {
                "w1b": n.sb("w1b", [P, HID]),
                "ones_bf16": n.sb("ones_bf16", [P, P], BF16),
                "before_bf16": n.sb("before_bf16", [P, P], BF16),
                "zeros": n.sb("zeros", [P, 512]),
                "src": n.sb("src", [P, ET + 1], I32),
                "to_base": n.sb("to_base", [P, ET + 1]),
                "sums": n.sb("sums", [P, FB, H, VN]),
                "tail_sums": n.sb("tail_sums", [P, H // 2, VN]),
                "acc": n.sb("acc", [P, FB + 1, N + W]),
            }
            setup_phase(nc, m, c, a)
            node_phase(nc, m, c, a, d)
            with Memory(nc, "v_") as v:
                w = UpdateWeights(v)
                edge_phase(nc, m, c, a, d, w)
                update_phase(nc, m, c, a, d, w)
        with Memory(nc, "o_") as o:
            c["z_all"] = o.sb("z_all", [P, NT, D])
            c["share"] = o.sb("share", [P, NT + 1, NE])
            with Memory(nc, "w_") as k:
                w = {
                    "w1": k.sb("w1", [P, NE, 2, FE]),
                    "w2": k.sb("w2", [P, NE, FE // P, D]),
                    "b1": k.sb("b1", [P, NE, FE // P]),
                    "in": [k.sem(f"in{j}") for j in range(NE // SET)],
                }
                route_phase(nc, m, c, a, d, w)
                expert_phase(nc, m, c, a, d, w)
            combine_phase(nc, m, c, a, d, out)


def _layout(inputs):
    import numpy as np

    def arr(k):
        return np.asarray(inputs[k])

    src, dst = arr("src"), arr("dst")
    whole = ET * P
    return {
        "x": arr("x"),
        "dst": dst,
        "dst_cols": dst[:whole].reshape(ET, P).T,
        "dst_tail": dst[whole:].reshape(EL, 1),
        "src_cols": src[:whole].reshape(ET, P).T,
        "src_tail": src[whole:].reshape(EL, 1),
        "attrT": arr("edge_attr_128").T,
        "u": arr("L0_gnn_u"),
        "W1": arr("L0_gnn_W1"), "b1": arr("L0_gnn_b1"), "W2": arr("L0_gnn_W2"), "b2": arr("L0_gnn_b2"),
        "W3": arr("L0_gnn_W3"), "b3": arr("L0_gnn_b3"), "W4": arr("L0_gnn_W4"), "b4": arr("L0_gnn_b4"),
        "gnn_gamma": arr("L0_gnn_gamma"), "gnn_beta": arr("L0_gnn_beta"),
        "wqkvT": arr("L0_mix_Wqkv").T, "bqkv": arr("L0_mix_bqkv"),
        "wprojT": arr("L0_mix_Wproj").T, "bproj": arr("L0_mix_bproj"),
        "temperature": arr("L0_mix_temperature").reshape(H),
        "gate_w": arr("L0_ffn_gate_w"), "gate_b": arr("L0_ffn_gate_b"),
        "ew1": arr("L0_ffn_w1").reshape(NE * D, FE),
        "eb1": arr("L0_ffn_b1").reshape(NE * (FE // P), P).T,
        "ew2": arr("L0_ffn_w2").reshape(NE * FE, D),
        "eb2": arr("L0_ffn_b2"),
        "ffn_gamma": arr("L0_ffn_gamma"), "ffn_beta": arr("L0_ffn_beta"),
    }


def kernel(**inputs):
    import numpy as np
    import concourse.bacc as bacc
    from concourse.bass_utils import run_bass_kernel_spmd

    nc = bacc.Bacc("TRN2", target_bir_lowering=False, num_devices=1)
    arrays, aps = {}, {}
    for name, value in _layout(inputs).items():
        value = np.ascontiguousarray(value)
        arrays[f"in_{name}"] = value
        aps[name] = nc.dram_tensor(f"in_{name}", value.shape, mybir.dt.from_np(value.dtype), kind="ExternalInput").ap()
    out = nc.dram_tensor("out_0", (N, D), F32, kind="ExternalOutput").ap()
    gps_layer_kernel(nc, aps, out)
    r = run_bass_kernel_spmd(nc, [arrays], core_ids=[0])
    return r.results[0]["out_0"]
```
